# Optimizing a Trainium2 kernel written in Bass

```python
import numpy as np
import jax
import jax.numpy as jnp

def _softmax(x, axis=-1):
    return jax.nn.softmax(x, axis=axis)

def _gelu(x):
    return jax.nn.gelu(x, approximate=True)

def _silu(x):
    return jax.nn.silu(x)

def _sigmoid(x):
    return jax.nn.sigmoid(x)

def _layernorm(x, axis=-1, eps=1e-05):
    m = jnp.mean(x, axis=axis, keepdims=True)
    v = jnp.var(x, axis=axis, keepdims=True)
    return (x - m) / jnp.sqrt(v + eps)

def _scatter_add(tgt, idx, src, axis=0):
    return tgt.at[idx].add(src)

def _segment_sum(src, seg, n):
    return jax.ops.segment_sum(src, seg, n)
kernel_name = 'mk_seq_postln_d2_jaxref_r8_d43f37'

def setup_inputs(seed: int=0):
    np.random.seed(seed)
    _w = jnp.asarray

    def _L0_attn_setup():
        import math
        import jax, jax.numpy as jnp
        import numpy as np
        HEADS = 16
        key = jax.random.key(seed)
        k1, k2, k3, k4, k5 = jax.random.split(key, 5)
        B, S, D = (2, 256, 128)
        return {'x': jax.random.normal(k1, (B, S, D), dtype=jnp.float32), 'Wqkv': jax.random.normal(k2, (3 * D, D), dtype=jnp.float32) * (1.0 / math.sqrt(D)), 'bqkv': jax.random.normal(k3, (3 * D,), dtype=jnp.float32) * 0.02, 'Wo': jax.random.normal(k4, (D, D), dtype=jnp.float32) * (1.0 / math.sqrt(D)), 'bo': jax.random.normal(k5, (D,), dtype=jnp.float32) * 0.02}
    _L0_attn_in = _L0_attn_setup()

    def _L0_ffn_setup():
        import jax, jax.numpy as jnp
        import numpy as np
        DIM = 128
        DEPTH = 6
        HEADS = 16
        DIM_HEAD = 64
        WINDOW = 32
        INNER = HEADS * DIM_HEAD
        DIM_INNER = int(DIM * 4 * 2 / 3)
        QK_SCALE = 8.0

        def shift_tokens(t):
            a, s = jnp.split(t, 2, -1)
            s = jnp.pad(s, ((0, 0), (1, 0), (0, 0)))[:, :-1]
            return jnp.concatenate([a, s], -1)

        def l2norm(t):
            return t / jnp.maximum(jnp.linalg.norm(t, axis=-1, keepdims=True), 1e-12)

        def rotate_half(x):
            x1, x2 = jnp.split(x, 2, -1)
            return jnp.concatenate([-x2, x1], -1)

        def rotary_tables(n):
            half = jnp.arange(0, DIM_HEAD, 2, dtype=jnp.float32)
            inv_freq = 1.0 / 10000.0 ** (half / DIM_HEAD)
            t = jnp.arange(n, dtype=jnp.float32)
            freqs = t[:, None] * inv_freq[None, :]
            freqs = jnp.concatenate([freqs, freqs], -1)
            base_scale = (half + 0.4 * DIM_HEAD) / (1.4 * DIM_HEAD)
            power = (t - n // 2) / (WINDOW // 2)
            scale = base_scale[None, :] ** power[:, None]
            scale = jnp.concatenate([scale, scale], -1)
            return (freqs, scale)

        def local_attention(q, k, v):
            b, h, n, d = q.shape
            w = WINDOW
            nw = n // w
            bq = q.reshape(b, h, nw, w, d)
            bk = k.reshape(b, h, nw, w, d)
            bv = v.reshape(b, h, nw, w, d)

            def look(t):
                p = jnp.pad(t, ((0, 0), (0, 0), (1, 0), (0, 0), (0, 0)))
                return jnp.concatenate([p[:, :, :nw], p[:, :, 1:]], axis=3)
            bk2, bv2 = (look(bk), look(bv))
            seq = jnp.arange(n).reshape(nw, w)
            seq_p = jnp.pad(seq, ((1, 0), (0, 0)), constant_values=-1)
            jt = jnp.concatenate([seq_p[:nw], seq_p[1:]], axis=1)
            it = seq[:, :, None]
            jb = jt[:, None, :]
            mask = (it < jb) | (it > jb + w) | (jb == -1)
            sim = jnp.einsum('bhwie,bhwje->bhwij', bq, bk2) * QK_SCALE
            sim = jnp.where(mask, -jnp.finfo(sim.dtype).max, sim)
            attn = jax.nn.softmax(sim, -1)
            out = jnp.einsum('bhwij,bhwje->bhwie', attn, bv2)
            return out.reshape(b, h, n, d)

        def attn_layer(x, Wqkv, qs, ksc, Wo):
            b, n, _ = x.shape
            qkv = x @ Wqkv
            q, k, v = jnp.split(qkv, 3, -1)
            sh = lambda t: t.reshape(b, n, HEADS, DIM_HEAD).transpose(0, 2, 1, 3)
            q, k, v = (sh(q), sh(k), sh(v))
            q = l2norm(q) * qs
            k = l2norm(k) * ksc
            freqs, scale = rotary_tables(n)
            cos, sin = (jnp.cos(freqs), jnp.sin(freqs))
            q = q * cos * scale + rotate_half(q) * sin * scale
            inv = 1.0 / scale
            k = k * cos * inv + rotate_half(k) * sin * inv
            out = local_attention(q, k, v)
            out = out.transpose(0, 2, 1, 3).reshape(b, n, INNER)
            return out @ Wo

        def ffn_layer(x, g, bln, W1, b1, W2, b2):
            mu = x.mean(-1, keepdims=True)
            var = ((x - mu) ** 2).mean(-1, keepdims=True)
            xn = (x - mu) / jnp.sqrt(var + 1e-05) * g + bln
            hg = xn @ W1 + b1
            a, gate = jnp.split(hg, 2, -1)
            return a * jax.nn.gelu(gate, approximate=False) @ W2 + b2
        key = jax.random.key(seed)
        ks = jax.random.split(key, 8)
        B, N = (2, 256)
        init = lambda k, shape: jax.random.normal(k, shape, jnp.float32) * 0.02
        return {'x': jax.random.normal(ks[0], (B, N, DIM), jnp.float32), 'Wqkv': init(ks[1], (DEPTH, DIM, 3 * INNER)), 'q_scale': jnp.ones((DEPTH, DIM_HEAD), jnp.float32), 'k_scale': jnp.ones((DEPTH, DIM_HEAD), jnp.float32), 'Wo': init(ks[2], (DEPTH, INNER, DIM)), 'ln_g': jnp.ones((DEPTH, DIM), jnp.float32), 'ln_b': jnp.zeros((DEPTH, DIM), jnp.float32), 'W1': init(ks[3], (DEPTH, DIM, 2 * DIM_INNER)), 'b1': jnp.zeros((DEPTH, 2 * DIM_INNER), jnp.float32), 'W2': init(ks[4], (DEPTH, DIM_INNER, DIM)), 'b2': jnp.zeros((DEPTH, DIM), jnp.float32)}
    _L0_ffn_in = _L0_ffn_setup()

    def _L1_attn_setup():
        import math
        import jax, jax.numpy as jnp
        import numpy as np
        HEADS = 8
        SCALE_BASE = 512.0
        GN_EPS = 1e-05

        def _gammas(heads):
            return 1.0 - np.exp(np.linspace(math.log(1.0 / 32.0), math.log(1.0 / 512.0), heads))

        def _xpos(x, downscale):
            N, S, d = x.shape
            half = d // 2
            scale = (jnp.arange(0, d, 2, dtype=jnp.float32) + 0.4 * d) / (1.4 * d)
            pos = jnp.arange(S, dtype=jnp.float32)
            sc = scale[None, :] ** (pos / SCALE_BASE)[:, None]
            inv_freq = 1.0 / 10000.0 ** (jnp.arange(half, dtype=jnp.float32) / half)
            sinusoid = pos[:, None] * inv_freq[None, :]
            sin, cos = (jnp.sin(sinusoid), jnp.cos(sinusoid))
            if downscale:
                sc = 1.0 / sc
            sin_s = jnp.repeat(sin * sc, 2, axis=-1)
            cos_s = jnp.repeat(cos * sc, 2, axis=-1)
            x1, x2 = (x[..., ::2], x[..., 1::2])
            rot = jnp.stack((-x2, x1), axis=-1).reshape(x.shape)
            return x * cos_s + rot * sin_s
        key = jax.random.key(seed)
        ks = jax.random.split(key, 6)
        B, S, H = (2, 256, 128)
        h = HEADS
        d = H // h
        X = jax.random.normal(ks[0], (B, S, H), dtype=jnp.float32)
        W_Q = jax.random.normal(ks[1], (h, d, d), dtype=jnp.float32) / d
        W_K = jax.random.normal(ks[2], (h, d, d), dtype=jnp.float32) / d
        W_V = jax.random.normal(ks[3], (h, d, d), dtype=jnp.float32) / d
        W_G = jax.random.normal(ks[4], (H, H), dtype=jnp.float32) / H
        W_O = jax.random.normal(ks[5], (H, H), dtype=jnp.float32) / H
        gn_weight = jnp.ones((H,), dtype=jnp.float32)
        gn_bias = jnp.zeros((H,), dtype=jnp.float32)
        return {'X': X, 'W_Q': W_Q, 'W_K': W_K, 'W_V': W_V, 'W_G': W_G, 'W_O': W_O, 'gn_weight': gn_weight, 'gn_bias': gn_bias}
    _L1_attn_in = _L1_attn_setup()

    def _L1_ffn_setup():
        import math
        import jax, jax.numpy as jnp
        import numpy as np
        D_MODEL = 128
        D_FF = 512
        E = 8
        K = 2
        CAP_FACTOR = 1.25
        CLAMP = 10000.0
        LN_EPS = 1e-05
        B, S = (2, 256)
        key = jax.random.key(seed)
        ks = jax.random.split(key, 6)
        b12 = math.sqrt(6.0 / (D_MODEL + 2 * D_FF))
        b3 = math.sqrt(6.0 / (D_FF + D_MODEL))
        br = 0.02 * math.sqrt(3.0)
        return {'x': jax.random.normal(ks[0], (B, S, D_MODEL), dtype=jnp.float32), 'ln_gamma': jnp.ones((D_MODEL,), jnp.float32), 'ln_beta': jnp.zeros((D_MODEL,), jnp.float32), 'router_w': jax.random.uniform(ks[1], (E, D_MODEL), jnp.float32, -br, br), 'w12': jax.random.uniform(ks[2], (E, 2 * D_FF, D_MODEL), jnp.float32, -b12, b12), 'w3': jax.random.uniform(ks[3], (E, D_MODEL, D_FF), jnp.float32, -b3, b3)}
    _L1_ffn_in = _L1_ffn_setup()
    _d = {'L0_attn_x': _L0_attn_in['x'], 'L0_attn_Wqkv': _L0_attn_in['Wqkv'], 'L0_attn_bqkv': _L0_attn_in['bqkv'], 'L0_attn_Wo': _L0_attn_in['Wo'], 'L0_attn_bo': _L0_attn_in['bo'], 'L0_ffn_Wqkv': _L0_ffn_in['Wqkv'], 'L0_ffn_q_scale': _L0_ffn_in['q_scale'], 'L0_ffn_k_scale': _L0_ffn_in['k_scale'], 'L0_ffn_Wo': _L0_ffn_in['Wo'], 'L0_ffn_ln_g': _L0_ffn_in['ln_g'], 'L0_ffn_ln_b': _L0_ffn_in['ln_b'], 'L0_ffn_W1': _L0_ffn_in['W1'], 'L0_ffn_b1': _L0_ffn_in['b1'], 'L0_ffn_W2': _L0_ffn_in['W2'], 'L0_ffn_b2': _L0_ffn_in['b2'], 'L1_attn_W_Q': _L1_attn_in['W_Q'], 'L1_attn_W_K': _L1_attn_in['W_K'], 'L1_attn_W_V': _L1_attn_in['W_V'], 'L1_attn_W_G': _L1_attn_in['W_G'], 'L1_attn_W_O': _L1_attn_in['W_O'], 'L1_attn_gn_weight': _L1_attn_in['gn_weight'], 'L1_attn_gn_bias': _L1_attn_in['gn_bias'], 'L1_ffn_ln_gamma': _L1_ffn_in['ln_gamma'], 'L1_ffn_ln_beta': _L1_ffn_in['ln_beta'], 'L1_ffn_router_w': _L1_ffn_in['router_w'], 'L1_ffn_w12': _L1_ffn_in['w12'], 'L1_ffn_w3': _L1_ffn_in['w3']}
    _x0 = _d['L0_attn_x']
    _d['L0_attn_x'] = jax.random.normal(jax.random.fold_in(jax.random.key(seed), 1), (2, 1024, 128), dtype=_x0.dtype)
    del _x0
    return _d

def reference(L0_attn_x, L0_attn_Wqkv, L0_attn_bqkv, L0_attn_Wo, L0_attn_bo, L0_ffn_Wqkv, L0_ffn_q_scale, L0_ffn_k_scale, L0_ffn_Wo, L0_ffn_ln_g, L0_ffn_ln_b, L0_ffn_W1, L0_ffn_b1, L0_ffn_W2, L0_ffn_b2, L1_attn_W_Q, L1_attn_W_K, L1_attn_W_V, L1_attn_W_G, L1_attn_W_O, L1_attn_gn_weight, L1_attn_gn_bias, L1_ffn_ln_gamma, L1_ffn_ln_beta, L1_ffn_router_w, L1_ffn_w12, L1_ffn_w3):

    def _L0_attn_ref(x, Wqkv, bqkv, Wo, bo):
        import math
        import jax, jax.numpy as jnp
        import numpy as np
        HEADS = 16
        B, S, D = x.shape
        H = HEADS
        hd = D // H
        qkv = x @ Wqkv.T + bqkv
        qkv = qkv.reshape(B, H, S, 3 * hd)
        q, k, v = jnp.split(qkv, 3, axis=-1)
        scores = jnp.einsum('bhsd,bhtd->bhst', q, k) * (1.0 / math.sqrt(hd))
        attn = jax.nn.softmax(scores, axis=-1)
        vals = jnp.einsum('bhst,bhtd->bhsd', attn, v)
        vals = vals.reshape(B, S, D)
        return vals @ Wo.T + bo

    def _L0_ffn_ref(x, Wqkv, q_scale, k_scale, Wo, ln_g, ln_b, W1, b1, W2, b2):
        import jax, jax.numpy as jnp
        import numpy as np
        DIM = 128
        DEPTH = 6
        HEADS = 16
        DIM_HEAD = 64
        WINDOW = 32
        INNER = HEADS * DIM_HEAD
        DIM_INNER = int(DIM * 4 * 2 / 3)
        QK_SCALE = 8.0

        def shift_tokens(t):
            a, s = jnp.split(t, 2, -1)
            s = jnp.pad(s, ((0, 0), (1, 0), (0, 0)))[:, :-1]
            return jnp.concatenate([a, s], -1)

        def l2norm(t):
            return t / jnp.maximum(jnp.linalg.norm(t, axis=-1, keepdims=True), 1e-12)

        def rotate_half(x):
            x1, x2 = jnp.split(x, 2, -1)
            return jnp.concatenate([-x2, x1], -1)

        def rotary_tables(n):
            half = jnp.arange(0, DIM_HEAD, 2, dtype=jnp.float32)
            inv_freq = 1.0 / 10000.0 ** (half / DIM_HEAD)
            t = jnp.arange(n, dtype=jnp.float32)
            freqs = t[:, None] * inv_freq[None, :]
            freqs = jnp.concatenate([freqs, freqs], -1)
            base_scale = (half + 0.4 * DIM_HEAD) / (1.4 * DIM_HEAD)
            power = (t - n // 2) / (WINDOW // 2)
            scale = base_scale[None, :] ** power[:, None]
            scale = jnp.concatenate([scale, scale], -1)
            return (freqs, scale)

        def local_attention(q, k, v):
            b, h, n, d = q.shape
            w = WINDOW
            nw = n // w
            bq = q.reshape(b, h, nw, w, d)
            bk = k.reshape(b, h, nw, w, d)
            bv = v.reshape(b, h, nw, w, d)

            def look(t):
                p = jnp.pad(t, ((0, 0), (0, 0), (1, 0), (0, 0), (0, 0)))
                return jnp.concatenate([p[:, :, :nw], p[:, :, 1:]], axis=3)
            bk2, bv2 = (look(bk), look(bv))
            seq = jnp.arange(n).reshape(nw, w)
            seq_p = jnp.pad(seq, ((1, 0), (0, 0)), constant_values=-1)
            jt = jnp.concatenate([seq_p[:nw], seq_p[1:]], axis=1)
            it = seq[:, :, None]
            jb = jt[:, None, :]
            mask = (it < jb) | (it > jb + w) | (jb == -1)
            sim = jnp.einsum('bhwie,bhwje->bhwij', bq, bk2) * QK_SCALE
            sim = jnp.where(mask, -jnp.finfo(sim.dtype).max, sim)
            attn = jax.nn.softmax(sim, -1)
            out = jnp.einsum('bhwij,bhwje->bhwie', attn, bv2)
            return out.reshape(b, h, n, d)

        def attn_layer(x, Wqkv, qs, ksc, Wo):
            b, n, _ = x.shape
            qkv = x @ Wqkv
            q, k, v = jnp.split(qkv, 3, -1)
            sh = lambda t: t.reshape(b, n, HEADS, DIM_HEAD).transpose(0, 2, 1, 3)
            q, k, v = (sh(q), sh(k), sh(v))
            q = l2norm(q) * qs
            k = l2norm(k) * ksc
            freqs, scale = rotary_tables(n)
            cos, sin = (jnp.cos(freqs), jnp.sin(freqs))
            q = q * cos * scale + rotate_half(q) * sin * scale
            inv = 1.0 / scale
            k = k * cos * inv + rotate_half(k) * sin * inv
            out = local_attention(q, k, v)
            out = out.transpose(0, 2, 1, 3).reshape(b, n, INNER)
            return out @ Wo

        def ffn_layer(x, g, bln, W1, b1, W2, b2):
            mu = x.mean(-1, keepdims=True)
            var = ((x - mu) ** 2).mean(-1, keepdims=True)
            xn = (x - mu) / jnp.sqrt(var + 1e-05) * g + bln
            hg = xn @ W1 + b1
            a, gate = jnp.split(hg, 2, -1)
            return a * jax.nn.gelu(gate, approximate=False) @ W2 + b2
        for i in range(DEPTH):
            x = attn_layer(shift_tokens(x), Wqkv[i], q_scale[i], k_scale[i], Wo[i]) + x
            x = ffn_layer(shift_tokens(x), ln_g[i], ln_b[i], W1[i], b1[i], W2[i], b2[i]) + x
        return x

    def _L1_attn_ref(X, W_Q, W_K, W_V, W_G, W_O, gn_weight, gn_bias):
        import math
        import jax, jax.numpy as jnp
        import numpy as np
        HEADS = 8
        SCALE_BASE = 512.0
        GN_EPS = 1e-05

        def _gammas(heads):
            return 1.0 - np.exp(np.linspace(math.log(1.0 / 32.0), math.log(1.0 / 512.0), heads))

        def _xpos(x, downscale):
            N, S, d = x.shape
            half = d // 2
            scale = (jnp.arange(0, d, 2, dtype=jnp.float32) + 0.4 * d) / (1.4 * d)
            pos = jnp.arange(S, dtype=jnp.float32)
            sc = scale[None, :] ** (pos / SCALE_BASE)[:, None]
            inv_freq = 1.0 / 10000.0 ** (jnp.arange(half, dtype=jnp.float32) / half)
            sinusoid = pos[:, None] * inv_freq[None, :]
            sin, cos = (jnp.sin(sinusoid), jnp.cos(sinusoid))
            if downscale:
                sc = 1.0 / sc
            sin_s = jnp.repeat(sin * sc, 2, axis=-1)
            cos_s = jnp.repeat(cos * sc, 2, axis=-1)
            x1, x2 = (x[..., ::2], x[..., 1::2])
            rot = jnp.stack((-x2, x1), axis=-1).reshape(x.shape)
            return x * cos_s + rot * sin_s
        B, S, H = X.shape
        h = HEADS
        d = H // h
        gammas = jnp.asarray(_gammas(h), dtype=X.dtype)
        Xh = X.reshape(B, S, h, d)
        Q = jnp.einsum('bshd,hde->bhse', Xh, W_Q)
        K = jnp.einsum('bshd,hde->bhse', Xh, W_K)
        V = jnp.einsum('bshd,hde->bhse', Xh, W_V)
        Q = _xpos(Q.reshape(B * h, S, d), downscale=False).reshape(B, h, S, d)
        K = _xpos(K.reshape(B * h, S, d), downscale=True).reshape(B, h, S, d)
        n = jnp.arange(S)
        diff = n[:, None] - n[None, :]
        causal = diff >= 0
        D = gammas[:, None, None] ** jnp.where(causal, diff, 0).astype(X.dtype) * causal[None].astype(X.dtype)
        att = jnp.einsum('bhsd,bhtd->bhst', Q, K) * D[None]
        Y = jnp.einsum('bhst,bhtd->bshd', att, V).reshape(B, S, H)
        Yg = Y.reshape(B * S, h, d)
        mu = Yg.mean(axis=-1, keepdims=True)
        var = Yg.var(axis=-1, keepdims=True)
        Yn = ((Yg - mu) / jnp.sqrt(var + GN_EPS)).reshape(B * S, H)
        Yn = (Yn * gn_weight + gn_bias).reshape(B, S, H)
        G = X @ W_G
        return G * jax.nn.sigmoid(G) * Yn @ W_O

    def _L1_ffn_ref(x, ln_gamma, ln_beta, router_w, w12, w3):
        import math
        import jax, jax.numpy as jnp
        import numpy as np
        D_MODEL = 128
        D_FF = 512
        E = 8
        K = 2
        CAP_FACTOR = 1.25
        CLAMP = 10000.0
        LN_EPS = 1e-05
        B, S = (2, 256)
        Bq, Sq, D = x.shape
        T = Bq * Sq
        mu = jnp.mean(x, axis=-1, keepdims=True)
        var = jnp.mean(jnp.square(x - mu), axis=-1, keepdims=True)
        xn = (x - mu) * jax.lax.rsqrt(var + LN_EPS) * ln_gamma + ln_beta
        xf = xn.reshape(T, D)
        logits = jnp.clip(xf @ router_w.T, -CLAMP, CLAMP)
        top_v, top_i = jax.lax.top_k(logits, K)
        m = jnp.max(top_v, axis=-1, keepdims=True)
        ev = jnp.exp(top_v - m)
        top_p = ev / (jnp.sum(ev, axis=-1, keepdims=True) + 1e-12)
        Stot = T * K
        experts = top_i.reshape(-1)
        weights = top_p.reshape(-1)
        tokens = jnp.repeat(jnp.arange(T), K)
        oh = (experts[:, None] == jnp.arange(E)[None, :]).astype(jnp.int32)
        pos = jnp.take_along_axis(jnp.cumsum(oh, axis=0) - 1, experts[:, None], axis=1)[:, 0]
        C = max(1, math.ceil(T * K * CAP_FACTOR / E))
        kept = pos < C
        slot = jnp.where(kept, experts * C + pos, E * C)
        buf = jnp.zeros((E * C + 1, D), x.dtype).at[slot].set(xf[tokens])
        xb = buf[:E * C].reshape(E, C, D)
        gu = jnp.einsum('ecd,efd->ecf', xb, w12)
        g, u = jnp.split(gu, 2, axis=-1)
        h = jax.nn.silu(g) * u
        yb = jnp.einsum('ecf,edf->ecd', h, w3).reshape(E * C, D)
        ys = yb[jnp.minimum(slot, E * C - 1)] * (weights * kept.astype(weights.dtype))[:, None]
        out = jnp.zeros((T, D), x.dtype).at[tokens].add(ys)
        return out.reshape(Bq, Sq, D)
    x = L0_attn_x
    x = _layernorm(x + _L0_attn_ref(x, L0_attn_Wqkv, L0_attn_bqkv, L0_attn_Wo, L0_attn_bo), axis=-1)
    x = _layernorm(x + _L0_ffn_ref(x, L0_ffn_Wqkv, L0_ffn_q_scale, L0_ffn_k_scale, L0_ffn_Wo, L0_ffn_ln_g, L0_ffn_ln_b, L0_ffn_W1, L0_ffn_b1, L0_ffn_W2, L0_ffn_b2), axis=-1)
    x = _layernorm(x + _L1_attn_ref(x, L1_attn_W_Q, L1_attn_W_K, L1_attn_W_V, L1_attn_W_G, L1_attn_W_O, L1_attn_gn_weight, L1_attn_gn_bias), axis=-1)
    x = _layernorm(x + _L1_ffn_ref(x, L1_ffn_ln_gamma, L1_ffn_ln_beta, L1_ffn_router_w, L1_ffn_w12, L1_ffn_w3), axis=-1)
    return x

_drawn_inputs = setup_inputs


def setup_inputs(seed=0):
    import zlib

    import numpy as np

    out = dict(_drawn_inputs(seed))
    spreads = {'L0_ffn_q_scale': (1.0, 0.6),
     'L0_ffn_k_scale': (1.0, 0.6),
     'L0_ffn_ln_g': (1.0, 0.6),
     'L0_ffn_ln_b': (0.0, 0.8),
     'L0_ffn_b1': (0.0, 0.526),
     'L0_ffn_b2': (0.0, 0.1),
     'L1_attn_gn_weight': (1.0, 0.6),
     'L1_attn_gn_bias': (0.0, 0.8),
     'L1_ffn_ln_gamma': (1.0, 0.2),
     'L1_ffn_ln_beta': (0.0, 0.1)}
    factors = {'L0_attn_bqkv': 3.859,
     'L0_ffn_W1': 2.855,
     'L0_ffn_W2': 2.909,
     'L1_attn_W_Q': 5.86,
     'L1_attn_W_K': 6.262,
     'L1_attn_W_V': 7.476,
     'L1_attn_W_G': 6.504,
     'L1_attn_W_O': 6.415}
    for name, (base, spread) in spreads.items():
        noise = np.random.default_rng([zlib.crc32(name.encode()), seed]).standard_normal(out[name].shape)
        drawn = base * np.exp(spread * noise) if base else spread * noise
        out[name] = jnp.asarray(drawn.astype(out[name].dtype))
    for name, factor in factors.items():
        out[name] = (out[name] * factor).astype(out[name].dtype)
    return out
```

```python
from contextlib import ExitStack

import concourse.bass as bass
from concourse import mybir

F32 = mybir.dt.float32
BF16 = mybir.dt.bfloat16
ALU = mybir.AluOpType
ACT = mybir.ActivationFunctionType
AX = mybir.AxisListType

P = 128
B, S, D = 2, 1024, 128
T = B * S
EPS = 1e-5
CHUNK = 512
CHUNKS = T // CHUNK

A_HEADS, A_HD = 16, 8
A_COLS = D // A_HD
A_TOK = S // A_HEADS
A_TILES = T // P
A_SCALE = A_HD ** -0.5

DEPTH, HEADS, HD, WIN = 6, 16, 64, 32
GROUP = 8
PAIRS = GROUP // 2
UNITS = B * HEADS // GROUP
GCOLS = GROUP * HD
QTILE = 96
QTILES = -(-S // QTILE)
TTILES = S // P
FF = int(D * 4 * 2 / 3)
FF_PARTS = [(0, 128), (128, 128), (256, FF - 256)]
QK_SCALE = 8.0

R_HEADS, R_HD = 8, 16
R_CHUNKS = S // P

EXPERTS, D_FF, TOPK = 8, 512, 2
CAP = max(1, -(-T * TOPK * 5 // (4 * EXPERTS)))
CLAMP = 10000.0
E_TILES = T // P
F_PARTS = D_FF // P
CHOSEN, TOPS = 13, 14
SQUARE = TOPS + 6 + E_TILES + 2 + 4
ROOT = SQUARE + 2
FINAL = ROOT + 2


def q_tile(t):
    q0 = t * QTILE
    nq = min(QTILE, S - q0)
    k0 = max(0, q0 - WIN)
    return q0, nq, k0, q0 + nq - k0


class Core:

    def __init__(self, nc, stack, prefix=""):
        self.nc, self.stack, self.prefix = nc, stack, prefix

    def sb(self, name, shape, dt=F32):
        return self.stack.enter_context(self.nc.sbuf_tensor(self.prefix + name, shape, dt))

    def psum(self, name, shape, dt=F32):
        return self.stack.enter_context(self.nc.psum_tensor(self.prefix + name, shape, dt))

    def sem(self, name):
        return self.stack.enter_context(self.nc.semaphore(self.prefix + name))


def load_constants(nc, keep, consts):
    with ExitStack() as stack:
        core = Core(nc, stack)
        loaded, cast = core.sem("const_loaded"), core.sem("const_cast")
        block = stack.enter_context(nc.Block())

        @block.sync
        def _(sp):
            sp.dma_start(keep["ident"][:], consts["c_ident"]).then_inc(loaded, 16)
            sp.wait_ge(loaded, 16)

        @block.vector
        def _(dve):
            dve.wait_ge(loaded, 16)
            nc.vector.tensor_copy(keep["identb"][:], keep["ident"][:]).then_inc(cast, 1)
            nc.vector.memset(keep["mean_w"][:], 1.0 / D).then_inc(cast, 1)
            dve.wait_ge(cast, 2)


def attention_stage(nc, keep, x, w_in_t, b_in, w_out_t, b_out, sel):
    resid, ident, identb = keep["resid"], keep["ident"], keep["identb"]
    with ExitStack() as stack:
        core = Core(nc, stack, "a_")
        sb, psum, sem = core.sb, core.psum, core.sem
        KROWS = 96
        XROWS = KROWS + 2
        x_tok = sb("x_tok", [P, 2, D])
        x_t = sb("x_t", [P, D])
        w_in = sb("w_in", [P, 3 * D])
        b_bc = sb("b_bc", [P, 3 * D])
        w_out = sb("w_out", [64, 2, D])
        b_col = sb("b_col", [P, 1])
        selm = sb("selm", [P, 18])
        qkv = sb("qkv", [P, A_COLS, 24])
        part = sb("part", [P, 3, A_COLS, 16], BF16)
        rest = sb("rest", [P, A_COLS, 16])
        q_arr = sb("q_arr", [P, A_COLS, KROWS], BF16)
        k_arr = sb("k_arr", [P, A_COLS, KROWS], BF16)
        v_two = sb("v_two", [P, A_COLS, 32])
        q_st = sb("q_st", [P, 2, A_COLS, A_TOK], BF16)
        k_st = sb("k_st", [P, 2, A_COLS, A_TOK], BF16)
        neg_max = sb("neg_max", [P, 2 * 8])
        max_part = sb("max_part", [P, 2 * 8, 2], BF16)
        probs = sb("probs", [P, 2, S])
        vals_t = sb("vals_t", [P, S])
        recip = sb("recip", [P, 8, 2])
        vals = sb("vals", [P, 2, 8, A_HD])
        feat = sb("feat", [64, 2, P])
        score = psum("score", [P, 4, CHUNK])
        acc = psum("acc", [P, 2, CHUNK])
        small = psum("small", [P, 2, CHUNK])

        loaded = sem("weights_loaded")
        x_in = sem("x_in")
        zeroed = sem("zeroed")
        xt_ready, xt_kept = sem("xt_ready"), sem("xt_kept")
        qkv_ready, qkv_kept = sem("qkv_ready"), sem("qkv_kept")
        split = sem("split")
        arranged = sem("arranged")
        stacked, stack_kept = sem("stacked"), sem("stack_kept")
        raw_ready, maxed = sem("raw_ready"), sem("maxed")
        max_split, max_rows, max_kept = sem("max_split"), sem("max_rows"), sem("max_kept")
        score_ready, exp_done, pv_done = sem("score_ready"), sem("exp_done"), sem("pv_done")
        acc_kept = sem("acc_kept")
        folded, inverted, normed = sem("folded"), sem("inverted"), sem("normed")
        turned, turn_kept = sem("turned"), sem("turn_kept")
        projected, added = sem("projected"), sem("added")
        block = stack.enter_context(nc.Block())

        @block.sync
        def _(sp):
            sp.dma_start(w_in[:], w_in_t).then_inc(loaded, 16)
            sp.dma_start(b_bc[:], b_in.unsqueeze(0).broadcast_to([P, 3 * D])).then_inc(loaded, 16)
            sp.dma_start(w_out[:], w_out_t).then_inc(loaded, 16)
            sp.dma_start(b_col[:], b_out.unsqueeze(1)).then_inc(loaded, 16)
            sp.dma_start(selm[:], sel).then_inc(loaded, 16)
            with sp.Fori(0, A_TILES) as i:
                sp.wait_ge(xt_ready, i)
                sp.dma_start(x_tok[:, 0, :], x[bass.ts(i, P), :]).then_inc(x_in, 16)

        @block.tensor
        def _(pe):
            pe.wait_ge(loaded, 80)
            pe.wait_ge(zeroed, 8)
            with pe.Fori(0, A_TILES) as i:
                pe.wait_ge(x_in, i * 16 + 16)
                pe.wait_ge(turn_kept, i)
                nc.tensor.transpose(small[:, 1, 0:P], x_tok[:, 0, :], ident[:]).then_inc(xt_ready, 1)
                pe.wait_ge(xt_kept, i + 1)
                pe.wait_ge(added, i)
                nc.tensor.matmul(small[:, 0, 0:3 * D], x_t[:], w_in[:], start=True, stop=True).then_inc(qkv_ready, 1)
                for n in range(8):
                    arr = q_arr if n < 4 else k_arr
                    pe.wait_ge(arranged, i * 8 + (3 if n < 4 else 6))
                    if n < 4:
                        pe.wait_ge(exp_done, i * 16)
                    else:
                        pe.wait_ge(stack_kept, i * 8 + n - 3)
                    for c in range(4):
                        last = nc.tensor.matmul(score[0:KROWS, n % 4, c * P:(c + 1) * P], arr[:, 4 * (n % 4) + c, :],
                                                identb[:], start=True, stop=True)
                    last.then_inc(stacked, 1)
                pe.wait_ge(stack_kept, i * 8 + 8)
                for n in range(16):
                    h, qb = n // 8, n % 8
                    if n >= 2:
                        pe.wait_ge(maxed, i * 16 + n - 1)
                    for j in range(2):
                        last = nc.tensor.matmul(score[:, 2 * (n % 2) + j, :], q_st[0:KROWS, h, 2 * qb:2 * qb + 2, :],
                                                k_st[0:KROWS, h, 8 * j:8 * j + 8, :], start=True, stop=True)
                    last.then_inc(raw_ready, 1)
                pe.wait_ge(max_split, i * 2 + 2)
                for n in range(16):
                    last = nc.tensor.matmul(score[KROWS:XROWS, n // 4, (n % 4) * P:(n % 4 + 1) * P],
                                            max_part[:, n, :], identb[:], start=True, stop=True)
                last.then_inc(max_rows, 1)
                pe.wait_ge(max_kept, i + 1)
                pe.wait_ge(acc_kept, i)

                def values(c):
                    pe.wait_ge(exp_done, i * 16 + c + 1)
                    for j in range(2):
                        last = nc.tensor.matmul(acc[32 * (c % 4):32 * (c % 4) + 32, j, :], v_two[:, c, :],
                                                probs[:, c % 2, j * CHUNK:(j + 1) * CHUNK],
                                                start=(c < 4), stop=(c >= A_COLS - 4))
                    last.then_inc(pv_done, 1)

                pe.wait_ge(arranged, i * 8 + 8)
                for c in range(A_COLS):
                    if c >= 2:
                        pe.wait_ge(exp_done, i * 16 + c - 1)
                    for j in range(2):
                        for h in range(2):
                            last = nc.tensor.matmul(score[64 * h:64 * h + 64, 2 * (c % 2) + j, :], k_st[0:XROWS, h, c, :],
                                                    q_st[0:XROWS, h, 8 * j:8 * j + 8, :], start=True, stop=True)
                    last.then_inc(score_ready, 1)
                    if c >= 1:
                        values(c - 1)
                values(A_COLS - 1)
                pe.wait_ge(acc_kept, i + 1)
                for n in range(8):
                    last = nc.tensor.matmul(small[:, 0, 18 * n:18 * n + 18], vals_t[:, n * P:(n + 1) * P], selm[:],
                                            start=True, stop=True)
                last.then_inc(folded, 1)
                pe.wait_ge(normed, i + 1)
                for h in range(2):
                    last = nc.tensor.matmul(small[0:64, 1, h * P:(h + 1) * P], vals[:, h, :, :], ident[:], start=True, stop=True)
                last.then_inc(turned, 1)
                pe.wait_ge(turn_kept, i + 1)
                for half in range(2):
                    last = nc.tensor.matmul(small[:, 0, 0:P], w_out[:, half, :], feat[:, half, :],
                                            start=(half == 0), stop=(half == 1))
                last.then_inc(projected, 1)

        @block.scalar
        def _(act):
            act.wait_ge(zeroed, 8)
            with act.Fori(0, A_TILES) as i:
                act.wait_ge(split, i * 4 + 4)
                for g in range(3):
                    nc.scalar.activation(q_arr[:, :, 32 * g:32 * g + 24].rearrange("p c (r d) -> p c r d", r=3),
                                         part[:, g, :, 0:8].unsqueeze(2).broadcast_to([P, A_COLS, 3, 8]), ACT.Copy)\
                        .then_inc(arranged, 1)
                for g in range(3):
                    nc.scalar.activation(k_arr[:, :, 32 * g:32 * g + 24].rearrange("p c (r d) -> p c r d", r=3),
                                         part[:, :, :, 8:16].rearrange("p r c d -> p c r d"), ACT.Copy).then_inc(arranged, 1)
                act.wait_ge(pv_done, i * 16)
                nc.scalar.activation(v_two[0:64, :, 0:8], qkv[0:64, :, 16:24], ACT.Copy).then_inc(arranged, 1)
                nc.scalar.activation(v_two[64:P, :, 16:24], qkv[64:P, :, 16:24], ACT.Copy).then_inc(arranged, 1)
                for n in range(8):
                    act.wait_ge(stacked, i * 8 + n + 1)
                    st = q_st if n < 4 else k_st
                    c0 = 4 * (n % 4)
                    nc.scalar.activation(
                        st[0:KROWS, :, c0:c0 + 4, :].rearrange("p h c t -> p c h t"),
                        score[0:KROWS, n % 4, :].rearrange("p (c h t) -> p c h t", c=4, h=2),
                        ACT.Copy).then_inc(stack_kept, 1)
                act.wait_ge(max_rows, i + 1)
                nc.scalar.activation(q_st[KROWS:XROWS, :, :, :].rearrange("p h c t -> p (h c t)"),
                                     score[KROWS:XROWS, :, :].rearrange("p a n -> p (a n)"), ACT.Copy).then_inc(max_kept, 1)
                for c in range(A_COLS):
                    act.wait_ge(score_ready, i * 16 + c + 1)
                    if c >= 2:
                        act.wait_ge(pv_done, i * 16 + c - 1)
                    nc.scalar.activation(probs[:, c % 2, :], score[:, 2 * (c % 2):2 * (c % 2) + 2, :].rearrange("p a n -> p (a n)"),
                                         ACT.Exp, scale=A_SCALE).then_inc(exp_done, 1)

        @block.gpsimd
        def _(pool):
            for n, (dst, value) in enumerate(((q_arr[:], 0.0), (k_arr[:], 0.0), (v_two[:], 0.0), (k_st[96:P], 1.0), (q_st[96:P], 0.0),
                                              (vals_t[:], 0.0), (v_two[0:64, :, 8:9], 1.0), (v_two[64:P, :, 24:25], 1.0))):
                nc.gpsimd.memset(dst, value).then_inc(zeroed, 1)
                pool.wait_ge(zeroed, n + 1)

        @block.vector
        def _(dve):
            dve.wait_ge(loaded, 80)
            with dve.Fori(0, A_TILES) as i:
                dve.wait_ge(xt_ready, i + 1)
                dve.wait_ge(added, i)
                nc.vector.tensor_copy(x_t[:], small[:, 1, 0:P]).then_inc(xt_kept, 1)
                dve.wait_ge(qkv_ready, i + 1)
                dve.wait_ge(arranged, i * 8)
                nc.vector.tensor_tensor(qkv[:].rearrange("p c e -> p (c e)"), small[:, 0, 0:3 * D], b_bc[:], ALU.add)\
                    .then_inc(qkv_kept, 1)
                dve.wait_ge(qkv_kept, i + 1)
                nc.vector.tensor_copy(part[:, 0], qkv[:, :, 0:16]).then_inc(split, 1)
                dve.wait_ge(split, i * 4 + 1)
                nc.vector.tensor_tensor(rest[:], qkv[:, :, 0:16], part[:, 0], ALU.subtract).then_inc(split, 1)
                dve.wait_ge(split, i * 4 + 2)
                nc.vector.tensor_copy(part[:, 1], rest[:]).then_inc(split, 1)
                dve.wait_ge(split, i * 4 + 3)
                nc.vector.tensor_tensor(part[:, 2], rest[:], part[:, 1], ALU.subtract).then_inc(split, 1)
                for n in range(16):
                    dve.wait_ge(raw_ready, i * 16 + n + 1)
                    nc.vector.tensor_reduce(neg_max[:, n:n + 1], score[:, 2 * (n % 2):2 * (n % 2) + 2, :], AX.XY, ALU.max,
                                            negate=True).then_inc(maxed, 1)
                dve.wait_ge(maxed, i * 16 + 16)
                nc.vector.tensor_copy(max_part[:, :, 0], neg_max[:]).then_inc(max_split, 1)
                dve.wait_ge(max_split, i * 2 + 1)
                nc.vector.tensor_tensor(max_part[:, :, 1], neg_max[:], max_part[:, :, 0], ALU.subtract).then_inc(max_split, 1)
                dve.wait_ge(pv_done, i * 16 + 16)
                nc.vector.tensor_copy(vals_t[:], acc[:].rearrange("p a n -> p (a n)")).then_inc(acc_kept, 1)
                dve.wait_ge(folded, i + 1)
                fold = small[:, 0, 0:144].rearrange("p (c h e) -> p c h e", c=8, h=2)
                nc.vector.reciprocal(recip[:], fold[:, :, :, 8]).then_inc(inverted, 1)
                dve.wait_ge(inverted, i + 1)
                nc.vector.tensor_tensor(vals[:].rearrange("p h c d -> p c h d"), fold[:, :, :, 0:8],
                                        recip[:].unsqueeze(3).broadcast_to([P, 8, 2, A_HD]), ALU.mult).then_inc(normed, 1)
                dve.wait_ge(turned, i + 1)
                nc.vector.tensor_copy(feat[:].rearrange("p a (h t) -> p h a t", h=2),
                                      small[0:64, 1, 0:2 * P].rearrange("p (h a t) -> p h a t", h=2, a=2)).then_inc(turn_kept, 1)
                dve.wait_ge(projected, i + 1)
                nc.vector.scalar_tensor_tensor(out=resid[:, bass.ts(i, P)], in0=small[:, 0, 0:P], scalar=b_col[:],
                                               in1=x_t[:], op0=ALU.add, op1=ALU.add).then_inc(added, 1)


NORM_STEPS = "mean_ready centred squared var_ready eps_added rooted inverted normed"


def norm_semaphores(core):
    return {n: core.sem("n_" + n) for n in NORM_STEPS.split()}


def norm_stage(nc, keep, call, out=None, affine=None):
    resid, mean_w = keep["resid"], keep["mean_w"]
    out = resid if out is None else out
    with ExitStack() as stack:
        core = Core(nc, stack, f"n{call}_")
        centre = core.sb("centre", [P, CHUNKS, CHUNK])
        square = core.sb("square", [P, CHUNKS, CHUNK])
        std = core.sb("std", [P, CHUNKS, CHUNK])
        rstd = core.sb("rstd", [P, CHUNKS, CHUNK])
        gain = core.sb("gain", [P, 2])
        mean = core.psum("mean_ps", [P, CHUNKS, CHUNK])
        var = core.psum("var_ps", [P, CHUNKS, CHUNK])
        mean_ready, centred, squared, var_ready, eps_added, rooted, inverted, normed = (keep["norm_sems"][n] for n in NORM_STEPS.split())
        gain_in, scaled = (core.sem("gain_in"), core.sem("scaled")) if affine else (None, None)
        past = call * CHUNKS
        block = stack.enter_context(nc.Block())

        @block.sync
        def _(sp):
            if affine:
                for n in range(2):
                    sp.dma_start(gain[:, n:n + 1], affine[n].unsqueeze(1)).then_inc(gain_in, 16)
                sp.wait_ge(gain_in, 32)

        @block.tensor
        def _(pe):
            for c in range(CHUNKS):
                nc.tensor.matmul(mean[:, c, :], mean_w[:], resid[:, c * CHUNK:(c + 1) * CHUNK], start=True, stop=True)\
                    .then_inc(mean_ready, 1)
            for c in range(CHUNKS):
                pe.wait_ge(squared, past + c + 1)
                nc.tensor.matmul(var[:, c, :], mean_w[:], square[:, c, :], start=True, stop=True).then_inc(var_ready, 1)

        @block.scalar
        def _(act):
            for c in range(CHUNKS):
                act.wait_ge(centred, past + c + 1)
                nc.scalar.activation(square[:, c, :], centre[:, c, :], ACT.Square).then_inc(squared, 1)
            for c in range(CHUNKS):
                act.wait_ge(eps_added, past + c + 1)
                nc.scalar.activation(std[:, c, :], std[:, c, :], ACT.Sqrt).then_inc(rooted, 1)

        @block.vector
        def _(dve):
            for c in range(CHUNKS):
                dve.wait_ge(mean_ready, past + c + 1)
                nc.vector.tensor_tensor(centre[:, c, :], resid[:, c * CHUNK:(c + 1) * CHUNK], mean[:, c, :], ALU.subtract)\
                    .then_inc(centred, 1)
            for c in range(CHUNKS):
                dve.wait_ge(var_ready, past + c + 1)
                nc.vector.tensor_scalar(std[:, c, :], var[:, c, :], EPS, None, ALU.add).then_inc(eps_added, 1)
            for c in range(CHUNKS):
                cols = slice(c * CHUNK, (c + 1) * CHUNK)
                dve.wait_ge(rooted, past + c + 1)
                nc.vector.reciprocal(rstd[:, c, :], std[:, c, :]).then_inc(inverted, 1)
                dve.wait_ge(inverted, past + c + 1)
                nc.vector.tensor_tensor(out[:, cols], centre[:, c, :], rstd[:, c, :], ALU.mult).then_inc(normed, 1)
                if affine:
                    dve.wait_ge(gain_in, 32)
                    dve.wait_ge(normed, past + c + 1)
                    nc.vector.tensor_scalar(out[:, cols], out[:, cols], gain[:, 0:1], gain[:, 1:2], ALU.mult, ALU.add)\
                        .then_inc(scaled, 1)
            dve.wait_ge(normed, past + CHUNKS)
            if affine:
                dve.wait_ge(scaled, CHUNKS)


def local_stage(nc, keep, w_qkv, q_scale, k_scale, w_out, ln_g, ln_b, w1, b1, w2, b2, rotary, band):
    resid, ident, identb, mean_w = (keep[k] for k in ("resid", "ident", "identb", "mean_w"))
    GROUPS = HEADS // GROUP
    NF = len(FF_PARTS)
    FF_LOADS = (1 + 3 * NF + 3) * 16
    HALF = HD // 2
    with ExitStack() as stack:
        core = Core(nc, stack, "b_")
        sb, sem = core.sb, core.sem
        stream = sb("stream", [P, B, S])
        shifted = sb("shifted", [P, B, S])
        xs = sb("xs", [P, S])
        w_qk = sb("w_qk", [P, 2, GCOLS])
        w_v = sb("w_v", [P, GCOLS])
        w_o = sb("w_o", [P, PAIRS, D])
        rot = sb("rot", [P, 4, TTILES, HD])
        scale_bc = sb("scale_bc", [P, 2, HD])
        tab = sb("tab", [P, 4, TTILES, HD])
        band_f = sb("band_f", [QTILE, P])
        band_b = sb("band_b", [QTILE, P], BF16)
        square = sb("square", [P, 2, 2 * GROUP, HD])
        norm = sb("norm", [P, 2 * GROUP])
        sum_sq = sb("sum_sq", [P, 2 * GROUP])
        clipped = sb("clipped", [P, 2 * GROUP])
        inv_norm = sb("inv_norm", [P, 2 * GROUP])
        unit = sb("unit", [P, 2 * GROUP, HD])
        with_cos = sb("with_cos", [P, 2, GROUP, HD])
        with_sin = sb("with_sin", [P, 2, GROUP, HD])
        turned = sb("turned", [P, 2, GROUP, HD])
        k_t = sb("k_t", [P, PAIRS, S])
        q_t = sb("q_t", [P, PAIRS, 2, S])
        v_tok = sb("v_tok", [P, QTILES, GCOLS])
        neg_max = sb("neg_max", [QTILE, GROUP])
        neg_bias = sb("neg_bias", [QTILE, 2, GROUP])
        probs = sb("probs", [QTILE, 2, GROUP, P])
        row_sum = sb("row_sum", [QTILE, 2, GROUP])
        inv_sum = sb("inv_sum", [QTILE, 2, GROUP])
        normed = sb("normed", [QTILE, 2, GROUP, P])
        probs_t = sb("probs_t", [P, 2, GROUP, QTILE])
        att = sb("att", [P, 2, PAIRS, QTILE])
        w1_s = sb("w1_s", [P, 2 * FF])
        w2_s = sb("w2_s", [P, NF, D])
        ln_s = sb("ln_s", [P, 2])
        b1_s = sb("b1_s", [P, 2, NF])
        b2_s = sb("b2_s", [P, 1])
        centre = sb("centre", [P, CHUNKS, CHUNK])
        spread = sb("spread", [P, CHUNKS, CHUNK])
        gate = sb("gate", [P, 2, CHUNK])
        hidden = sb("hidden", [P, NF, CHUNK])
        banks = core.psum("banks", [P, 8, CHUNK])
        flat = stream[:].rearrange("p b s -> p (b s)")
        flat_shifted = shifted[:].rearrange("p b s -> p (b s)")

        names = """consts zeroed band_ready begun shift_a shift_f scale_in tab_ready wqkv_in wo_in wf_in xs_ready
            qk_ready squared summed clip_done rooted unit_ready cos_ready sin_ready turn_ready qkt_ready qkt_kept
            v_ready v_kept score_ready maxed bias_ready exp_done inverted p_normed p_turned pt_kept att_ready att_kept
            out_ready added f_mean f_centred f_squared f_var f_eps f_root f_normed f_affine f_gate f_gelu f_a f_hid
            f_out f_added final reload_ok f_inverted norm_inv"""
        (consts, zeroed, band_ready, begun, shift_a, shift_f, scale_in, tab_ready, wqkv_in, wo_in, wf_in, xs_ready,
         qk_ready, squared, summed, clip_done, rooted, unit_ready, cos_ready, sin_ready, turn_ready, qkt_ready, qkt_kept,
         v_ready, v_kept, score_ready, maxed, bias_ready, exp_done, inverted, p_normed, p_turned, pt_kept, att_ready, att_kept,
         out_ready, added, f_mean, f_centred, f_squared, f_var, f_eps, f_root, f_normed, f_affine, f_gate, f_gelu, f_a, f_hid,
         f_out, f_added, final, reload_ok, f_inverted, norm_inv) = (sem(n) for n in names.split())
        block = stack.enter_context(nc.Block())

        def qk_banks(t):
            return banks[:, 6 * (t % 2):6 * (t % 2) + 2, :]

        @block.sync
        def _(sp):
            sp.dma_start(rot[:], rotary).then_inc(consts, 16)
            sp.dma_start(band_f[:], band).then_inc(consts, 16)
            with sp.Fori(0, DEPTH) as l:
                sp.wait_ge(tab_ready, l * 6)
                sp.sem_inc(reload_ok, 1)
                sp.dma_start(scale_bc[:, 0, :], q_scale[bass.ds(l, 1), :].broadcast_to([P, HD])).then_inc(scale_in, 16)
                sp.dma_start(scale_bc[:, 1, :], k_scale[bass.ds(l, 1), :].broadcast_to([P, HD])).then_inc(scale_in, 16)
                sp.wait_ge(f_added, l * CHUNKS)
                sp.sem_inc(reload_ok, 1)
                sp.dma_start(w1_s[:], w1[bass.ds(l, 1), :, :].rearrange("a p n -> p (a n)")).then_inc(wf_in, 16)
                for n, (f0, fn) in enumerate(FF_PARTS):
                    sp.dma_start(w2_s[0:fn, n, :], w2[bass.ds(l, 1), f0:f0 + fn, :].rearrange("a p n -> p (a n)")).then_inc(wf_in, 16)
                    for side in range(2):
                        sp.dma_start(b1_s[0:fn, side, n:n + 1],
                                     b1[bass.ds(l, 1), side * FF + f0:side * FF + f0 + fn].rearrange("a p -> p a")).then_inc(wf_in, 16)
                sp.dma_start(b2_s[:], b2[bass.ds(l, 1), :].rearrange("a p -> p a")).then_inc(wf_in, 16)
                sp.dma_start(ln_s[:, 0:1], ln_g[bass.ds(l, 1), :].rearrange("a p -> p a")).then_inc(wf_in, 16)
                sp.dma_start(ln_s[:, 1:2], ln_b[bass.ds(l, 1), :].rearrange("a p -> p a")).then_inc(wf_in, 16)
                with sp.Fori(0, GROUPS) as g:
                    lg = l * GROUPS + g
                    sp.wait_ge(qk_ready, lg * (B * TTILES))
                    sp.sem_inc(reload_ok, 1)
                    sp.wait_ge(v_ready, lg * (B * QTILES))
                    sp.sem_inc(reload_ok, 1)
                    for m in range(2):
                        sp.dma_start(w_qk[:, m, :], w_qkv[bass.ds(l * (3 * GROUPS) + g + m * GROUPS, 1), :, :]
                                     .rearrange("a p n -> p (a n)")).then_inc(wqkv_in, 16)
                    sp.dma_start(w_v[:], w_qkv[bass.ds(l * (3 * GROUPS) + g + 2 * GROUPS, 1), :, :]
                                 .rearrange("a p n -> p (a n)")).then_inc(wqkv_in, 16)
                    sp.wait_ge(out_ready, lg * (B * QTILES))
                    sp.sem_inc(reload_ok, 1)
                    sp.dma_start(w_o[:], w_out[bass.ds(lg, 1), :, :, :].rearrange("a p h n -> p (a h) n")).then_inc(wo_in, 16)

        @block.tensor
        def _(pe):
            def turn_tile(u, t):
                pe.wait_ge(turn_ready, u * TTILES + t + 1)
                pe.wait_ge(qkt_kept, u * TTILES + t)
                if t == 0:
                    pe.wait_ge(added, u * QTILES)
                for m in range(2):
                    for h in range(PAIRS):
                        last = nc.tensor.transpose(banks[:, 2 + m, h * P:(h + 1) * P], turned[:, m, 2 * h:2 * h + 2, :], ident[:])
                last.then_inc(qkt_ready, 1)

            def value_rows(u, t):
                _, _, k0, nk = q_tile(t)
                if t == 0:
                    pe.wait_ge(exp_done, u * QTILES)
                if t >= 2:
                    pe.wait_ge(v_kept, u * QTILES + t - 1)
                nc.tensor.matmul(banks[0:nk, 4 + t % 2, :], xs[:, k0:k0 + nk], w_v[:], start=True, stop=True).then_inc(v_ready, 1)

            def scores(u, t):
                q0, nq, k0, nk = q_tile(t)
                if t == 0:
                    pe.wait_ge(qkt_kept, u * TTILES + TTILES)
                    pe.wait_ge(v_kept, u * QTILES + QTILES)
                pe.wait_ge(exp_done, u * QTILES + t)
                off = WIN - (q0 - k0)
                for half in range(2):
                    out = banks[0:nq, 4 + half, :].rearrange("p (h k) -> p h k", h=4)[:, :, 0:nk]
                    nc.tensor.matmul(out, identb[0:QTILE, 0:nq],
                                     band_b[:, off:off + nk].unsqueeze(1).broadcast_to([QTILE, 4, nk]),
                                     start=True, stop=False, skip_group_check=True)
                    for n in range(4):
                        h = 4 * half + n
                        last = nc.tensor.matmul(out[:, n, :], q_t[:, h // 2, h % 2, q0:q0 + nq], k_t[:, h // 2, k0:k0 + nk],
                                                start=False, stop=(n == 3), skip_group_check=True)
                last.then_inc(score_ready, 1)

            def values(u, t):
                _, nq, _, nk = q_tile(t)
                w = t % 2
                pe.wait_ge(p_normed, u * QTILES + t + 1)
                pe.wait_ge(pt_kept, u * QTILES + t)
                for h in range(GROUP):
                    last = nc.tensor.matmul(banks[0:nk, 6 + h // 4, (h % 4) * P:(h % 4) * P + nq], normed[0:nq, w, h, 0:nk],
                                            ident[0:nq, 0:nq], start=True, stop=True, is_transpose=nq == QTILE)
                last.then_inc(p_turned, 1)
                pe.wait_ge(pt_kept, u * QTILES + t + 1)
                if t >= 2:
                    pe.wait_ge(att_kept, u * QTILES + t - 1)
                for h in range(GROUP):
                    r = HD * (h % 2)
                    last = nc.tensor.matmul(banks[r:r + HD, w, (h // 2) * P:(h // 2) * P + nq], v_tok[0:nk, t, h * HD:(h + 1) * HD],
                                            probs_t[0:nk, w, h, 0:nq], start=True, stop=True)
                last.then_inc(att_ready, 1)

            def project(u, t):
                _, nq, _, _ = q_tile(t)
                w = t % 2
                pe.wait_ge(att_kept, u * QTILES + t + 1)
                if t >= 2:
                    pe.wait_ge(added, u * QTILES + t - 1)
                for h in range(PAIRS):
                    last = nc.tensor.matmul(banks[:, 2 + w, 0:nq], w_o[:, h, :], att[:, w, h, 0:nq], start=(h == 0), stop=(h == PAIRS - 1))
                last.then_inc(out_ready, 1)

            pe.wait_ge(band_ready, 1)
            pe.wait_ge(zeroed, 2)
            with pe.Fori(0, DEPTH) as l:
                with pe.Fori(0, GROUPS) as g:
                    lg = l * GROUPS + g
                    with pe.Fori(0, B) as b:
                        u = lg * B + b
                        pe.wait_ge(wqkv_in, lg * 48 + 48)
                        pe.wait_ge(wo_in, lg * 16 + 16)
                        pe.wait_ge(xs_ready, u + 1)
                        pe.wait_ge(att_kept, u * QTILES)
                        pe.wait_ge(pt_kept, u * QTILES)
                        for t in range(QTILES):
                            if t < TTILES:
                                if t >= 2:
                                    pe.wait_ge(unit_ready, u * TTILES + t - 1)
                                for m in range(2):
                                    last = nc.tensor.matmul(qk_banks(t)[:, m, :], xs[:, t * P:(t + 1) * P], w_qk[:, m, :],
                                                            start=True, stop=True)
                                last.then_inc(qk_ready, 1)
                            value_rows(u, t)
                            if 1 <= t <= TTILES:
                                turn_tile(u, t - 1)
                        pe.wait_ge(unit_ready, u * TTILES + TTILES)
                        for t in range(QTILES + 2):
                            if t < QTILES:
                                scores(u, t)
                            if 1 <= t <= QTILES:
                                values(u, t - 1)
                            if t >= 2:
                                project(u, t - 2)
                pe.wait_ge(wf_in, l * FF_LOADS + FF_LOADS)
                pe.wait_ge(shift_f, l * 2 + 2)
                for c in range(CHUNKS):
                    nc.tensor.matmul(banks[:, c, :], mean_w[:], flat_shifted[:, c * CHUNK:(c + 1) * CHUNK], start=True, stop=True)\
                        .then_inc(f_mean, 1)
                for c in range(CHUNKS):
                    pe.wait_ge(f_squared, l * CHUNKS + c + 1)
                    nc.tensor.matmul(banks[:, 4 + c, :], mean_w[:], spread[:, c, :], start=True, stop=True).then_inc(f_var, 1)
                pe.wait_ge(f_centred, l * CHUNKS + CHUNKS)
                for c in range(CHUNKS):
                    pe.wait_ge(f_affine, l * CHUNKS + c + 1)
                    for n, (f0, fn) in enumerate(FF_PARTS):
                        k = c * NF + n
                        if k >= 2:
                            pe.wait_ge(f_hid, l * (CHUNKS * NF) + k - 1)
                        nc.tensor.matmul(banks[0:fn, k % 2, :], w1_s[:, FF + f0:FF + f0 + fn], centre[:, c, :], start=True, stop=True)\
                            .then_inc(f_gate, 1)
                        nc.tensor.matmul(banks[0:fn, 2 + k % 2, :], w1_s[:, f0:f0 + fn], centre[:, c, :], start=True, stop=True)\
                            .then_inc(f_a, 1)
                    pe.wait_ge(f_hid, l * (CHUNKS * NF) + (c + 1) * NF)
                    pe.wait_ge(f_eps, l * CHUNKS + CHUNKS)
                    if c >= 2:
                        pe.wait_ge(f_added, l * CHUNKS + c - 1)
                    for n, (f0, fn) in enumerate(FF_PARTS):
                        last = nc.tensor.matmul(banks[:, 4 + c % 2, :], w2_s[0:fn, n, :], hidden[0:fn, n, :], start=(n == 0), stop=(n == NF - 1))
                    last.then_inc(f_out, 1)

        @block.scalar
        def _(act):
            def keep_turned(u, t):
                act.wait_ge(qkt_ready, u * TTILES + t + 1)
                if t == 0:
                    act.wait_ge(score_ready, u * QTILES)
                cols = slice(t * P, (t + 1) * P)
                nc.scalar.activation(q_t[0:HD, :, 0, cols], banks[0:HD, 2, :].rearrange("p (h s) -> p h s", h=PAIRS), ACT.Copy)
                nc.scalar.activation(q_t[HD:P, :, 1, cols], banks[HD:P, 2, :].rearrange("p (h s) -> p h s", h=PAIRS), ACT.Copy)
                nc.scalar.activation(k_t[:, :, cols], banks[:, 3, :].rearrange("p (h s) -> p h s", h=PAIRS), ACT.Copy)\
                    .then_inc(qkt_kept, 1)

            def keep_values(u, t):
                _, nq, _, _ = q_tile(t)
                w = t % 2
                act.wait_ge(att_ready, u * QTILES + t + 1)
                if t >= 2:
                    act.wait_ge(out_ready, u * QTILES + t - 1)
                if t == 0:
                    act.wait_ge(out_ready, u * QTILES)
                nc.scalar.activation(att[:, w, :, 0:nq], banks[:, w, :].rearrange("p (h s) -> p h s", h=PAIRS)[:, :, 0:nq], ACT.Copy)\
                    .then_inc(att_kept, 1)

            act.wait_ge(zeroed, 2)
            with act.Fori(0, DEPTH) as l:
                with act.Fori(0, UNITS) as v:
                    u = l * UNITS + v
                    for t in range(QTILES):
                        _, _, _, nk = q_tile(t)
                        if t < TTILES:
                            act.wait_ge(qk_ready, u * TTILES + t + 1)
                            if t >= 2:
                                act.wait_ge(summed, u * TTILES + t - 1)
                            if t == 0:
                                act.wait_ge(summed, u * TTILES)
                            nc.scalar.activation(square[:, t % 2, :, :].rearrange("p h d -> p (h d)"),
                                                 qk_banks(t).rearrange("p m n -> p (m n)"), ACT.Square).then_inc(squared, 1)
                        if t < TTILES:
                            act.wait_ge(summed, u * TTILES + t + 1)
                            nc.scalar.activation(norm[:], sum_sq[:], ACT.Sqrt).then_inc(rooted, 1)
                        act.wait_ge(v_ready, u * QTILES + t + 1)
                        if t == 0:
                            act.wait_ge(att_ready, u * QTILES)
                        nc.scalar.activation(v_tok[0:nk, t, :], banks[0:nk, 4 + t % 2, :], ACT.Copy).then_inc(v_kept, 1)
                        if 1 <= t <= TTILES:
                            keep_turned(u, t - 1)
                    for t in range(QTILES + 1):
                        if t < QTILES:
                            _, nq, _, nk = q_tile(t)
                            w = t % 2
                            act.wait_ge(bias_ready, u * QTILES + t + 1)
                            if t >= 2:
                                act.wait_ge(p_normed, u * QTILES + t - 1)
                            if t == 0:
                                act.wait_ge(p_normed, u * QTILES)
                            for h in range(GROUP):
                                last = nc.scalar.activation(probs[0:nq, w, h, 0:nk], banks[0:nq, 4 + h // 4, (h % 4) * P:(h % 4) * P + nk],
                                                            ACT.Exp, bias=neg_bias[0:nq, w, h:h + 1], scale=QK_SCALE,
                                                            accum_out=row_sum[0:nq, w, h:h + 1])
                            last.then_inc(exp_done, 1)
                        if t >= 1:
                            keep_values(u, t - 1)
                for c in range(CHUNKS):
                    act.wait_ge(f_centred, l * CHUNKS + c + 1)
                    nc.scalar.activation(spread[:, c, :], centre[:, c, :], ACT.Square).then_inc(f_squared, 1)
                for c in range(CHUNKS):
                    act.wait_ge(f_eps, l * CHUNKS + c + 1)
                    nc.scalar.activation(spread[:, c, :], spread[:, c, :], ACT.Sqrt).then_inc(f_root, 1)
                for c in range(CHUNKS):
                    for n, (f0, fn) in enumerate(FF_PARTS):
                        k = c * NF + n
                        act.wait_ge(f_gate, l * (CHUNKS * NF) + k + 1)
                        if k >= 2:
                            act.wait_ge(f_hid, l * (CHUNKS * NF) + k - 1)
                        nc.scalar.activation(gate[0:fn, k % 2, :], banks[0:fn, k % 2, :], ACT.Gelu, bias=b1_s[0:fn, 1, n:n + 1])\
                            .then_inc(f_gelu, 1)

        @block.gpsimd
        def _(pool):
            nc.gpsimd.memset(q_t[:], 0.0).then_inc(zeroed, 1)
            pool.wait_ge(zeroed, 1)
            nc.gpsimd.memset(shifted[HD:P, :, 0:1], 0.0).then_inc(zeroed, 1)
            pool.wait_ge(zeroed, 2)
            pool.wait_ge(consts, 32)
            with pool.Fori(0, DEPTH) as l:
                pool.wait_ge(scale_in, l * 32 + 32)
                pool.wait_ge(cos_ready, l * (UNITS * TTILES))
                pool.wait_ge(p_normed, l * (UNITS * QTILES))
                for m in range(2):
                    def scales(lo):
                        return scale_bc[:, m, lo:lo + HALF].unsqueeze(1).broadcast_to([P, TTILES, HALF])
                    nc.gpsimd.tensor_tensor(tab[:, m], rot[:, m], scale_bc[:, m, :].unsqueeze(1).broadcast_to([P, TTILES, HD]), ALU.mult)\
                        .then_inc(tab_ready, 1)
                    nc.gpsimd.tensor_tensor(tab[:, 2 + m, :, 0:HALF], rot[:, 2 + m, :, 0:HALF], scales(HALF), ALU.mult).then_inc(tab_ready, 1)
                    nc.gpsimd.tensor_tensor(tab[:, 2 + m, :, HALF:HD], rot[:, 2 + m, :, HALF:HD], scales(0), ALU.mult).then_inc(tab_ready, 1)
                with pool.Fori(0, UNITS) as v:
                    u = l * UNITS + v
                    for t in range(TTILES):
                        if t == 0:
                            pool.wait_ge(tab_ready, l * 6 + 6)
                            pool.wait_ge(p_normed, u * QTILES)
                        pool.wait_ge(unit_ready, u * TTILES + t + 1)
                        pool.wait_ge(turn_ready, u * TTILES + t)
                        un = unit[:].rearrange("p (m h) d -> p m h d", m=2)
                        for m in range(2):
                            for lo, hi in ((0, HALF), (HALF, 0)):
                                nc.gpsimd.tensor_tensor(with_sin[:, m, :, lo:lo + HALF], un[:, m, :, hi:hi + HALF],
                                                        tab[:, 2 + m, t, lo:lo + HALF].unsqueeze(1).broadcast_to([P, GROUP, HALF]),
                                                        ALU.mult).then_inc(sin_ready, 1)
                    for t in range(QTILES):
                        _, nq, _, nk = q_tile(t)
                        w = t % 2
                        pool.wait_ge(inverted, u * QTILES + t + 1)
                        pool.wait_ge(p_normed, u * QTILES + t)
                        if t == 0:
                            pool.wait_ge(sin_ready, (u + 1) * (4 * TTILES))
                        if t >= 2:
                            pool.wait_ge(p_turned, u * QTILES + t - 1)
                        if t == 0:
                            pool.wait_ge(p_turned, u * QTILES)
                        nc.gpsimd.tensor_tensor(normed[0:nq, w, :, 0:nk], probs[0:nq, w, :, 0:nk],
                                                inv_sum[0:nq, w, :].unsqueeze(2).broadcast_to([nq, GROUP, nk]), ALU.mult).then_inc(p_normed, 1)

        @block.vector
        def _(dve):
            dve.wait_ge(consts, 32)
            nc.vector.tensor_copy(band_b[:], band_f[:]).then_inc(band_ready, 1)
            nc.vector.tensor_copy(flat, resid[:]).then_inc(begun, 1)
            dve.wait_ge(begun, 1)

            def shift(done):
                nc.vector.tensor_copy(shifted[0:HD], stream[0:HD]).then_inc(done, 1)
                nc.vector.tensor_copy(shifted[HD:P, :, 1:S], stream[HD:P, :, 0:S - 1]).then_inc(done, 1)

            def add_tile(u, b, t):
                q0, nq, _, _ = q_tile(t)
                dve.wait_ge(out_ready, u * QTILES + t + 1)
                nc.vector.tensor_tensor(flat[:, bass.ds(b * S + q0, nq)], banks[:, 2 + t % 2, 0:nq],
                                        flat[:, bass.ds(b * S + q0, nq)], ALU.add).then_inc(added, 1)

            def turn_add(u, t):
                dve.wait_ge(sin_ready, u * (4 * TTILES) + 4 * t + 4)
                dve.wait_ge(cos_ready, u * TTILES + t + 1)
                dve.wait_ge(qkt_ready, u * TTILES + t)
                nc.vector.tensor_tensor(turned[:], with_cos[:], with_sin[:], ALU.add).then_inc(turn_ready, 1)

            with dve.Fori(0, DEPTH) as l:
                dve.wait_ge(f_added, l * CHUNKS)
                shift(shift_a)
                with dve.Fori(0, GROUPS) as g:
                    with dve.Fori(0, B) as b:
                        u = (l * GROUPS + g) * B + b
                        dve.wait_ge(v_ready, u * QTILES)
                        dve.wait_ge(shift_a, l * 2 + 2)
                        dve.wait_ge(zeroed, 2)
                        nc.vector.tensor_scalar(xs[:], flat_shifted[:, bass.ds(b * S, S)], 1.0, None, ALU.mult).then_inc(xs_ready, 1)
                        for t in range(TTILES + 1):
                            if t < TTILES:
                                dve.wait_ge(squared, u * TTILES + t + 1)
                                nc.vector.tensor_reduce(sum_sq[:], square[:, t % 2], AX.X, ALU.add).then_inc(summed, 1)
                            if t >= 1:
                                turn_add(u, t - 1)
                            if t < TTILES:
                                dve.wait_ge(rooted, u * TTILES + t + 1)
                                nc.vector.tensor_scalar(clipped[:], norm[:], 1e-12, None, ALU.max).then_inc(clip_done, 1)
                                dve.wait_ge(clip_done, u * TTILES + t + 1)
                                nc.vector.reciprocal(inv_norm[:], clipped[:]).then_inc(norm_inv, 1)
                                dve.wait_ge(norm_inv, u * TTILES + t + 1)
                                nc.vector.tensor_tensor(unit[:], qk_banks(t).rearrange("p m (h d) -> p (m h) d", h=GROUP),
                                                        inv_norm[:].unsqueeze(2).broadcast_to([P, 2 * GROUP, HD]), ALU.mult)\
                                    .then_inc(unit_ready, 1)
                                dve.wait_ge(unit_ready, u * TTILES + t + 1)
                                dve.wait_ge(turn_ready, u * TTILES + t)
                                if t == 0:
                                    dve.wait_ge(tab_ready, l * 6 + 6)
                                un = unit[:].rearrange("p (m h) d -> p m h d", m=2)
                                nc.vector.tensor_tensor(with_cos[:], un, tab[:, 0:2, t, :].unsqueeze(2).broadcast_to([P, 2, GROUP, HD]),
                                                        ALU.mult).then_inc(cos_ready, 1)
                        for t in range(QTILES + 2):
                            if 1 <= t <= QTILES:
                                _, nq, _, _ = q_tile(t - 1)
                                w = (t - 1) % 2
                                dve.wait_ge(exp_done, u * QTILES + t)
                                dve.wait_ge(p_normed, u * QTILES + max(0, t - 2))
                                nc.vector.reciprocal(inv_sum[0:nq, w, :], row_sum[0:nq, w, :]).then_inc(inverted, 1)
                            if t < QTILES:
                                _, nq, _, nk = q_tile(t)
                                dve.wait_ge(score_ready, u * QTILES + t + 1)
                                dve.wait_ge(bias_ready, u * QTILES + t)
                                nc.vector.tensor_reduce(neg_max[0:nq, :],
                                                        banks[0:nq, 4:6, :].rearrange("p a (h k) -> p (a h) k", h=4)[:, :, 0:nk],
                                                        AX.X, ALU.max, negate=True).then_inc(maxed, 1)
                                dve.wait_ge(maxed, u * QTILES + t + 1)
                                nc.vector.tensor_scalar(neg_bias[0:nq, t % 2, :], neg_max[0:nq, :], QK_SCALE, None, ALU.mult)\
                                    .then_inc(bias_ready, 1)
                            if 1 <= t <= QTILES:
                                _, nq, _, nk = q_tile(t - 1)
                                dve.wait_ge(p_turned, u * QTILES + t)
                                dve.wait_ge(att_ready, u * QTILES + max(0, t - 2))
                                nc.vector.tensor_copy(probs_t[0:nk, (t - 1) % 2, :, 0:nq],
                                                      banks[0:nk, 6:8, :].rearrange("p a (h q) -> p (a h) q", h=4)[:, :, 0:nq])\
                                    .then_inc(pt_kept, 1)
                            if t >= 2:
                                add_tile(u, b, t - 2)
                dve.wait_ge(added, (l + 1) * (UNITS * QTILES))
                shift(shift_f)
                for c in range(CHUNKS):
                    cols = slice(c * CHUNK, (c + 1) * CHUNK)
                    dve.wait_ge(f_mean, l * CHUNKS + c + 1)
                    dve.wait_ge(shift_f, l * 2 + 2)
                    nc.vector.tensor_tensor(centre[:, c, :], flat_shifted[:, cols], banks[:, c, :], ALU.subtract).then_inc(f_centred, 1)
                for c in range(CHUNKS):
                    dve.wait_ge(f_var, l * CHUNKS + c + 1)
                    nc.vector.tensor_scalar(spread[:, c, :], banks[:, 4 + c, :], EPS, None, ALU.add).then_inc(f_eps, 1)
                for c in range(CHUNKS):
                    dve.wait_ge(f_root, l * CHUNKS + c + 1)
                    nc.vector.reciprocal(spread[:, c, :], spread[:, c, :]).then_inc(f_inverted, 1)
                    dve.wait_ge(f_inverted, l * CHUNKS + c + 1)
                    nc.vector.tensor_tensor(centre[:, c, :], centre[:, c, :], spread[:, c, :], ALU.mult).then_inc(f_normed, 1)
                    dve.wait_ge(f_normed, l * CHUNKS + c + 1)
                    if c == 0:
                        dve.wait_ge(wf_in, l * FF_LOADS + FF_LOADS)
                    nc.vector.tensor_scalar(centre[:, c, :], centre[:, c, :], ln_s[:, 0:1], ln_s[:, 1:2], ALU.mult, ALU.add)\
                        .then_inc(f_affine, 1)
                for c in range(CHUNKS):
                    cols = slice(c * CHUNK, (c + 1) * CHUNK)
                    for n, (f0, fn) in enumerate(FF_PARTS):
                        k = c * NF + n
                        dve.wait_ge(f_gelu, l * (CHUNKS * NF) + k + 1)
                        dve.wait_ge(f_a, l * (CHUNKS * NF) + k + 1)
                        if n == 0:
                            dve.wait_ge(f_out, l * CHUNKS + c)
                        nc.vector.scalar_tensor_tensor(out=hidden[0:fn, n, :], in0=banks[0:fn, 2 + k % 2, :], scalar=b1_s[0:fn, 0, n:n + 1],
                                                       in1=gate[0:fn, k % 2, :], op0=ALU.add, op1=ALU.mult).then_inc(f_hid, 1)
                    dve.wait_ge(f_out, l * CHUNKS + c + 1)
                    nc.vector.scalar_tensor_tensor(out=flat[:, cols], in0=banks[:, 4 + c % 2, :], scalar=b2_s[:], in1=flat[:, cols],
                                                   op0=ALU.add, op1=ALU.add).then_inc(f_added, 1)
            dve.wait_ge(f_added, DEPTH * CHUNKS)
            nc.vector.tensor_tensor(resid[:], resid[:], flat, ALU.add).then_inc(final, 1)
            dve.wait_ge(final, 1)


def retention_stage(nc, keep, w_q, w_k, w_v, w_gate, w_out, gn_w, gn_b, tables, masks, causal_c):
    resid, ident = keep["resid"], keep["ident"]
    N = B * R_CHUNKS
    with ExitStack() as stack:
        core = Core(nc, stack)
        sb, sem = core.sb, core.sem
        w_bd = sb("r_w_bd", [P, 5, D])
        w_g = sb("r_w_g", [P, D])
        w_o = sb("r_w_o", [P, D])
        gn = sb("r_gn", [P, 2, D])
        tab = sb("r_tab", [P, 4, S])
        mask = sb("r_mask", [P, R_HEADS + D + 1])
        causal = sb("r_causal", [P, P])
        plain = sb("r_plain", [P, 2, CHUNK])
        crossed = sb("r_crossed", [P, 2, CHUNK])
        q_all = sb("r_q_all", [P, T])
        k_all = sb("r_k_all", [P, T])
        x_c = sb("r_x_c", [P, P])
        q_c = sb("r_q_c", [P, P])
        k_c = sb("r_k_c", [P, P])
        q_heads = sb("r_q_heads", [P, R_HEADS, P])
        kv = sb("r_kv", [P, 2, D])
        masked = sb("r_masked", [P, R_HEADS, P])
        update = sb("r_update", [P, D])
        summed = sb("r_summed", [P, D])
        state = sb("r_state", [P, D])
        y_all = sb("r_y_all", [P, N, D])
        g_all = sb("r_g_all", [P, N, D])
        work = sb("r_work", [P, N, D])
        stat = sb("r_stat", [P, 2, N * R_HEADS])
        z_t = sb("r_z_t", [P, T])
        banks = core.psum("r_banks", [P, 8, CHUNK])
        names = """loaded zeroed swapped proj_ready plain_ready crossed_ready qk_all x_ready q_ready k_ready heads_ready
            rows_ready kv_kept g_kept raw_ready masked_ready y_ready y_kept delta_ready updated summed_ready state_ready
            stat_done act_done turned turn_kept out_ready added"""
        (loaded, zeroed, swapped, proj_ready, plain_ready, crossed_ready, qk_all, x_ready, q_ready, k_ready, heads_ready,
         rows_ready, kv_kept, g_kept, raw_ready, masked_ready, y_ready, y_kept, delta_ready, updated, summed_ready, state_ready,
         stat_done, act_done, turned, turn_kept, out_ready, added) = (sem("r_" + n) for n in names.split())
        LOADS = (3 * R_HEADS + 7) * 16
        block = stack.enter_context(nc.Block())

        @block.sync
        def _(sp):
            sp.wait_ge(zeroed, 1)
            for m, w in enumerate((w_q, w_k, w_v)):
                for h in range(R_HEADS):
                    rows = slice(h * R_HD, (h + 1) * R_HD)
                    sp.dma_start(w_bd[rows, m, rows], w[h]).then_inc(loaded, 16)
            sp.dma_start(w_g[:], w_gate).then_inc(loaded, 16)
            sp.dma_start(w_o[:], w_out).then_inc(loaded, 16)
            sp.dma_start(gn[:, 0], gn_w.unsqueeze(0).broadcast_to([P, D])).then_inc(loaded, 16)
            sp.dma_start(gn[:, 1], gn_b.unsqueeze(0).broadcast_to([P, D])).then_inc(loaded, 16)
            sp.dma_start(tab[:], tables).then_inc(loaded, 16)
            sp.dma_start(mask[:], masks).then_inc(loaded, 16)
            sp.dma_start(causal[:], causal_c).then_inc(loaded, 16)
            sp.wait_ge(loaded, LOADS)

        @block.tensor
        def _(pe):
            pe.wait_ge(loaded, LOADS)
            pe.wait_ge(swapped, 4)
            for n in range(2 * CHUNKS):
                c, m = n // 2, n % 2
                if n >= 2:
                    pe.wait_ge(crossed_ready, n - 1)
                for swap in range(2):
                    last = nc.tensor.matmul(banks[:, 2 * (n % 2) + swap, :], w_bd[:, m + 3 * swap, :],
                                            resid[:, c * CHUNK:(c + 1) * CHUNK], start=True, stop=True)
                last.then_inc(proj_ready, 1)
            pe.wait_ge(crossed_ready, 2 * CHUNKS)
            with pe.Fori(0, N) as i:
                pe.wait_ge(k_ready, i + 1)
                pe.wait_ge(kv_kept, i)
                pe.wait_ge(g_kept, i)
                nc.tensor.transpose(banks[:, 0, 0:P], k_c[:], ident[:])
                nc.tensor.matmul(banks[:, 0, P:2 * P], x_c[:], w_bd[:, 2, :], start=True, stop=True)
                nc.tensor.matmul(banks[:, 0, 2 * P:3 * P], x_c[:], w_g[:], start=True, stop=True).then_inc(rows_ready, 1)
                pe.wait_ge(heads_ready, i + 1)
                pe.wait_ge(masked_ready, i)
                for half in range(2):
                    last = nc.tensor.matmul(banks[:, 1 + half, :], k_c[:], q_heads[:, 4 * half:4 * half + 4, :], start=True, stop=True)
                last.then_inc(raw_ready, 1)
                pe.wait_ge(kv_kept, i + 1)
                pe.wait_ge(updated, i)
                nc.tensor.matmul(banks[:, 4, 0:D], kv[:, 0, :], kv[:, 1, :], start=True, stop=True).then_inc(delta_ready, 1)
                pe.wait_ge(y_kept, i)
                pe.wait_ge(masked_ready, i + 1)
                pe.wait_ge(state_ready, i + 1)
                nc.tensor.matmul(banks[:, 3, 0:D], q_c[:], state[:], start=True, stop=False, skip_group_check=True)
                for h in range(R_HEADS):
                    cols = slice(h * R_HD, (h + 1) * R_HD)
                    last = nc.tensor.matmul(banks[:, 3, cols], masked[:, h, :], kv[:, 1, cols], start=False, stop=(h == R_HEADS - 1),
                                            skip_group_check=True)
                last.then_inc(y_ready, 1)
            pe.wait_ge(stat_done, 9)
            for c in range(CHUNKS):
                for n in range(4):
                    last = nc.tensor.transpose(banks[:, 5 + c % 2, n * P:(n + 1) * P], work[:, 4 * c + n, :], ident[:])
                last.then_inc(turned, 1)
                pe.wait_ge(turn_kept, c + 1)
                if c >= 1:
                    pe.wait_ge(added, c)
                nc.tensor.matmul(banks[:, 7, :], w_o[:], z_t[:, c * CHUNK:(c + 1) * CHUNK], start=True, stop=True).then_inc(out_ready, 1)

        @block.scalar
        def _(act):
            with act.Fori(0, N) as i:
                act.wait_ge(rows_ready, i + 1)
                act.wait_ge(y_ready, i)
                nc.scalar.activation(kv[:].rearrange("p m n -> p (m n)"), banks[:, 0, 0:2 * P], ACT.Copy).then_inc(kv_kept, 1)
            act.wait_ge(stat_done, 3)
            nc.scalar.activation(work[:], y_all[:], ACT.Square).then_inc(act_done, 1)
            act.wait_ge(stat_done, 5)
            nc.scalar.activation(stat[:, 1, :], stat[:, 1, :], ACT.Sqrt).then_inc(act_done, 1)
            nc.scalar.activation(g_all[:], g_all[:], ACT.Silu).then_inc(act_done, 1)
            for c in range(CHUNKS):
                act.wait_ge(turned, c + 1)
                nc.scalar.activation(z_t[:, c * CHUNK:(c + 1) * CHUNK], banks[:, 5 + c % 2, :], ACT.Copy).then_inc(turn_kept, 1)

        @block.gpsimd
        def _(pool):
            nc.gpsimd.memset(w_bd[:], 0.0).then_inc(zeroed, 1)
            pool.wait_ge(loaded, LOADS)
            with pool.Fori(0, N) as i:
                pool.wait_ge(q_ready, i + 1)
                pool.wait_ge(raw_ready, i)
                nc.gpsimd.tensor_tensor(q_heads[:], q_c[:].unsqueeze(1).broadcast_to([P, R_HEADS, P]),
                                        mask[:, 0:R_HEADS].unsqueeze(2).broadcast_to([P, R_HEADS, P]), ALU.mult).then_inc(heads_ready, 1)

        @block.vector
        def _(dve):
            dve.wait_ge(loaded, LOADS)
            for m in range(2):
                src = w_bd[:, m, :].rearrange("p (n two) -> p n two", two=2)
                dst = w_bd[:, 3 + m, :].rearrange("p (n two) -> p n two", two=2)
                nc.vector.tensor_copy(dst[:, :, 0:1], src[:, :, 1:2]).then_inc(swapped, 1)
                nc.vector.tensor_copy(dst[:, :, 1:2], src[:, :, 0:1]).then_inc(swapped, 1)
            for n in range(2 * CHUNKS):
                c, m = n // 2, n % 2
                cols = slice(c * CHUNK, (c + 1) * CHUNK)
                pos = slice(c * CHUNK % S, c * CHUNK % S + CHUNK)
                w = n % 2
                dve.wait_ge(proj_ready, n + 1)
                if n >= 2:
                    dve.wait_ge(qk_all, n - 1)
                nc.vector.tensor_tensor(plain[:, w, :], banks[:, 2 * w, :], tab[:, m, pos], ALU.mult).then_inc(plain_ready, 1)
                nc.vector.tensor_tensor(crossed[:, w, :], banks[:, 2 * w + 1, :], tab[:, 2 + m, pos], ALU.mult).then_inc(crossed_ready, 1)
                dve.wait_ge(plain_ready, n + 1)
                dve.wait_ge(crossed_ready, n + 1)
                nc.vector.tensor_tensor((q_all if m == 0 else k_all)[:, cols], plain[:, w, :], crossed[:, w, :], ALU.add).then_inc(qk_all, 1)
            dve.wait_ge(qk_all, 2 * CHUNKS)
            with dve.Fori(0, B) as b:
                dve.wait_ge(y_ready, b * R_CHUNKS)
                dve.wait_ge(summed_ready, b * (R_CHUNKS + 1))
                nc.vector.memset(summed[:], 0.0).then_inc(summed_ready, 1)
                with dve.Fori(0, R_CHUNKS) as n:
                    i = b * R_CHUNKS + n
                    dve.wait_ge(y_ready, i)
                    nc.vector.tensor_scalar(q_c[:], q_all[:, bass.ds(i * P, P)], 1.0, None, ALU.mult).then_inc(q_ready, 1)
                    nc.vector.tensor_scalar(x_c[:], resid[:, bass.ds(i * P, P)], 1.0, None, ALU.mult).then_inc(x_ready, 1)
                    nc.vector.tensor_scalar(k_c[:], k_all[:, bass.ds(i * P, P)], 1.0, None, ALU.mult).then_inc(k_ready, 1)
                    dve.wait_ge(summed_ready, i + b + 1)
                    nc.vector.tensor_scalar(state[:], summed[:], mask[:, R_HEADS + D:R_HEADS + D + 1], None, ALU.mult).then_inc(state_ready, 1)
                    dve.wait_ge(rows_ready, i + 1)
                    dve.wait_ge(kv_kept, i + 1)
                    nc.vector.tensor_scalar(g_all[:, bass.ds(i, 1), :].rearrange("p a n -> p (a n)"), banks[:, 0, 2 * P:3 * P], 1.0, None,
                                            ALU.mult).then_inc(g_kept, 1)
                    dve.wait_ge(raw_ready, i + 1)
                    nc.vector.tensor_tensor(masked[:], banks[:, 1:3, :].rearrange("p a (h s) -> p (a h) s", h=4),
                                            causal[:].unsqueeze(1).broadcast_to([P, R_HEADS, P]), ALU.mult).then_inc(masked_ready, 1)
                    dve.wait_ge(delta_ready, i + 1)
                    nc.vector.tensor_tensor(update[:], banks[:, 4, 0:D], mask[:, R_HEADS:R_HEADS + D], ALU.mult).then_inc(updated, 1)
                    dve.wait_ge(updated, i + 1)
                    dve.wait_ge(state_ready, i + 1)
                    nc.vector.tensor_tensor(summed[:], state[:], update[:], ALU.add).then_inc(summed_ready, 1)
                    dve.wait_ge(y_ready, i + 1)
                    nc.vector.tensor_scalar(y_all[:, bass.ds(i, 1), :].rearrange("p a n -> p (a n)"), banks[:, 3, 0:D], 1.0, None,
                                            ALU.mult).then_inc(y_kept, 1)
            heads = "p n (h d) -> p (n h) d"
            y_h = y_all[:].rearrange(heads, d=R_HD)
            w_h = work[:].rearrange(heads, d=R_HD)
            chain = [0]

            def done(ins):
                chain[0] += 1
                ins.then_inc(stat_done, 1)
                dve.wait_ge(stat_done, chain[0])

            def spread(col):
                return stat[:, col, :].unsqueeze(2).broadcast_to([P, N * R_HEADS, R_HD])

            dve.wait_ge(y_kept, N)
            done(nc.vector.tensor_reduce(stat[:, 0, :], y_h, AX.X, ALU.add))
            done(nc.vector.tensor_scalar(stat[:, 0, :], stat[:, 0, :], 1.0 / R_HD, None, ALU.mult))
            done(nc.vector.tensor_tensor(y_h, y_h, spread(0), ALU.subtract))
            dve.wait_ge(act_done, 1)
            done(nc.vector.tensor_reduce(stat[:, 1, :], w_h, AX.X, ALU.add))
            done(nc.vector.tensor_scalar(stat[:, 1, :], stat[:, 1, :], 1.0 / R_HD, EPS, ALU.mult, ALU.add))
            dve.wait_ge(act_done, 2)
            done(nc.vector.reciprocal(stat[:, 0, :], stat[:, 1, :]))
            done(nc.vector.tensor_tensor(w_h, y_h, spread(0), ALU.mult))
            nc.vector.tensor_tensor(work[:], work[:], gn[:, 0, :].unsqueeze(1).broadcast_to([P, N, D]), ALU.mult).then_inc(updated, 1)
            dve.wait_ge(updated, N + 1)
            done(nc.vector.tensor_tensor(work[:], work[:], gn[:, 1, :].unsqueeze(1).broadcast_to([P, N, D]), ALU.add))
            dve.wait_ge(act_done, 3)
            done(nc.vector.tensor_tensor(work[:], work[:], g_all[:], ALU.mult))
            for c in range(CHUNKS):
                cols = slice(c * CHUNK, (c + 1) * CHUNK)
                dve.wait_ge(out_ready, c + 1)
                nc.vector.tensor_tensor(resid[:, cols], resid[:, cols], banks[:, 7, :], ALU.add).then_inc(added, 1)
            dve.wait_ge(added, CHUNKS)


def expert_stage(nc, keep, xn, router_t, w12_t, w3_t, out, consts):
    resid, ident = keep["resid"], keep["ident"]
    E, N = EXPERTS, E_TILES
    with ExitStack() as stack:
        core = Core(nc, stack)
        sb, sem = core.sb, core.sem
        rw = sb("e_rw", [P, E])
        cst = sb("e_cst", [P, P + E])
        ones = sb("e_ones", [P, P])
        logit = sb("e_logit", [P, N, E])
        second = sb("e_second", [P, N, E])
        best = sb("e_best", [P, 4, N])
        hit = sb("e_hit", [P, 2, N, E])
        chosen = sb("e_chosen", [P, N, E])
        before = sb("e_before", [P, N, E])
        place = sb("e_place", [P, N, E])
        prob = sb("e_prob", [P, 4, N])
        weight = sb("e_weight", [P, E, N])
        w12 = sb("e_w12", [P, 2, 2 * D_FF])
        w3 = sb("e_w3", [P, 2, F_PARTS, D])
        silu = sb("e_silu", [P, 2, CHUNK])
        hidden = sb("e_hidden", [P, 2, F_PARTS, CHUNK])
        scaled = sb("e_scaled", [P, 2, CHUNK])
        total = sb("e_total", [P, N, D])
        pre = sb("e_pre", [P, N, D])
        stat = sb("e_stat", [P, 2, N])
        banks = core.psum("e_banks", [P, 8, CHUNK])
        names = """loaded zeroed logit_ready step prefix_ready exp_done gate_ready silu_done hid_ready y_ready scaled_ready
            total_ready x_ready act_done stored weight_ready"""
        (loaded, zeroed, logit_ready, step, prefix_ready, exp_done, gate_ready, silu_done, hid_ready, y_ready, scaled_ready,
         total_ready, x_ready, act_done, stored, weight_ready) = (sem("e_" + n) for n in names.split())
        w_in = [sem("e_w_even_in"), sem("e_w_odd_in")]
        PER = CHUNKS * F_PARTS
        block = stack.enter_context(nc.Block())

        def combine(pe, i, m):
            par = m // CHUNKS
            pe.wait_ge(hid_ready, i * (2 * PER) + (m + 1) * F_PARTS)
            if m >= 2:
                pe.wait_ge(scaled_ready, i * (2 * CHUNKS) + m - 1)
            elif m == 0:
                pe.wait_ge(scaled_ready, i * (2 * CHUNKS))
            for t in range(4):
                for f in range(F_PARTS):
                    last = nc.tensor.matmul(banks[:, 4 + m % 2, t * P:(t + 1) * P], hidden[:, m % 2, f, t * P:(t + 1) * P],
                                            w3[:, par, f, :], start=(f == 0), stop=(f == F_PARTS - 1))
            last.then_inc(y_ready, 1)

        def weigh(dve, i, m):
            par, c = m // CHUNKS, m % CHUNKS
            dve.wait_ge(y_ready, i * (2 * CHUNKS) + m + 1)
            if m >= 2:
                dve.wait_ge(total_ready, i * (2 * CHUNKS) + m - 1)
            else:
                dve.wait_ge(total_ready, i * (2 * CHUNKS))
            wcol = weight[:, bass.ds(i * 2 + par, 1), 4 * c:4 * c + 4].rearrange("p a n -> p (a n)")
            nc.vector.tensor_tensor(scaled[:, m % 2, :].rearrange("p (n d) -> p n d", d=D),
                                    banks[:, 4 + m % 2, :].rearrange("p (n d) -> p n d", d=D),
                                    wcol.unsqueeze(2).broadcast_to([P, 4, D]), ALU.mult).then_inc(scaled_ready, 1)

        @block.sync
        def _(sp):
            sp.dma_start(rw[:], router_t).then_inc(loaded, 16)
            sp.dma_start(cst[:], consts).then_inc(loaded, 16)

            def load_expert(e, par):
                sp.dma_start(w12[:, par, :], w12_t[bass.ds(e, 1), :, :].rearrange("a p n -> p (a n)")).then_inc(w_in[par], 16)
                sp.dma_start(w3[:, par], w3_t[bass.ds(e, 1), :, :, :].rearrange("a p f n -> p (a f) n")).then_inc(w_in[par], 16)

            load_expert(0, 0)
            with sp.Fori(0, E // 2 - 1) as i:
                sp.wait_ge(y_ready, i * (2 * CHUNKS))
                sp.sem_inc(stored, 1)
                load_expert(i * 2 + 1, 1)
                sp.wait_ge(y_ready, i * (2 * CHUNKS) + CHUNKS)
                sp.sem_inc(stored, 1)
                load_expert(i * 2 + 2, 0)
            sp.wait_ge(y_ready, (E - 2) * CHUNKS)
            load_expert(E - 1, 1)
            sp.wait_ge(step, FINAL)
            sp.dma_start(out.rearrange("(n p) d -> p n d", p=P), pre[:]).then_inc(loaded, 16)
            sp.wait_ge(loaded, 48)

        @block.tensor
        def _(pe):
            pe.wait_ge(loaded, 32)
            for n in range(N):
                last = nc.tensor.matmul(banks[:, 6, n * E:(n + 1) * E], xn[:, n * P:(n + 1) * P], rw[:], start=True, stop=True)
            last.then_inc(logit_ready, 1)
            pe.wait_ge(zeroed, 2)
            pe.wait_ge(step, CHOSEN)
            flat = chosen[:].rearrange("p n e -> p (n e)")
            nc.tensor.matmul(banks[:, 6, P:2 * P], cst[:, 0:P], flat, start=True, stop=True)
            nc.tensor.matmul(banks[:, 6, 2 * P:3 * P], ones[:], flat, start=True, stop=True).then_inc(prefix_ready, 1)
            with pe.Fori(0, E // 2) as i:
                for par in range(2):
                    for c in range(CHUNKS):
                        for f in range(F_PARTS):
                            k = par * PER + c * F_PARTS + f
                            if par == 0 and c == 0 and f == 0:
                                pe.wait_ge(w_in[0], i * 32 + 32)
                                pe.wait_ge(hid_ready, i * (2 * PER))
                            elif c == 0 and f == 0:
                                pe.wait_ge(w_in[1], i * 32 + 32)
                            if k >= 2:
                                pe.wait_ge(hid_ready, i * (2 * PER) + k - 1)
                            b0 = 2 * (k % 2)
                            for side in range(2):
                                last = nc.tensor.matmul(banks[:, b0 + side, :], w12[:, par, side * D_FF + f * P:side * D_FF + (f + 1) * P],
                                                        xn[:, c * CHUNK:(c + 1) * CHUNK], start=True, stop=True)
                            last.then_inc(gate_ready, 1)
                        m = par * CHUNKS + c
                        if m >= 1:
                            combine(pe, i, m - 1)
                combine(pe, i, 2 * CHUNKS - 1)
            for n in range(N):
                if n % 4 == 0:
                    pe.wait_ge(scaled_ready, E * CHUNKS)
                last = nc.tensor.transpose(banks[:, n // 4, (n % 4) * P:(n % 4 + 1) * P], resid[:, n * P:(n + 1) * P], ident[:])
            last.then_inc(x_ready, 1)

        @block.scalar
        def _(act):
            act.wait_ge(step, TOPS)
            nc.scalar.activation(prob[:, 1, :], prob[:, 0, :], ACT.Exp).then_inc(exp_done, 1)
            with act.Fori(0, E // 2) as i:
                for k in range(2 * PER):
                    act.wait_ge(gate_ready, i * (2 * PER) + k + 1)
                    if k >= 2:
                        act.wait_ge(hid_ready, i * (2 * PER) + k - 1)
                    nc.scalar.activation(silu[:, k % 2, :], banks[:, 2 * (k % 2), :], ACT.Silu).then_inc(silu_done, 1)
            act.wait_ge(step, SQUARE)
            nc.scalar.activation(total[:], pre[:], ACT.Square).then_inc(act_done, 1)
            act.wait_ge(step, ROOT)
            nc.scalar.activation(stat[:, 1, :], stat[:, 1, :], ACT.Sqrt).then_inc(act_done, 1)

        @block.gpsimd
        def _(pool):
            nc.gpsimd.memset(ones[:], 1.0).then_inc(zeroed, 1)
            nc.gpsimd.memset(total[:], 0.0).then_inc(zeroed, 1)
            pool.wait_ge(zeroed, 2)
            with pool.Fori(0, E // 2) as i:
                for m in range(2 * CHUNKS):
                    c = m % CHUNKS
                    pool.wait_ge(scaled_ready, i * (2 * CHUNKS) + m + 1)
                    pool.wait_ge(total_ready, i * (2 * CHUNKS) + m)
                    acc = total[:, 4 * c:4 * c + 4, :].rearrange("p n d -> p (n d)")
                    nc.gpsimd.tensor_tensor(acc, acc, scaled[:, m % 2, :], ALU.add).then_inc(total_ready, 1)

        @block.vector
        def _(dve):
            count = [0]

            def done(ins):
                count[0] += 1
                ins.then_inc(step, 1)
                dve.wait_ge(step, count[0])

            def over_e(a):
                return a.unsqueeze(2).broadcast_to([P, N, E])

            rev = cst[:, P:P + E].unsqueeze(1).broadcast_to([P, N, E])
            dve.wait_ge(loaded, 32)
            dve.wait_ge(logit_ready, 1)
            done(nc.vector.tensor_scalar(logit[:].rearrange("p n e -> p (n e)"), banks[:, 6, 0:N * E], CLAMP, -CLAMP, ALU.min, ALU.max))
            for k, values in enumerate((logit, second)):
                done(nc.vector.tensor_reduce(best[:, k, :], values[:], AX.X, ALU.max))
                done(nc.vector.tensor_tensor(hit[:, k], values[:], over_e(best[:, k, :]), ALU.is_equal))
                done(nc.vector.tensor_tensor(hit[:, k], hit[:, k], rev, ALU.mult))
                done(nc.vector.tensor_reduce(best[:, 2 + k, :], hit[:, k], AX.X, ALU.max))
                done(nc.vector.tensor_tensor(hit[:, k], rev, over_e(best[:, 2 + k, :]), ALU.is_equal))
                if k == 0:
                    done(nc.vector.scalar_tensor_tensor(out=second[:], in0=hit[:, 0], scalar=-1e9, in1=logit[:], op0=ALU.mult, op1=ALU.add))
            done(nc.vector.tensor_tensor(chosen[:], hit[:, 0], hit[:, 1], ALU.add))
            assert count[0] == CHOSEN
            done(nc.vector.tensor_tensor(prob[:, 0, :], best[:, 1, :], best[:, 0, :], ALU.subtract))
            assert count[0] == TOPS
            dve.wait_ge(exp_done, 1)
            done(nc.vector.tensor_scalar(prob[:, 2, :], prob[:, 1, :], 1.0, 1e-12, ALU.add, ALU.add))
            done(nc.vector.reciprocal(prob[:, 0, :], prob[:, 2, :]))
            done(nc.vector.tensor_tensor(prob[:, 3, :], prob[:, 1, :], prob[:, 0, :], ALU.mult))
            done(nc.vector.tensor_tensor(hit[:, 0], hit[:, 0], over_e(prob[:, 0, :]), ALU.mult))
            done(nc.vector.tensor_tensor(hit[:, 1], hit[:, 1], over_e(prob[:, 3, :]), ALU.mult))
            done(nc.vector.tensor_tensor(hit[:, 0], hit[:, 0], hit[:, 1], ALU.add))
            dve.wait_ge(prefix_ready, 1)
            tile_total = banks[:, 6, 2 * P:3 * P].rearrange("p (n e) -> p n e", e=E)
            done(nc.vector.memset(before[:], 0.0))
            for n in range(1, N):
                done(nc.vector.tensor_tensor(before[:, n, :], tile_total[:, n - 1, :], before[:, n - 1, :], ALU.add))
            done(nc.vector.tensor_tensor(place[:], banks[:, 6, P:2 * P].rearrange("p (n e) -> p n e", e=E), before[:], ALU.add))
            done(nc.vector.tensor_scalar(place[:], place[:], float(CAP), None, ALU.is_lt))
            nc.vector.tensor_tensor(weight[:].rearrange("p e n -> p n e"), hit[:, 0], place[:], ALU.mult).then_inc(weight_ready, 1)
            dve.wait_ge(weight_ready, 1)
            with dve.Fori(0, E // 2) as i:
                for m in range(2 * CHUNKS):
                    par, c = m // CHUNKS, m % CHUNKS
                    for f in range(F_PARTS):
                        k = m * F_PARTS + f
                        dve.wait_ge(silu_done, i * (2 * PER) + k + 1)
                        if f == 0 and m >= 2:
                            dve.wait_ge(y_ready, i * (2 * CHUNKS) + m - 1)
                        if f == 0 and m == 0:
                            dve.wait_ge(y_ready, i * (2 * CHUNKS))
                        nc.vector.tensor_tensor(hidden[:, m % 2, f, :], banks[:, 2 * (k % 2) + 1, :], silu[:, k % 2, :], ALU.mult)\
                            .then_inc(hid_ready, 1)
                    if m >= 1:
                        weigh(dve, i, m - 1)
                weigh(dve, i, 2 * CHUNKS - 1)
            dve.wait_ge(x_ready, 1)
            dve.wait_ge(total_ready, E * CHUNKS)
            fl = "p n d -> p (n d)"
            done(nc.vector.tensor_tensor(pre[:].rearrange(fl), banks[:, 0:4, :].rearrange("p a n -> p (a n)"), total[:].rearrange(fl), ALU.add))
            over_d = lambda a: a.unsqueeze(2).broadcast_to([P, N, D])
            done(nc.vector.tensor_reduce(stat[:, 0, :], pre[:], AX.X, ALU.add))
            done(nc.vector.tensor_scalar(stat[:, 0, :], stat[:, 0, :], 1.0 / D, None, ALU.mult))
            done(nc.vector.tensor_tensor(pre[:], pre[:], over_d(stat[:, 0, :]), ALU.subtract))
            assert count[0] == SQUARE
            dve.wait_ge(act_done, 1)
            done(nc.vector.tensor_reduce(stat[:, 1, :], total[:], AX.X, ALU.add))
            done(nc.vector.tensor_scalar(stat[:, 1, :], stat[:, 1, :], 1.0 / D, EPS, ALU.mult, ALU.add))
            assert count[0] == ROOT
            dve.wait_ge(act_done, 2)
            done(nc.vector.reciprocal(stat[:, 0, :], stat[:, 1, :]))
            done(nc.vector.tensor_tensor(pre[:], pre[:], over_d(stat[:, 0, :]), ALU.mult))
            assert count[0] == FINAL



def program(nc, t, c, out):
    with ExitStack() as stack:
        core = Core(nc, stack)
        keep = {"resid": core.sb("resid", [P, T]), "ident": core.sb("ident", [P, P]), "identb": core.sb("identb", [P, P], BF16),
                "mean_w": core.sb("mean_w", [P, P]), "norm_sems": norm_semaphores(core)}
        load_constants(nc, keep, c)
        attention_stage(nc, keep, t["L0_attn_x"], t["L0_attn_Wqkv"], t["L0_attn_bqkv"], t["L0_attn_Wo"], t["L0_attn_bo"], c["c_sel"])
        norm_stage(nc, keep, 0)
        f = lambda n: t["L0_ffn_" + n]
        local_stage(nc, keep, f("Wqkv"), f("q_scale"), f("k_scale"), f("Wo"), f("ln_g"), f("ln_b"), f("W1"), f("b1"), f("W2"), f("b2"),
                    c["c_rotary"], c["c_band"])
        norm_stage(nc, keep, 1)
        r = lambda n: t["L1_attn_" + n]
        retention_stage(nc, keep, r("W_Q"), r("W_K"), r("W_V"), r("W_G"), r("W_O"), r("gn_weight"), r("gn_bias"),
                        c["c_decay"], c["c_masks"], c["c_causal"])
        norm_stage(nc, keep, 2)
        with ExitStack() as last:
            xn = Core(nc, last).sb("xn", [P, T])
            norm_stage(nc, keep, 3, out=xn, affine=(t["L1_ffn_ln_gamma"], t["L1_ffn_ln_beta"]))
            expert_stage(nc, keep, xn, t["L1_ffn_router_w"], t["L1_ffn_w12"], t["L1_ffn_w3"], out, c["c_expert"])


def _shape_constants():
    import numpy as np
    c = {"c_ident": np.eye(P)}
    sel = np.zeros((P, 18))
    for q in range(4):
        for h in range(2):
            for e in range(9):
                sel[32 * q + 16 * h + e, 9 * h + e] = 1
    c["c_sel"] = sel
    half = np.arange(0, HD, 2)
    pos = np.arange(S)
    freqs = np.concatenate([pos[:, None] * (1.0 / 10000.0 ** (half / HD))[None, :]] * 2, -1)
    scale = ((half + 0.4 * HD) / (1.4 * HD))[None, :] ** ((pos - S // 2) / (WIN // 2))[:, None]
    scale = np.concatenate([scale, scale], -1)
    sign = np.where(np.arange(HD) < HD // 2, -1.0, 1.0)
    rotary = np.stack([np.cos(freqs) * scale, np.cos(freqs) / scale, np.sin(freqs) * scale * sign, np.sin(freqs) / scale * sign])
    c["c_rotary"] = rotary.reshape(4, TTILES, P, HD).transpose(2, 0, 1, 3)
    i, j = np.arange(QTILE)[:, None], np.arange(P)[None]
    c["c_band"] = np.where((i <= j) & (j <= i + WIN), 0, -1e30)
    gamma = 1.0 - np.exp(np.linspace(np.log(1.0 / 32.0), np.log(1.0 / 512.0), R_HEADS))
    gamma = np.repeat(gamma, R_HD)[:, None]
    d = R_HD
    sc = np.repeat((np.arange(0, d, 2) + 0.4 * d) / (1.4 * d), 2)[:, None] ** (pos / 512.0)[None, :]
    ang = np.repeat(1.0 / 10000.0 ** (np.arange(d // 2) / (d // 2)), 2)[:, None] * pos[None, :]
    sc, ang = np.tile(sc, (R_HEADS, 1)), np.tile(ang, (R_HEADS, 1))
    dec = gamma ** (pos % P)[None, :]
    sg = np.where(np.arange(P) % 2 == 0, -1.0, 1.0)[:, None]
    c["c_decay"] = np.stack([np.cos(ang) * sc * dec, np.cos(ang) / sc / dec, np.sin(ang) * sc * dec * sg, np.sin(ang) / sc / dec * sg], 1)
    head = np.arange(P) // R_HD
    c["c_masks"] = np.concatenate([head[:, None] == np.arange(R_HEADS)[None], head[:, None] == head[None], gamma ** P], 1)
    c["c_causal"] = np.arange(P)[:, None] <= np.arange(P)[None]
    c["c_expert"] = np.concatenate([np.arange(P)[:, None] < np.arange(P)[None], np.tile(EXPERTS - np.arange(EXPERTS), (P, 1))], 1)
    return {k: np.ascontiguousarray(v, dtype=np.float32) for k, v in c.items()}


def _laid_out(inputs):
    import numpy as np
    a = {k: np.asarray(v) for k, v in inputs.items()}
    a["L0_attn_x"] = a["L0_attn_x"].reshape(T, D)
    a["L0_attn_Wqkv"] = a["L0_attn_Wqkv"].T
    a["L0_attn_Wo"] = a["L0_attn_Wo"].T.reshape(8, 2, A_HD, D).transpose(0, 2, 1, 3).reshape(64, 2, D)
    groups = HEADS // GROUP
    a["L0_ffn_Wqkv"] = a["L0_ffn_Wqkv"].reshape(DEPTH, D, 3, groups, GCOLS).transpose(0, 2, 3, 1, 4).reshape(DEPTH * 3 * groups, D, GCOLS)
    a["L0_ffn_Wo"] = a["L0_ffn_Wo"].reshape(DEPTH * groups, PAIRS, P, D).transpose(0, 2, 1, 3)
    a["L1_ffn_router_w"] = a["L1_ffn_router_w"].T
    a["L1_ffn_w12"] = a["L1_ffn_w12"].transpose(0, 2, 1)
    a["L1_ffn_w3"] = a["L1_ffn_w3"].transpose(0, 2, 1).reshape(EXPERTS, F_PARTS, P, D).transpose(0, 2, 1, 3)
    return {k: np.ascontiguousarray(v) for k, v in a.items()}


def kernel(**inputs):
    import concourse.bacc as bacc
    from concourse.bass_utils import run_bass_kernel_spmd

    nc = bacc.Bacc("TRN2", target_bir_lowering=False, num_devices=1)
    arrays, handles = {}, {}
    for name, a in {**_laid_out(inputs), **_shape_constants()}.items():
        arrays["in_" + name] = a
        handles[name] = nc.dram_tensor("in_" + name, a.shape, mybir.dt.from_np(a.dtype), kind="ExternalInput").ap()
    out = nc.dram_tensor("out_x", (T, D), F32, kind="ExternalOutput").ap()
    program(nc, handles, handles, out)
    result = run_bass_kernel_spmd(nc, [arrays], core_ids=[0])
    return result.results[0]["out_x"].reshape(B, S, D)
```

```python
from contextlib import ExitStack

import concourse.bass as bass
from concourse import mybir

F32 = mybir.dt.float32
BF16 = mybir.dt.bfloat16
ALU = mybir.AluOpType
ACT = mybir.ActivationFunctionType
AX = mybir.AxisListType

P = 128
B, S, D = 2, 1024, 128
T = B * S
EPS = 1e-5
CHUNK = 512
CHUNKS = T // CHUNK

START = 1

A_HEADS, A_HD = 16, 8
A_COLS = D // A_HD
A_TOK = S // A_HEADS
A_TILES = T // P
A_SCALE = A_HD ** -0.5

DEPTH, HEADS, HD, WIN = 6, 16, 64, 32
GROUP = 8
PAIRS = GROUP // 2
UNITS = B * HEADS // GROUP
GCOLS = GROUP * HD
QTILE = 96
QTILES = -(-S // QTILE)
TTILES = S // P
FF = int(D * 4 * 2 / 3)
FF_PARTS = [(0, 128), (128, 128), (256, FF - 256)]
QK_SCALE = 8.0

R_HEADS, R_HD = 8, 16
R_CHUNKS = S // P

EXPERTS, D_FF, TOPK = 8, 512, 2
CAP = max(1, -(-T * TOPK * 5 // (4 * EXPERTS)))
CLAMP = 10000.0
E_TILES = T // P
F_PARTS = D_FF // P
CHOSEN, TOPS = 13, 14
SQUARE = TOPS + 6 + E_TILES + 2 + 4
ROOT = SQUARE + 2
FINAL = ROOT + 2


def q_tile(t):
    q0 = t * QTILE
    nq = min(QTILE, S - q0)
    k0 = max(0, q0 - WIN)
    return q0, nq, k0, q0 + nq - k0


class Core:

    def __init__(self, nc, stack, prefix=""):
        self.nc, self.stack, self.prefix = nc, stack, prefix
        self.sems = []

    def sb(self, name, shape, dt=F32):
        return self.stack.enter_context(self.nc.sbuf_tensor(self.prefix + name, shape, dt))

    def psum(self, name, shape, dt=F32):
        return self.stack.enter_context(self.nc.psum_tensor(self.prefix + name, shape, dt))

    def sem(self, name):
        self.sems.append(self.stack.enter_context(self.nc.semaphore(self.prefix + name)))
        return self.sems[-1]


def start_counts(nc, core):
    def share(engine, n):
        for s in core.sems[n::5]:
            engine.sem_inc(s, START)

    with nc.Block() as block:
        @block.sync
        def _(sp):
            share(sp, 0)

        @block.tensor
        def _(pe):
            share(pe, 1)

        @block.scalar
        def _(act):
            share(act, 2)

        @block.gpsimd
        def _(pool):
            share(pool, 3)

        @block.vector
        def _(dve):
            share(dve, 4)


def load_constants(nc, keep, consts):
    with ExitStack() as stack:
        core = Core(nc, stack)
        loaded, cast = core.sem("const_loaded"), core.sem("const_cast")
        block = stack.enter_context(nc.Block())

        @block.sync
        def _(sp):
            sp.dma_start(keep["ident"][:], consts["c_ident"]).then_inc(loaded, 16)
            sp.wait_ge(loaded, 16)

        @block.vector
        def _(dve):
            dve.wait_ge(loaded, 16)
            nc.vector.tensor_copy(keep["identb"][:], keep["ident"][:]).then_inc(cast, 1)
            nc.vector.memset(keep["mean_w"][:], 1.0 / D).then_inc(cast, 1)
            nc.vector.memset(keep["eps"][:], EPS).then_inc(cast, 1)
            dve.wait_ge(cast, 3)


def attention_stage(nc, keep, x, w_in_t, b_in, w_out_t, b_out, sel):
    resid, ident, identb = keep["resid"], keep["ident"], keep["identb"]
    with ExitStack() as stack:
        core = Core(nc, stack, "a_")
        sb, psum, sem = core.sb, core.psum, core.sem
        KROWS = 96
        XROWS = KROWS + 2
        x_tok = sb("x_tok", [P, D])
        x_t = sb("x_t", [P, D])
        w_in = sb("w_in", [P, 3 * D])
        b_bc = sb("b_bc", [P, 3 * D])
        w_out = sb("w_out", [64, 2, D])
        b_col = sb("b_col", [P, 1])
        selm = sb("selm", [P, 18])
        qkv = sb("qkv", [P, A_COLS, 24])
        part = sb("part", [P, 3, A_COLS, 16], BF16)
        rest = sb("rest", [P, A_COLS, 16])
        q_arr = sb("q_arr", [P, A_COLS, KROWS], BF16)
        k_arr = sb("k_arr", [P, A_COLS, KROWS], BF16)
        v_two = sb("v_two", [P, 2, A_COLS, 32])
        q_st = sb("q_st", [P, 2, 2, A_COLS, A_TOK], BF16)
        k_st = sb("k_st", [P, 2, 2, A_COLS, A_TOK], BF16)
        neg_half = sb("neg_half", [P, 2 * 16])
        neg_max = sb("neg_max", [P, 2 * 8])
        max_part = sb("max_part", [P, 2 * 8, 2], BF16)
        probs = sb("probs", [P, 8, S])
        vals_t = sb("vals_t", [P, S])
        recip = sb("recip", [P, 8, 2])
        vals = sb("vals", [P, 2, 8, A_HD])
        feat = sb("feat", [64, 2, P])
        score = psum("score", [P, 3, CHUNK])
        acc = psum("acc", [P, 2, CHUNK])
        side = psum("side", [P, 3, CHUNK])

        loaded = sem("weights_loaded")
        x_in = sem("x_in")
        zeroed = sem("zeroed")
        xt_ready, xt_kept = sem("xt_ready"), sem("xt_kept")
        qkv_ready, qkv_kept = sem("qkv_ready"), sem("qkv_kept")
        split = sem("split")
        arranged, based, v_kept = sem("arranged"), sem("based"), sem("v_kept")
        stacked, stack_kept = sem("stacked"), sem("stack_kept")
        raw_ready, maxed = sem("raw_ready"), sem("maxed")
        max_split, max_rows, max_kept = sem("max_split"), sem("max_rows"), sem("max_kept")
        score_ready, exp_done, pv_done = sem("score_ready"), sem("exp_done"), sem("pv_done")
        acc_kept = sem("acc_kept")
        folded, inverted, normed = sem("folded"), sem("inverted"), sem("normed")
        turned, turn_kept = sem("turned"), sem("turn_kept")
        projected, added = sem("projected"), sem("added")
        start_counts(nc, core)
        block = stack.enter_context(nc.Block())
        STEPS = 2 * A_COLS
        VALUES_AT = (2, 4)
        BLOCKS = 2 * S // P
        HALVES = 2 * BLOCKS
        STACKS, ROWS = 8, 4

        def schedule(i, reader=False):
            plan = [[] for _ in range(STEPS)]
            if i < A_TILES - 2:
                for n, step in enumerate((19, 30)):
                    plan[step].append(("prepare", n))
                for n in range(6):
                    plan[30 + n // 3].append(("arrange", n))
            if i >= 1:
                for n, step in enumerate((11, 21, 30)):
                    plan[step].append(("finish", n))
            if i < A_TILES - 1:
                for n in range(STACKS):
                    plan[1 + n * 6 // STACKS + (2 if reader else 0)].append(("stack", n))
                for n in range(HALVES):
                    plan[9 + n * 18 // HALVES].append(("max", n))
                plan[26].append(("max_parts", 0))
                for n in range(ROWS):
                    plan[28 + n].append(("max_row", n))
            return plan

        def tiles(engine, tile):
            tile(0, 0, 0)
            tile(1, 1, 1)
            with engine.Fori(0, A_TILES // 2 - 2) as pair:
                for par in range(2):
                    tile(pair * 2 + (2 + par), par, 2)
            tile(A_TILES - 2, 0, A_TILES - 2)
            tile(A_TILES - 1, 1, A_TILES - 1)

        def first_stages(stages):
            prepare, arrange, stacks, maxima, parts, rows = stages
            for stage, i, n in FIRST:
                if stage == "prepare":
                    prepare(i, n)
                elif stage == "arrange":
                    arrange(i, n)
                elif stage == "stack":
                    stacks(0, 0, n)
                elif stage == "max":
                    maxima(0, 0, n)
                    if n == HALVES - 1:
                        parts(0)
                else:
                    rows(0, 0, n)

        def carry(plan, i, par, stages, finish):
            prepare, arrange, stacks, maxima, parts, rows = stages
            for stage, n in plan:
                if stage == "stack":
                    stacks(i + 1, 1 - par, n)
                elif stage == "max":
                    maxima(i + 1, 1 - par, n)
                elif stage == "max_parts":
                    parts(i + 1)
                elif stage == "max_row":
                    rows(i + 1, 1 - par, n)
                elif stage == "finish":
                    finish(i - 1, n)
                elif stage == "arrange":
                    arrange(i + 2, n)
                else:
                    prepare(i + 2, n)

        FIRST = ([("prepare", 0, n) for n in range(2)] + [("arrange", 0, n) for n in range(6)]
                 + [("stack", 0, n) for n in range(STACKS)] + [("max", 0, n) for n in range(HALVES)]
                 + [("prepare", 1, n) for n in range(2)] + [("arrange", 1, n) for n in range(6)] + [("max_row", 0, n) for n in range(ROWS)])

        @block.sync
        def _(sp):
            sp.dma_start(w_in[:], w_in_t).then_inc(loaded, 16)
            sp.dma_start(b_bc[:], b_in.unsqueeze(0).broadcast_to([P, 3 * D])).then_inc(loaded, 16)
            sp.dma_start(w_out[:], w_out_t).then_inc(loaded, 16)
            sp.dma_start(b_col[:], b_out.unsqueeze(1)).then_inc(loaded, 16)
            sp.dma_start(selm[:], sel).then_inc(loaded, 16)
            with sp.Fori(0, A_TILES) as i:
                sp.wait_ge(xt_ready, START + i)
                sp.dma_start(x_tok[:], x[bass.ts(i, P), :]).then_inc(x_in, 16)

        @block.tensor
        def _(pe):
            pe.wait_ge(loaded, START + 80)
            pe.wait_ge(zeroed, START + 8)

            def prepare(i, n):
                if n == 0:
                    pe.wait_ge(x_in, START + i * 16 + 16)
                    pe.wait_ge(qkv_kept, START + i)
                    nc.tensor.transpose(side[:, 2, 0:P], x_tok[:], ident[:]).then_inc(xt_ready, 1)
                elif n == 1:
                    pe.wait_ge(xt_kept, START + i + 1)
                    nc.tensor.matmul(side[:, 2, 0:3 * D], x_t[:], w_in[:], start=True, stop=True).then_inc(qkv_ready, 1)

            def stacks(i, par, n):
                arr = q_arr if n < 4 else k_arr
                pe.wait_ge(arranged, START + i * 6 + (3 if n < 4 else 6))
                if n < 2:
                    pe.wait_ge(max_kept, START + i * ROWS)
                else:
                    pe.wait_ge(stack_kept, START + i * STACKS + n - 1)
                for c in range(4):
                    last = nc.tensor.matmul(side[0:KROWS, n % 2, c * P:(c + 1) * P], arr[:, 4 * (n % 4) + c, :],
                                            identb[:], start=True, stop=True)
                last.then_inc(stacked, 1)

            def maxima(i, par, n):
                h, qb, j = n // BLOCKS, n // 2 % (BLOCKS // 2), n % 2
                pe.wait_ge(stack_kept, START + i * STACKS + STACKS)
                if n >= 2:
                    pe.wait_ge(maxed, START + i * HALVES + n - 1)
                nc.tensor.matmul(side[:, n % 2, :], q_st[0:KROWS, par, h, 2 * qb:2 * qb + 2, :],
                                 k_st[0:KROWS, par, h, 8 * j:8 * j + 8, :], start=True, stop=True).then_inc(raw_ready, 1)

            def nothing(*_):
                pass

            def rows(i, par, n):
                pe.wait_ge(max_split, START + i * 3 + 3)
                if n >= 2:
                    pe.wait_ge(max_kept, START + i * ROWS + n - 1)
                for m in range(4):
                    last = nc.tensor.matmul(side[KROWS:XROWS, n % 2, m * P:(m + 1) * P], max_part[:, 4 * n + m, :], identb[:],
                                            start=True, stop=True)
                last.then_inc(max_rows, 1)

            def finish(i, n):
                if n == 0:
                    pe.wait_ge(acc_kept, START + i + 1)
                    pe.wait_ge(added, START + i)
                    for c in range(8):
                        last = nc.tensor.matmul(side[:, 2, 18 * c:18 * c + 18], vals_t[:, c * P:(c + 1) * P], selm[:], start=True, stop=True)
                    last.then_inc(folded, 1)
                elif n == 1:
                    pe.wait_ge(normed, START + i + 1)
                    for h in range(2):
                        last = nc.tensor.matmul(side[0:64, 2, h * P:(h + 1) * P], vals[:, h, :, :], ident[:], start=True, stop=True)
                    last.then_inc(turned, 1)
                else:
                    pe.wait_ge(turn_kept, START + i + 1)
                    for half in range(2):
                        last = nc.tensor.matmul(side[:, 2, 0:P], w_out[:, half, :], feat[:, half, :],
                                                start=(half == 0), stop=(half == 1))
                    last.then_inc(projected, 1)

            def scores(i, par, u):
                c, j = u // 2, u % 2
                if u == 0:
                    pe.wait_ge(max_kept, START + i * ROWS + ROWS)
                pe.wait_ge(exp_done, START + i * STEPS + max(0, u - 2))
                for h in range(2):
                    last = nc.tensor.matmul(score[64 * h:64 * h + 64, u % 3, :], k_st[0:XROWS, par, h, c, :],
                                            q_st[0:XROWS, par, h, 8 * j:8 * j + 8, :], start=True, stop=True)
                last.then_inc(score_ready, 1)

            def values(i, par, group, j):
                if group == 0 and j == 0:
                    pe.wait_ge(acc_kept, START + i)
                    pe.wait_ge(v_kept, START + i * 2 + 2)
                pe.wait_ge(exp_done, START + i * STEPS + 8 * group + 7 + j)
                for q in range(4):
                    c = 4 * group + q
                    last = nc.tensor.matmul(acc[32 * q:32 * q + 32, j, :], v_two[:, par, c, :],
                                            probs[:, c % 8, j * CHUNK:(j + 1) * CHUNK],
                                            start=(group == 0), stop=(group == A_COLS // 4 - 1))
                last.then_inc(pv_done, 1)

            stages = (prepare, nothing, stacks, maxima, nothing, rows)

            def tile(i, par, kind):
                plan = schedule(kind)
                for u in range(2):
                    scores(i, par, u)
                for u in range(STEPS):
                    if u + 2 < STEPS:
                        scores(i, par, u + 2)
                    if u >= 8 and u % 8 in VALUES_AT:
                        values(i, par, u // 8 - 1, VALUES_AT.index(u % 8))
                    for stage, n in plan[u]:
                        if stage == "prepare":
                            pe.wait_ge(normed if n == 0 else turn_kept, START + i)
                        if stage == "finish" and n == 0 and kind == 1:
                            pe.wait_ge(qkv_kept, START + 3)
                        if stage == "finish" and n >= 1 and kind < A_TILES - 2:
                            pe.wait_ge(xt_kept if n == 1 else qkv_kept, START + i + 3)
                        carry([(stage, n)], i, par, stages, finish)
                for j in range(2):
                    values(i, par, A_COLS // 4 - 1, j)

            first_stages(stages)
            tiles(pe, tile)
            for n in range(3):
                finish(A_TILES - 1, n)

        @block.scalar
        def _(act):
            act.wait_ge(zeroed, START + 8)

            def arrange(i, n):
                act.wait_ge(split, START + i * 4 + 4)
                act.wait_ge(stacked, START + i * STACKS)
                g = n % 3
                arr = q_arr if n < 3 else k_arr
                src = (part[:, g, :, 0:8].unsqueeze(2).broadcast_to([P, A_COLS, 3, 8]) if n < 3
                       else part[:, :, :, 8:16].rearrange("p r c d -> p c r d"))
                nc.scalar.activation(arr[:, :, 32 * g:32 * g + 24].rearrange("p c (r d) -> p c r d", r=3), src, ACT.Copy).then_inc(arranged, 1)

            def stacks(i, par, n):
                if n == 0:
                    nc.scalar.activation(v_two[0:64, par, :, 0:8], qkv[0:64, :, 16:24], ACT.Copy).then_inc(v_kept, 1)
                    nc.scalar.activation(v_two[64:P, par, :, 16:24], qkv[64:P, :, 16:24], ACT.Copy).then_inc(v_kept, 1)
                act.wait_ge(stacked, START + i * STACKS + n + 1)
                st = q_st if n < 4 else k_st
                c0 = 4 * (n % 4)
                nc.scalar.activation(st[0:KROWS, par, :, c0:c0 + 4, :].rearrange("p h c t -> p c h t"),
                                     side[0:KROWS, n % 2, :].rearrange("p (c h t) -> p c h t", c=4, h=2), ACT.Copy).then_inc(stack_kept, 1)

            def nothing(*_):
                pass

            def rows(i, par, n):
                act.wait_ge(max_rows, START + i * ROWS + n + 1)
                h, c0 = n // 2, n % 2 * 8
                nc.scalar.activation(q_st[KROWS:XROWS, par, h, c0:c0 + 8, :].rearrange("p c t -> p (c t)"),
                                     side[KROWS:XROWS, n % 2, :], ACT.Copy).then_inc(max_kept, 1)

            stages = (nothing, arrange, stacks, nothing, nothing, rows)

            def tile(i, par, kind):
                plan = schedule(kind, reader=True)
                for u in range(STEPS):
                    c, j = u // 2, u % 2
                    act.wait_ge(score_ready, START + i * STEPS + u + 1)
                    act.wait_ge(pv_done, START + i * (A_COLS // 2) + max(0, 2 * (c // 4) - 2))
                    nc.scalar.activation(probs[:, c % 8, j * CHUNK:(j + 1) * CHUNK], score[:, u % 3, :],
                                         ACT.Exp, scale=A_SCALE).then_inc(exp_done, 1)
                    carry(plan[u], i, par, stages, nothing)

            first_stages(stages)
            tiles(act, tile)

        @block.gpsimd
        def _(pool):
            for n, (dst, value) in enumerate(((q_arr[:], 0.0), (k_arr[:], 0.0), (v_two[:], 0.0), (k_st[96:P], 1.0), (q_st[96:P], 0.0),
                                              (vals_t[:], 0.0), (v_two[0:64, :, :, 8:9], 1.0), (v_two[64:P, :, :, 24:25], 1.0))):
                nc.gpsimd.memset(dst, value).then_inc(zeroed, 1)
                pool.wait_ge(zeroed, START + n + 1)

        @block.vector
        def _(dve):
            dve.wait_ge(loaded, START + 80)
            dve.wait_ge(zeroed, START + 8)

            def prepare(i, n):
                if n == 0:
                    dve.wait_ge(xt_ready, START + i + 1)
                    dve.wait_ge(based, START + i)
                    dve.wait_ge(qkv_ready, START + i)
                    nc.vector.tensor_copy(x_t[:], side[:, 2, 0:P]).then_inc(xt_kept, 1)
                    dve.wait_ge(xt_kept, START + i + 1)
                    nc.vector.tensor_scalar(resid[:, bass.ts(i, P)], x_t[:], b_col[:], None, ALU.add).then_inc(based, 1)
                elif n == 1:
                    dve.wait_ge(qkv_ready, START + i + 1)
                    dve.wait_ge(v_kept, START + i * 2)
                    dve.wait_ge(split, START + i * 4)
                    nc.vector.tensor_tensor(qkv[:].rearrange("p c e -> p (c e)"), side[:, 2, 0:3 * D], b_bc[:], ALU.add)\
                        .then_inc(qkv_kept, 1)
                    dve.wait_ge(qkv_kept, START + i + 1)
                    dve.wait_ge(arranged, START + i * 6)
                    nc.vector.tensor_copy(part[:, 0], qkv[:, :, 0:16]).then_inc(split, 1)
                    dve.wait_ge(split, START + i * 4 + 1)
                    nc.vector.tensor_tensor(rest[:], qkv[:, :, 0:16], part[:, 0], ALU.subtract).then_inc(split, 1)
                    dve.wait_ge(split, START + i * 4 + 2)
                    nc.vector.tensor_copy(part[:, 1], rest[:]).then_inc(split, 1)
                    dve.wait_ge(split, START + i * 4 + 3)
                    nc.vector.tensor_tensor(part[:, 2], rest[:], part[:, 1], ALU.subtract).then_inc(split, 1)

            def maxima(i, par, n):
                dve.wait_ge(raw_ready, START + i * HALVES + n + 1)
                if n == 0:
                    dve.wait_ge(max_split, START + i * 3)
                nc.vector.tensor_reduce(neg_half[:, n:n + 1], side[:, n % 2, :], AX.X, ALU.max, negate=True).then_inc(maxed, 1)

            def parts(i):
                dve.wait_ge(maxed, START + i * HALVES + HALVES)
                dve.wait_ge(max_rows, START + i * ROWS)
                nc.vector.tensor_reduce(neg_max[:], neg_half[:].rearrange("p (b j) -> p b j", j=2), AX.X, ALU.min).then_inc(max_split, 1)
                dve.wait_ge(max_split, START + i * 3 + 1)
                nc.vector.tensor_copy(max_part[:, :, 0], neg_max[:]).then_inc(max_split, 1)
                dve.wait_ge(max_split, START + i * 3 + 2)
                nc.vector.tensor_tensor(max_part[:, :, 1], neg_max[:], max_part[:, :, 0], ALU.subtract).then_inc(max_split, 1)

            def nothing(*_):
                pass

            def finish(i, n):
                if n == 0:
                    dve.wait_ge(folded, START + i + 1)
                    fold = side[:, 2, 0:144].rearrange("p (c h e) -> p c h e", c=8, h=2)
                    nc.vector.reciprocal(recip[:], fold[:, :, :, 8]).then_inc(inverted, 1)
                    dve.wait_ge(inverted, START + i + 1)
                    nc.vector.tensor_tensor(vals[:].rearrange("p h c d -> p c h d"), fold[:, :, :, 0:8],
                                            recip[:].unsqueeze(3).broadcast_to([P, 8, 2, A_HD]), ALU.mult).then_inc(normed, 1)
                elif n == 1:
                    dve.wait_ge(turned, START + i + 1)
                    nc.vector.tensor_copy(feat[:].rearrange("p a (h t) -> p h a t", h=2),
                                          side[0:64, 2, 0:2 * P].rearrange("p (h a t) -> p h a t", h=2, a=2)).then_inc(turn_kept, 1)
                else:
                    dve.wait_ge(projected, START + i + 1)
                    nc.vector.tensor_tensor(resid[:, bass.ts(i, P)], side[:, 2, 0:P], resid[:, bass.ts(i, P)], ALU.add).then_inc(added, 1)

            stages = (prepare, nothing, nothing, maxima, parts, nothing)

            def tile(i, par, kind):
                plan = schedule(kind, reader=True)
                for step in plan:
                    carry(step, i, par, stages, finish)
                dve.wait_ge(pv_done, START + i * (A_COLS // 2) + A_COLS // 2)
                dve.wait_ge(folded, START + i)
                nc.vector.tensor_copy(vals_t[:], acc[:].rearrange("p a n -> p (a n)")).then_inc(acc_kept, 1)

            first_stages(stages)
            tiles(dve, tile)
            for n in range(3):
                finish(A_TILES - 1, n)


NORM_STEPS = "mean_ready centred squared var_ready logged rooted normed"


def norm_semaphores(core):
    return {n: core.sem("n_" + n) for n in NORM_STEPS.split()}


def norm_stage(nc, keep, call, out=None, affine=None):
    resid, mean_w = keep["resid"], keep["mean_w"]
    out = resid if out is None else out
    with ExitStack() as stack:
        core = Core(nc, stack, f"n{call}_")
        centre = core.sb("centre", [P, CHUNKS, CHUNK])
        square = core.sb("square", [P, CHUNKS, CHUNK])
        logs = core.sb("logs", [P, CHUNKS, CHUNK])
        rstd = core.sb("rstd", [P, CHUNKS, CHUNK])
        gain = core.sb("gain", [P, 2])
        mean = core.psum("mean_ps", [P, CHUNKS, CHUNK])
        var = core.psum("var_ps", [P, CHUNKS, CHUNK])
        mean_ready, centred, squared, var_ready, logged, rooted, normed = (keep["norm_sems"][n] for n in NORM_STEPS.split())
        gain_in, scaled = (core.sem("gain_in"), core.sem("scaled")) if affine else (None, None)
        past = call * CHUNKS
        block = stack.enter_context(nc.Block())

        @block.sync
        def _(sp):
            if affine:
                for n in range(2):
                    sp.dma_start(gain[:, n:n + 1], affine[n].unsqueeze(1)).then_inc(gain_in, 16)
                sp.wait_ge(gain_in, 32)

        @block.tensor
        def _(pe):
            for c in range(CHUNKS):
                nc.tensor.matmul(mean[:, c, :], mean_w[:], resid[:, c * CHUNK:(c + 1) * CHUNK], start=True, stop=True)\
                    .then_inc(mean_ready, 1)
            for c in range(CHUNKS):
                pe.wait_ge(squared, past + c + 1)
                nc.tensor.matmul(var[:, c, :], mean_w[:], square[:, c, :], start=True, stop=True).then_inc(var_ready, 1)

        @block.scalar
        def _(act):
            for c in range(CHUNKS):
                act.wait_ge(centred, past + c + 1)
                nc.scalar.activation(square[:, c, :], centre[:, c, :], ACT.Square).then_inc(squared, 1)
            for c in range(CHUNKS):
                act.wait_ge(var_ready, past + c + 1)
                nc.scalar.activation(logs[:, c, :], var[:, c, :], ACT.Ln, bias=keep["eps"][:]).then_inc(logged, 1)
            for c in range(CHUNKS):
                act.wait_ge(logged, past + c + 1)
                nc.scalar.activation(rstd[:, c, :], logs[:, c, :], ACT.Exp, scale=-0.5).then_inc(rooted, 1)

        @block.vector
        def _(dve):
            for c in range(CHUNKS):
                dve.wait_ge(mean_ready, past + c + 1)
                nc.vector.tensor_tensor(centre[:, c, :], resid[:, c * CHUNK:(c + 1) * CHUNK], mean[:, c, :], ALU.subtract)\
                    .then_inc(centred, 1)
            for c in range(CHUNKS):
                cols = slice(c * CHUNK, (c + 1) * CHUNK)
                dve.wait_ge(rooted, past + c + 1)
                nc.vector.tensor_tensor(out[:, cols], centre[:, c, :], rstd[:, c, :], ALU.mult).then_inc(normed, 1)
                if affine:
                    dve.wait_ge(gain_in, 32)
                    dve.wait_ge(normed, past + c + 1)
                    nc.vector.tensor_scalar(out[:, cols], out[:, cols], gain[:, 0:1], gain[:, 1:2], ALU.mult, ALU.add)\
                        .then_inc(scaled, 1)
            dve.wait_ge(normed, past + CHUNKS)
            if affine:
                dve.wait_ge(scaled, CHUNKS)


def local_stage(nc, keep, w_qkv, q_scale, k_scale, w_out, ln_g, ln_b, w1, b1, w2, b2, rotary, band):
    resid, ident, identb, mean_w = (keep[k] for k in ("resid", "ident", "identb", "mean_w"))
    GROUPS = HEADS // GROUP
    KN, JN = UNITS * TTILES, UNITS * QTILES
    NF = len(FF_PARTS)
    FF_LOADS = (1 + 3 * NF + 3) * 16
    HALF = HD // 2
    LEAD = 4
    first_use = [next(j for j in range(QTILES) if q_tile(j)[0] + q_tile(j)[1] > t * P) for t in range(TTILES)]
    PROJECT_IN = {n * QTILES + first_use[t] - LEAD: n * TTILES + t for n in range(UNITS) for t in range(TTILES)}
    TURN_IN = {j + LEAD - 1: k for j, k in PROJECT_IN.items()}
    HEAD, BODY = range(-LEAD, 0), range(JN + 2)
    HEAD_AT = {(2, 1): -4, (3, 0): -3, (3, 2): -2}
    with ExitStack() as stack:
        core = Core(nc, stack, "b_")
        sb, sem = core.sb, core.sem
        stream = sb("stream", [P, B, S])
        shifted = sb("shifted", [P, B, S])
        w_all = sb("w_all", [P, 3, HEADS * HD])
        w_o = sb("w_o", [P, GROUPS * PAIRS, D])
        rot = sb("rot", [P, 4, TTILES, HD])
        scale_bc = sb("scale_bc", [P, 2, HD])
        tab = sb("tab", [P, 4, TTILES, HD])
        band_f = sb("band_f", [QTILE, P])
        band_b = sb("band_b", [QTILE, P], BF16)
        square = sb("square", [P, 2 * GROUP, HD])
        sum_sq = sb("sum_sq", [P, 2 * GROUP])
        clipped = sb("clipped", [P, 2 * GROUP])
        neg_half = sb("neg_half", [P, 2 * GROUP])
        inv_norm = sb("inv_norm", [P, 2 * GROUP])
        unit = sb("unit", [P, 2 * GROUP, HD])
        with_cos = sb("with_cos", [P, 2, GROUP, HD])
        with_sin = sb("with_sin", [P, 2, GROUP, HD])
        turned = sb("turned", [P, 2, 2, GROUP, HD])
        k_t = sb("k_t", [P, PAIRS, S])
        q_t = sb("q_t", [P, PAIRS, 2, S])
        v_tok = sb("v_tok", [P, 2, GCOLS])
        neg_max = sb("neg_max", [QTILE, GROUP])
        neg_bias = sb("neg_bias", [QTILE, 2, GROUP])
        probs = sb("probs", [QTILE, 2, GROUP, P])
        row_sum = sb("row_sum", [QTILE, 2, GROUP])
        inv_sum = sb("inv_sum", [QTILE, 2, GROUP])
        normed = sb("normed", [QTILE, 2, GROUP, P])
        probs_t = sb("probs_t", [P, 2, GROUP, QTILE])
        att = sb("att", [P, 2, PAIRS, QTILE])
        w1_s = sb("w1_s", [P, 2 * FF])
        w2_s = sb("w2_s", [P, NF, D])
        ln_s = sb("ln_s", [P, 2])
        b1_s = sb("b1_s", [P, 2, NF])
        b2_s = sb("b2_s", [P, 1])
        centre = sb("centre", [P, CHUNKS, CHUNK])
        spread = sb("spread", [P, CHUNKS, CHUNK])
        gate = sb("gate", [P, 2, CHUNK])
        hidden = sb("hidden", [P, NF, CHUNK])
        banks = core.psum("banks", [P, 8, CHUNK])
        QK, TURN, V, ATT, SCORE = 0, 2, 4, 5, 6
        OUT_COL = PAIRS * QTILE
        flat = stream[:].rearrange("p b s -> p (b s)")
        flat_shifted = shifted[:].rearrange("p b s -> p (b s)")

        names = """consts zeroed band_ready begun shift_a shift_f scale_in tab_ready wqkv_in wo_in wf_in
            qk_ready squared summed clip_done norm_inv unit_ready cos_ready sin_ready turn_ready qkt_ready qkt_kept
            v_ready v_kept score_ready maxed bias_ready exp_done inverted p_normed p_turned pt_kept att_ready att_kept
            out_ready added f_mean f_centred f_squared f_var f_log f_root f_normed f_affine f_gate f_gelu f_a f_hid
            f_out f_added final reload_ok"""
        (consts, zeroed, band_ready, begun, shift_a, shift_f, scale_in, tab_ready, wqkv_in, wo_in, wf_in,
         qk_ready, squared, summed, clip_done, norm_inv, unit_ready, cos_ready, sin_ready, turn_ready, qkt_ready, qkt_kept,
         v_ready, v_kept, score_ready, maxed, bias_ready, exp_done, inverted, p_normed, p_turned, pt_kept, att_ready, att_kept,
         out_ready, added, f_mean, f_centred, f_squared, f_var, f_log, f_root, f_normed, f_affine, f_gate, f_gelu, f_a, f_hid,
         f_out, f_added, final, reload_ok) = (sem(n) for n in names.split())
        start_counts(nc, core)
        block = stack.enter_context(nc.Block())
        all_q = range(JN)

        def token_tile(k):
            n = k // TTILES
            return n % B, n // B, k % TTILES

        def query_tile(j):
            n = j // QTILES
            return n % B, n // B, j % QTILES

        EARLY = range(CHUNKS // B * (B - 1))
        LATE = range(len(EARLY), CHUNKS)

        def layers(engine, attend, feed_forward):
            attend(0, HEAD)
            with engine.Fori(0, DEPTH - 1) as l:
                attend(l, BODY)
                feed_forward(l, True)
            attend(DEPTH - 1, BODY)
            feed_forward(DEPTH - 1, False)

        @block.sync
        def _(sp):
            sp.dma_start(rot[:], rotary).then_inc(consts, 16)
            sp.dma_start(band_f[:], band).then_inc(consts, 16)
            with sp.Fori(0, DEPTH) as l:
                sp.wait_ge(v_ready, START + l * JN)
                sp.sem_inc(reload_ok, 1)
                sp.dma_start(w_all[:], w_qkv[bass.ds(l, 1), :, :].rearrange("a p (m n) -> p (a m) n", m=3)).then_inc(wqkv_in, 16)
                sp.wait_ge(tab_ready, START + l * 6)
                sp.sem_inc(reload_ok, 1)
                sp.dma_start(scale_bc[:, 0, :], q_scale[bass.ds(l, 1), :].broadcast_to([P, HD])).then_inc(scale_in, 16)
                sp.dma_start(scale_bc[:, 1, :], k_scale[bass.ds(l, 1), :].broadcast_to([P, HD])).then_inc(scale_in, 16)
                sp.wait_ge(out_ready, START + l * JN)
                sp.sem_inc(reload_ok, 1)
                sp.dma_start(w_o[:], w_out[bass.ds(l, 1), :, :, :].rearrange("a p h n -> p (a h) n")).then_inc(wo_in, 16)
                sp.wait_ge(f_added, START + l * CHUNKS)
                sp.sem_inc(reload_ok, 1)
                sp.dma_start(w1_s[:], w1[bass.ds(l, 1), :, :].rearrange("a p n -> p (a n)")).then_inc(wf_in, 16)
                for n, (f0, fn) in enumerate(FF_PARTS):
                    sp.dma_start(w2_s[0:fn, n, :], w2[bass.ds(l, 1), f0:f0 + fn, :].rearrange("a p n -> p (a n)")).then_inc(wf_in, 16)
                    for side in range(2):
                        sp.dma_start(b1_s[0:fn, side, n:n + 1],
                                     b1[bass.ds(l, 1), side * FF + f0:side * FF + f0 + fn].rearrange("a p -> p a")).then_inc(wf_in, 16)
                sp.dma_start(b2_s[:], b2[bass.ds(l, 1), :].rearrange("a p -> p a")).then_inc(wf_in, 16)
                sp.dma_start(ln_s[:, 0:1], ln_g[bass.ds(l, 1), :].rearrange("a p -> p a")).then_inc(wf_in, 16)
                sp.dma_start(ln_s[:, 1:2], ln_b[bass.ds(l, 1), :].rearrange("a p -> p a")).then_inc(wf_in, 16)

        @block.tensor
        def _(pe):
            def project(l, k):
                b, g, t = token_tile(k)
                if k == 0:
                    pe.wait_ge(wqkv_in, START + l * 16 + 16)
                if k in (0, TTILES):
                    pe.wait_ge(shift_a, START + l * 4 + 2 + 2 * b)
                pe.wait_ge(unit_ready, START + l * KN + k)
                for m in range(2):
                    last = nc.tensor.matmul(banks[:, QK + m, :], shifted[:, b, t * P:(t + 1) * P],
                                            w_all[:, m, g * GCOLS:(g + 1) * GCOLS], start=True, stop=True)
                last.then_inc(qk_ready, 1)

            def turn_tile(l, k, turned_probs):
                pe.wait_ge(turn_ready, START + l * KN + k + 1)
                for m in range(2):
                    pe.wait_ge(pt_kept, START + l * (2 * JN) + max(0, 2 * turned_probs + m - 1))
                    pe.wait_ge(qkt_kept, START + l * (2 * KN) + max(0, 2 * k + m - 1))
                    for h in range(PAIRS):
                        last = nc.tensor.transpose(banks[:, TURN + m, h * P:(h + 1) * P], turned[:, k % 2, m, 2 * h:2 * h + 2, :], ident[:])
                    last.then_inc(qkt_ready, 1)

            def value_rows(l, j):
                b, g, t = query_tile(j)
                _, _, k0, nk = q_tile(t)
                pe.wait_ge(v_kept, START + l * JN + j)
                nc.tensor.matmul(banks[0:nk, V, :], shifted[:, b, k0:k0 + nk], w_all[:, 2, g * GCOLS:(g + 1) * GCOLS], start=True, stop=True)\
                    .then_inc(v_ready, 1)

            def scores(l, j):
                q0, nq, k0, nk = q_tile(j % QTILES)
                pe.wait_ge(qkt_kept, START + l * (2 * KN) + 2 * (j // QTILES * TTILES + -(-(q0 + nq) // P)))
                if j == 0:
                    pe.wait_ge(f_added, START + l * CHUNKS)
                off = WIN - (q0 - k0)
                for half in range(2):
                    pe.wait_ge(exp_done, START + l * (2 * JN) + max(0, 2 * j + half - 1))
                    out = banks[0:nq, SCORE + half, :].rearrange("p (h k) -> p h k", h=4)[:, :, 0:nk]
                    nc.tensor.matmul(out, identb[0:QTILE, 0:nq],
                                     band_b[:, off:off + nk].unsqueeze(1).broadcast_to([QTILE, 4, nk]),
                                     start=True, stop=False, skip_group_check=True)
                    for n in range(4):
                        h = 4 * half + n
                        last = nc.tensor.matmul(out[:, n, :], q_t[:, h // 2, h % 2, q0:q0 + nq], k_t[:, h // 2, k0:k0 + nk],
                                                start=False, stop=(n == 3), skip_group_check=True)
                    last.then_inc(score_ready, 1)

            def turn_probs(l, j, turned_tiles):
                _, nq, _, nk = q_tile(j % QTILES)
                pe.wait_ge(p_normed, START + l * JN + j + 1)
                for h in range(GROUP):
                    if h % 4 == 0:
                        pe.wait_ge(pt_kept, START + l * (2 * JN) + max(0, 2 * j + h // 4 - 1))
                        pe.wait_ge(qkt_kept, START + l * (2 * KN) + max(0, 2 * turned_tiles + h // 4 - 1))
                    last = nc.tensor.matmul(banks[0:nk, TURN + h // 4, (h % 4) * P:(h % 4) * P + nq], normed[0:nq, j % 2, h, 0:nk],
                                            ident[0:nq, 0:nq], start=True, stop=True, is_transpose=nq == QTILE)
                    if h % 4 == 3:
                        last.then_inc(p_turned, 1)

            def values(l, j):
                _, nq, _, nk = q_tile(j % QTILES)
                pe.wait_ge(v_kept, START + l * JN + j + 1)
                pe.wait_ge(added, START + l * JN + j)
                for h in range(GROUP):
                    r = HD * (h % 2)
                    if h % 4 == 0:
                        pe.wait_ge(pt_kept, START + l * (2 * JN) + 2 * j + h // 4 + 1)
                    last = nc.tensor.matmul(banks[r:r + HD, ATT, (h // 2) * QTILE:(h // 2) * QTILE + nq], v_tok[0:nk, j % 2, h * HD:(h + 1) * HD],
                                            probs_t[0:nk, j % 2, h, 0:nq], start=True, stop=True)
                last.then_inc(att_ready, 1)

            def output(l, j):
                _, g, t = query_tile(j)
                _, nq, _, _ = q_tile(t)
                if j == 0:
                    pe.wait_ge(wo_in, START + l * 16 + 16)
                pe.wait_ge(att_kept, START + l * JN + j + 1)
                for h in range(PAIRS):
                    last = nc.tensor.matmul(banks[:, ATT, OUT_COL:OUT_COL + nq], w_o[:, g * PAIRS + h, :], att[:, j % 2, h, 0:nq],
                                            start=(h == 0), stop=(h == PAIRS - 1))
                last.then_inc(out_ready, 1)

            def means(l, chunks):
                pe.wait_ge(unit_ready, START + l * KN + KN)
                for c in chunks:
                    pe.wait_ge(shift_f, START + l * (2 * B) + 2 * (c * CHUNK // S) + 2)
                    nc.tensor.matmul(banks[:, c, :], mean_w[:], flat_shifted[:, c * CHUNK:(c + 1) * CHUNK], start=True, stop=True)\
                        .then_inc(f_mean, 1)

            def variances(l, chunks):
                for c in chunks:
                    pe.wait_ge(f_squared, START + l * CHUNKS + c + 1)
                    nc.tensor.matmul(banks[:, c, :], mean_w[:], spread[:, c, :], start=True, stop=True).then_inc(f_var, 1)

            pe.wait_ge(band_ready, START + 1)

            def attend(l, slots):
                for j in slots:
                    if j in all_q:
                        scores(l, j)
                    if j - 2 in all_q:
                        values(l, j - 2)
                    if j in TURN_IN:
                        turn_tile(l, TURN_IN[j], min(JN, max(0, j - 1)))
                    if j - 2 in all_q:
                        output(l, j - 2)
                    if j in all_q:
                        value_rows(l, j)
                    if j in PROJECT_IN:
                        project(l, PROJECT_IN[j])
                    if j - 1 in all_q:
                        turn_probs(l, j - 1, sum(1 for i in TURN_IN if i <= j))
                    if j == JN - 1:
                        means(l, EARLY)
                    if j == JN + 1:
                        variances(l, EARLY)

            def feed_forward(l, head):
                pe.wait_ge(wf_in, START + l * FF_LOADS + FF_LOADS)
                means(l, LATE)
                variances(l, LATE)
                pe.wait_ge(f_log, START + l * CHUNKS + CHUNKS)
                for c in range(CHUNKS):
                    pe.wait_ge(f_affine, START + l * CHUNKS + c + 1)
                    for n, (f0, fn) in enumerate(FF_PARTS):
                        k = c * NF + n
                        pe.wait_ge(f_gelu, START + l * (CHUNKS * NF) + k)
                        nc.tensor.matmul(banks[0:fn, 4, :], w1_s[:, FF + f0:FF + f0 + fn], centre[:, c, :], start=True, stop=True)\
                            .then_inc(f_gate, 1)
                        pe.wait_ge(f_hid, START + l * (CHUNKS * NF) + k)
                        nc.tensor.matmul(banks[0:fn, 5, :], w1_s[:, f0:f0 + fn], centre[:, c, :], start=True, stop=True)\
                            .then_inc(f_a, 1)
                        if head and (c, n) in HEAD_AT:
                            attend(l + 1, (HEAD_AT[c, n],))
                    pe.wait_ge(f_hid, START + l * (CHUNKS * NF) + (c + 1) * NF)
                    if c >= 2:
                        pe.wait_ge(f_added, START + l * CHUNKS + c - 1)
                    for n, (f0, fn) in enumerate(FF_PARTS):
                        last = nc.tensor.matmul(banks[:, 6 + c % 2, :], w2_s[0:fn, n, :], hidden[0:fn, n, :], start=(n == 0), stop=(n == NF - 1))
                    last.then_inc(f_out, 1)
                if head:
                    attend(l + 1, HEAD[-1:])

            layers(pe, attend, feed_forward)

        @block.scalar
        def _(act):
            def keep_turned(l, k):
                _, _, t = token_tile(k)
                act.wait_ge(qkt_ready, START + l * (2 * KN) + 2 * k + 1)
                cols = slice(t * P, (t + 1) * P)
                nc.scalar.activation(q_t[0:HD, :, 0, cols], banks[0:HD, TURN, :].rearrange("p (h s) -> p h s", h=PAIRS), ACT.Copy)
                nc.scalar.activation(q_t[HD:P, :, 1, cols], banks[HD:P, TURN, :].rearrange("p (h s) -> p h s", h=PAIRS), ACT.Copy)\
                    .then_inc(qkt_kept, 1)
                act.wait_ge(qkt_ready, START + l * (2 * KN) + 2 * k + 2)
                nc.scalar.activation(k_t[:, :, cols], banks[:, TURN + 1, :].rearrange("p (h s) -> p h s", h=PAIRS), ACT.Copy)\
                    .then_inc(qkt_kept, 1)

            def keep_values(l, j):
                _, nq, _, _ = q_tile(j % QTILES)
                act.wait_ge(att_ready, START + l * JN + j + 1)
                if j >= 2:
                    act.wait_ge(out_ready, START + l * JN + j - 1)
                nc.scalar.activation(att[:, j % 2, :, 0:nq], banks[:, ATT, 0:OUT_COL].rearrange("p (h s) -> p h s", h=PAIRS)[:, :, 0:nq],
                                     ACT.Copy).then_inc(att_kept, 1)

            def exponentials(l, j):
                _, nq, _, nk = q_tile(j % QTILES)
                w = j % 2
                act.wait_ge(p_normed, START + l * JN + max(0, j - 1))
                for h in range(GROUP):
                    if h % 4 == 0:
                        act.wait_ge(bias_ready, START + l * (2 * JN) + 2 * j + h // 4 + 1)
                    last = nc.scalar.activation(probs[0:nq, w, h, 0:nk], banks[0:nq, SCORE + h // 4, (h % 4) * P:(h % 4) * P + nk],
                                                ACT.Exp, bias=neg_bias[0:nq, w, h:h + 1], scale=QK_SCALE,
                                                accum_out=row_sum[0:nq, w, h:h + 1])
                    if h % 4 == 3:
                        last.then_inc(exp_done, 1)

            act.wait_ge(zeroed, START + 2)

            def attend(l, slots):
                for j in slots:
                    if j - 2 in all_q:
                        keep_values(l, j - 2)
                    if j in TURN_IN:
                        keep_turned(l, TURN_IN[j])
                    if j in all_q:
                        exponentials(l, j)
                    if j in PROJECT_IN:
                        k = PROJECT_IN[j]
                        act.wait_ge(qk_ready, START + l * KN + k + 1)
                        act.wait_ge(summed, START + l * KN + k)
                        nc.scalar.activation(square[:].rearrange("p h d -> p (h d)"),
                                             banks[:, QK:QK + 2, :].rearrange("p m n -> p (m n)"), ACT.Square).then_inc(squared, 1)
                    if j in all_q:
                        _, _, _, nk = q_tile(j % QTILES)
                        act.wait_ge(v_ready, START + l * JN + j + 1)
                        nc.scalar.activation(v_tok[0:nk, j % 2, :], banks[0:nk, V, :], ACT.Copy).then_inc(v_kept, 1)
                    if j == JN + 1:
                        squares(l, EARLY)

            def squares(l, chunks):
                for c in chunks:
                    act.wait_ge(f_centred, START + l * CHUNKS + c + 1)
                    nc.scalar.activation(spread[:, c, :], centre[:, c, :], ACT.Square).then_inc(f_squared, 1)

            def feed_forward(l, head):
                squares(l, LATE)
                for c in range(CHUNKS):
                    act.wait_ge(f_var, START + l * CHUNKS + c + 1)
                    nc.scalar.activation(spread[:, c, :], banks[:, c, :], ACT.Ln, bias=keep["eps"][:]).then_inc(f_log, 1)
                for c in range(CHUNKS):
                    act.wait_ge(f_log, START + l * CHUNKS + c + 1)
                    nc.scalar.activation(spread[:, c, :], spread[:, c, :], ACT.Exp, scale=-0.5).then_inc(f_root, 1)
                for c in range(CHUNKS):
                    for n, (f0, fn) in enumerate(FF_PARTS):
                        k = c * NF + n
                        act.wait_ge(f_gate, START + l * (CHUNKS * NF) + k + 1)
                        if k >= 2:
                            act.wait_ge(f_hid, START + l * (CHUNKS * NF) + k - 1)
                        nc.scalar.activation(gate[0:fn, k % 2, :], banks[0:fn, 4, :], ACT.Gelu, bias=b1_s[0:fn, 1, n:n + 1])\
                            .then_inc(f_gelu, 1)
                        if head and (c, n) in HEAD_AT:
                            attend(l + 1, (HEAD_AT[c, n],))
                if head:
                    attend(l + 1, HEAD[-1:])

            layers(act, attend, feed_forward)

        @block.gpsimd
        def _(pool):
            nc.gpsimd.memset(shifted[HD:P, :, 0:1], 0.0).then_inc(zeroed, 1)
            pool.wait_ge(zeroed, START + 1)
            nc.gpsimd.memset(q_t[:], 0.0).then_inc(zeroed, 1)
            pool.wait_ge(zeroed, START + 2)
            pool.wait_ge(consts, START + 32)

            def tables(l):
                pool.wait_ge(scale_in, START + l * 32 + 32)
                pool.wait_ge(cos_ready, START + l * KN)
                pool.wait_ge(p_normed, START + l * JN)
                for m in range(2):
                    def scales(lo):
                        return scale_bc[:, m, lo:lo + HALF].unsqueeze(1).broadcast_to([P, TTILES, HALF])
                    nc.gpsimd.tensor_tensor(tab[:, m], rot[:, m], scale_bc[:, m, :].unsqueeze(1).broadcast_to([P, TTILES, HD]), ALU.mult)\
                        .then_inc(tab_ready, 1)
                    nc.gpsimd.tensor_tensor(tab[:, 2 + m, :, 0:HALF], rot[:, 2 + m, :, 0:HALF], scales(HALF), ALU.mult).then_inc(tab_ready, 1)
                    nc.gpsimd.tensor_tensor(tab[:, 2 + m, :, HALF:HD], rot[:, 2 + m, :, HALF:HD], scales(0), ALU.mult).then_inc(tab_ready, 1)

            def attend(l, slots):
                if slots == HEAD:
                    tables(l)
                for j in slots:
                    if j - 1 in PROJECT_IN:
                        k = PROJECT_IN[j - 1]
                        if k == 0:
                            pool.wait_ge(tab_ready, START + l * 6 + 6)
                        pool.wait_ge(unit_ready, START + l * KN + k + 1)
                        pool.wait_ge(turn_ready, START + l * KN + k)
                        un = unit[:].rearrange("p (m h) d -> p m h d", m=2)
                        for m in range(2):
                            for lo, hi in ((0, HALF), (HALF, 0)):
                                nc.gpsimd.tensor_tensor(with_sin[:, m, :, lo:lo + HALF], un[:, m, :, hi:hi + HALF],
                                                        tab[:, 2 + m, k % TTILES, lo:lo + HALF].unsqueeze(1).broadcast_to([P, GROUP, HALF]),
                                                        ALU.mult).then_inc(sin_ready, 1)
                    if j in all_q:
                        _, nq, _, nk = q_tile(j % QTILES)
                        w = j % 2
                        pool.wait_ge(inverted, START + l * JN + j + 1)
                        pool.wait_ge(p_normed, START + l * JN + j)
                        pool.wait_ge(sin_ready, START + l * (4 * KN) + 4 * sum(1 for i in PROJECT_IN if i + 1 <= j))
                        pool.wait_ge(norm_inv, START + l * KN + sum(1 for i in PROJECT_IN if i < j))
                        pool.wait_ge(p_turned, START + l * (2 * JN) + max(0, 2 * j - 2))
                        nc.gpsimd.tensor_tensor(normed[0:nq, w, :, 0:nk], probs[0:nq, w, :, 0:nk],
                                                inv_sum[0:nq, w, :].unsqueeze(2).broadcast_to([nq, GROUP, nk]), ALU.mult).then_inc(p_normed, 1)
                    if j in PROJECT_IN:
                        k = PROJECT_IN[j]
                        pool.wait_ge(p_normed, START + l * JN + min(JN, max(0, j + 1)))
                        pool.wait_ge(unit_ready, START + l * KN + k)
                        pool.wait_ge(clip_done, START + l * KN + k + 1)
                        nc.gpsimd.tensor_tensor(inv_norm[:], clipped[:], neg_half[:], ALU.pow).then_inc(norm_inv, 1)

            def feed_forward(l, head):
                if head:
                    attend(l + 1, HEAD)

            layers(pool, attend, feed_forward)

        @block.vector
        def _(dve):
            dve.wait_ge(consts, START + 32)
            nc.vector.tensor_copy(band_b[:], band_f[:]).then_inc(band_ready, 1)
            nc.vector.memset(neg_half[:], -0.5)
            nc.vector.tensor_copy(flat, resid[:]).then_inc(begun, 1)
            dve.wait_ge(begun, START + 1)

            def shift(batches, done):
                nc.vector.tensor_copy(shifted[0:HD, batches], stream[0:HD, batches]).then_inc(done, 1)
                nc.vector.tensor_copy(shifted[HD:P, batches, 1:S], stream[HD:P, batches, 0:S - 1]).then_inc(done, 1)

            def centres(l, chunks):
                for c in chunks:
                    dve.wait_ge(f_mean, START + l * CHUNKS + c + 1)
                    dve.wait_ge(shift_f, START + l * (2 * B) + 2 * (c * CHUNK // S) + 2)
                    nc.vector.tensor_tensor(centre[:, c, :], flat_shifted[:, c * CHUNK:(c + 1) * CHUNK], banks[:, c, :], ALU.subtract)\
                        .then_inc(f_centred, 1)

            def maximum(l, j):
                _, nq, _, nk = q_tile(j % QTILES)
                for half in range(2):
                    heads = slice(4 * half, 4 * half + 4)
                    dve.wait_ge(score_ready, START + l * (2 * JN) + 2 * j + half + 1)
                    dve.wait_ge(bias_ready, START + l * (2 * JN) + max(0, 2 * j + half - 1))
                    nc.vector.tensor_reduce(neg_max[0:nq, heads], banks[0:nq, SCORE + half, :].rearrange("p (h k) -> p h k", h=4)[:, :, 0:nk],
                                            AX.X, ALU.max, negate=True).then_inc(maxed, 1)
                    dve.wait_ge(maxed, START + l * (2 * JN) + 2 * j + half + 1)
                    nc.vector.tensor_scalar(neg_bias[0:nq, j % 2, heads], neg_max[0:nq, heads], QK_SCALE, None, ALU.mult).then_inc(bias_ready, 1)

            def unit_and_cosines(l, k):
                dve.wait_ge(norm_inv, START + l * KN + k + 1)
                dve.wait_ge(cos_ready, START + l * KN + k)
                dve.wait_ge(sin_ready, START + l * (4 * KN) + 4 * k)
                nc.vector.tensor_tensor(unit[:], banks[:, QK:QK + 2, :].rearrange("p m (h d) -> p (m h) d", h=GROUP),
                                        inv_norm[:].unsqueeze(2).broadcast_to([P, 2 * GROUP, HD]), ALU.mult).then_inc(unit_ready, 1)
                dve.wait_ge(unit_ready, START + l * KN + k + 1)
                dve.wait_ge(turn_ready, START + l * KN + k)
                if k == 0:
                    dve.wait_ge(tab_ready, START + l * 6 + 6)
                nc.vector.tensor_tensor(with_cos[:], unit[:].rearrange("p (m h) d -> p m h d", m=2),
                                        tab[:, 0:2, k % TTILES, :].unsqueeze(2).broadcast_to([P, 2, GROUP, HD]), ALU.mult).then_inc(cos_ready, 1)

            def turn(l, k):
                dve.wait_ge(sin_ready, START + l * (4 * KN) + 4 * k + 4)
                dve.wait_ge(cos_ready, START + l * KN + k + 1)
                dve.wait_ge(qkt_ready, START + l * (2 * KN) + max(0, 2 * k - 2))
                nc.vector.tensor_tensor(turned[:, k % 2], with_cos[:], with_sin[:], ALU.add).then_inc(turn_ready, 1)

            def attend(l, slots):
                for j in slots:
                    if j in all_q:
                        maximum(l, j)
                    if j - 1 in PROJECT_IN:
                        unit_and_cosines(l, PROJECT_IN[j - 1])
                    if j - 2 in all_q:
                        b, _, t = query_tile(j - 2)
                        q0, nq, _, _ = q_tile(t)
                        dve.wait_ge(out_ready, START + l * JN + j - 1)
                        nc.vector.tensor_tensor(stream[:, b, q0:q0 + nq], banks[:, ATT, OUT_COL:OUT_COL + nq], stream[:, b, q0:q0 + nq], ALU.add)\
                            .then_inc(added, 1)
                    if j in all_q:
                        _, nq, _, _ = q_tile(j % QTILES)
                        dve.wait_ge(exp_done, START + l * (2 * JN) + 2 * j + 2)
                        dve.wait_ge(p_normed, START + l * JN + max(0, j - 1))
                        nc.vector.reciprocal(inv_sum[0:nq, j % 2, :], row_sum[0:nq, j % 2, :]).then_inc(inverted, 1)
                    if j - 1 in all_q:
                        _, nq, _, nk = q_tile((j - 1) % QTILES)
                        w = (j - 1) % 2
                        dve.wait_ge(att_ready, START + l * JN + max(0, j - 2))
                        for half in range(2):
                            dve.wait_ge(p_turned, START + l * (2 * JN) + 2 * (j - 1) + half + 1)
                            nc.vector.tensor_copy(probs_t[0:nk, w, 4 * half:4 * half + 4, 0:nq],
                                                  banks[0:nk, TURN + half, :].rearrange("p (h q) -> p h q", h=4)[:, :, 0:nq]).then_inc(pt_kept, 1)
                    if j in PROJECT_IN:
                        k = PROJECT_IN[j]
                        dve.wait_ge(squared, START + l * KN + k + 1)
                        dve.wait_ge(norm_inv, START + l * KN + k)
                        nc.vector.tensor_reduce(sum_sq[:], square[:], AX.X, ALU.add).then_inc(summed, 1)
                        dve.wait_ge(summed, START + l * KN + k + 1)
                        nc.vector.tensor_scalar(clipped[:], sum_sq[:], 1e-24, None, ALU.max).then_inc(clip_done, 1)
                    if j - 1 in PROJECT_IN:
                        turn(l, PROJECT_IN[j - 1])
                    if j == JN - 2:
                        dve.wait_ge(added, START + l * JN + JN - QTILES)
                        for b in range(B - 1):
                            shift(slice(b, b + 1), shift_f)
                    if j == JN:
                        centres(l, EARLY)

            def feed_forward(l, head):
                dve.wait_ge(added, START + l * JN + JN)
                shift(slice(B - 1, B), shift_f)
                centres(l, LATE)
                for c in range(CHUNKS):
                    dve.wait_ge(f_root, START + l * CHUNKS + c + 1)
                    nc.vector.tensor_tensor(centre[:, c, :], centre[:, c, :], spread[:, c, :], ALU.mult).then_inc(f_normed, 1)
                    dve.wait_ge(f_normed, START + l * CHUNKS + c + 1)
                    if c == 0:
                        dve.wait_ge(wf_in, START + l * FF_LOADS + FF_LOADS)
                    nc.vector.tensor_scalar(centre[:, c, :], centre[:, c, :], ln_s[:, 0:1], ln_s[:, 1:2], ALU.mult, ALU.add)\
                        .then_inc(f_affine, 1)
                for c in range(CHUNKS):
                    cols = slice(c * CHUNK, (c + 1) * CHUNK)
                    for n, (f0, fn) in enumerate(FF_PARTS):
                        k = c * NF + n
                        dve.wait_ge(f_gelu, START + l * (CHUNKS * NF) + k + 1)
                        dve.wait_ge(f_a, START + l * (CHUNKS * NF) + k + 1)
                        if n == 0:
                            dve.wait_ge(f_out, START + l * CHUNKS + c)
                        nc.vector.scalar_tensor_tensor(out=hidden[0:fn, n, :], in0=banks[0:fn, 5, :], scalar=b1_s[0:fn, 0, n:n + 1],
                                                       in1=gate[0:fn, k % 2, :], op0=ALU.add, op1=ALU.mult).then_inc(f_hid, 1)
                        if head and (c, n) in HEAD_AT:
                            attend(l + 1, (HEAD_AT[c, n],))
                    dve.wait_ge(f_out, START + l * CHUNKS + c + 1)
                    nc.vector.scalar_tensor_tensor(out=flat[:, cols], in0=banks[:, 6 + c % 2, :], scalar=b2_s[:], in1=flat[:, cols],
                                                   op0=ALU.add, op1=ALU.add).then_inc(f_added, 1)
                    if head and (c + 1) % (CHUNKS // B) == 0:
                        b = c // (CHUNKS // B)
                        dve.wait_ge(f_centred, START + l * CHUNKS + CHUNKS)
                        dve.wait_ge(f_added, START + l * CHUNKS + c + 1)
                        shift(slice(b, b + 1), shift_a)
                if head:
                    attend(l + 1, HEAD[-1:])

            dve.wait_ge(zeroed, START + 1)
            for b in range(B):
                shift(slice(b, b + 1), shift_a)
            layers(dve, attend, feed_forward)
            dve.wait_ge(f_added, START + DEPTH * CHUNKS)
            nc.vector.tensor_tensor(resid[:], resid[:], flat, ALU.add).then_inc(final, 1)
            dve.wait_ge(final, START + 1)


def retention_stage(nc, keep, w_qkv_heads, w_gate, w_out, gn_w, gn_b, tables, masks, causal_c):
    resid, ident = keep["resid"], keep["ident"]
    N = B * R_CHUNKS
    with ExitStack() as stack:
        core = Core(nc, stack)
        sb, sem = core.sb, core.sem
        w_heads = sb("r_w_heads", [P, 3, R_HD])
        w_bd = sb("r_w_bd", [P, 5, D])
        w_g = sb("r_w_g", [P, D])
        w_o = sb("r_w_o", [P, D])
        gn = sb("r_gn", [P, 2, D])
        tab = sb("r_tab", [P, 4, S])
        mask = sb("r_mask", [P, R_HEADS + D + 1])
        causal = sb("r_causal", [P, P])
        plain = sb("r_plain", [P, 2, CHUNK])
        crossed = sb("r_crossed", [P, 2, CHUNK])
        q_all = sb("r_q_all", [P, T])
        k_all = sb("r_k_all", [P, T])
        x_c = sb("r_x_c", [P, 2, P])
        q_c = sb("r_q_c", [P, 2, P])
        k_c = sb("r_k_c", [P, 2, P])
        q_heads = sb("r_q_heads", [P, 2, R_HEADS, P])
        kv = sb("r_kv", [P, 2, 2, D])
        masked = sb("r_masked", [P, 2, R_HEADS, P])
        update = sb("r_update", [P, D])
        summed = sb("r_summed", [P, D])
        state = sb("r_state", [P, D])
        y_all = sb("r_y_all", [P, N, D])
        g_all = sb("r_g_all", [P, N, D])
        work = sb("r_work", [P, N, D])
        stat = sb("r_stat", [P, 2, N * R_HEADS])
        z_t = sb("r_z_t", [P, T])
        banks = core.psum("r_banks", [P, 8, CHUNK])
        names = """loaded placed swapped proj_ready plain_ready crossed_ready qk_all x_ready q_ready k_ready heads_ready
            rows_ready kv_kept g_kept raw_ready masked_ready y_ready y_kept delta_ready updated summed_ready state_ready
            stat_done act_done turned turn_kept out_ready added"""
        (loaded, placed, swapped, proj_ready, plain_ready, crossed_ready, qk_all, x_ready, q_ready, k_ready, heads_ready,
         rows_ready, kv_kept, g_kept, raw_ready, masked_ready, y_ready, y_kept, delta_ready, updated, summed_ready, state_ready,
         stat_done, act_done, turned, turn_kept, out_ready, added) = (sem("r_" + n) for n in names.split())
        LOADS = 10 * 16
        start_counts(nc, core)
        block = stack.enter_context(nc.Block())

        UPDATE, VALUES = 6, 7

        def chunks(engine, front, back, start=lambda b: None):
            with engine.Fori(0, B) as b:
                start(b)
                first = b * R_CHUNKS
                front(first, 0)
                with engine.Fori(0, R_CHUNKS // 2 - 1) as pair:
                    for par in range(2):
                        front(first + pair * 2 + (par + 1), 1 - par)
                        back(first + pair * 2 + par, par, b)
                front(first + (R_CHUNKS - 1), 1)
                back(first + (R_CHUNKS - 2), 0, b)
                back(first + (R_CHUNKS - 1), 1, b)

        @block.sync
        def _(sp):
            for m, w in enumerate(w_qkv_heads):
                sp.dma_start(w_heads[:, m, :], w.rearrange("h d e -> (h d) e")).then_inc(loaded, 16)
            sp.dma_start(w_g[:], w_gate).then_inc(loaded, 16)
            sp.dma_start(w_o[:], w_out).then_inc(loaded, 16)
            sp.dma_start(gn[:, 0], gn_w.unsqueeze(0).broadcast_to([P, D])).then_inc(loaded, 16)
            sp.dma_start(gn[:, 1], gn_b.unsqueeze(0).broadcast_to([P, D])).then_inc(loaded, 16)
            sp.dma_start(tab[:], tables).then_inc(loaded, 16)
            sp.dma_start(mask[:], masks).then_inc(loaded, 16)
            sp.dma_start(causal[:], causal_c).then_inc(loaded, 16)
            sp.wait_ge(loaded, START + LOADS)

        @block.tensor
        def _(pe):
            pe.wait_ge(loaded, START + LOADS)
            pe.wait_ge(swapped, START + 4)
            for n in range(2 * CHUNKS):
                c, m = n // 2, n % 2
                if n >= 2:
                    pe.wait_ge(crossed_ready, START + n - 1)
                for swap in range(2):
                    last = nc.tensor.matmul(banks[:, 2 * (n % 2) + swap, :], w_bd[:, m + 3 * swap, :],
                                            resid[:, c * CHUNK:(c + 1) * CHUNK], start=True, stop=True)
                last.then_inc(proj_ready, 1)
            pe.wait_ge(crossed_ready, START + 2 * CHUNKS)

            def front(i, par):
                pe.wait_ge(k_ready, START + i + 1)
                nc.tensor.transpose(banks[:, par, 0:P], k_c[:, par, :], ident[:])
                nc.tensor.matmul(banks[:, par, P:2 * P], x_c[:, par, :], w_bd[:, 2, :], start=True, stop=True)
                nc.tensor.matmul(banks[:, par, 2 * P:3 * P], x_c[:, par, :], w_g[:], start=True, stop=True).then_inc(rows_ready, 1)
                pe.wait_ge(heads_ready, START + i + 1)
                for half in range(2):
                    last = nc.tensor.matmul(banks[:, 2 + 2 * par + half, :], k_c[:, par, :], q_heads[:, par, 4 * half:4 * half + 4, :],
                                            start=True, stop=True)
                last.then_inc(raw_ready, 1)

            def back(i, par, b):
                pe.wait_ge(kv_kept, START + i + 1)
                pe.wait_ge(g_kept, START + i + 1)
                pe.wait_ge(updated, START + i)
                nc.tensor.matmul(banks[:, UPDATE, 0:D], kv[:, par, 0, :], kv[:, par, 1, :], start=True, stop=True).then_inc(delta_ready, 1)
                pe.wait_ge(y_kept, START + i)
                pe.wait_ge(masked_ready, START + i + 1)
                pe.wait_ge(state_ready, START + i + 1)
                nc.tensor.matmul(banks[:, VALUES, 0:D], q_c[:, par, :], state[:], start=True, stop=False, skip_group_check=True)
                for h in range(R_HEADS):
                    cols = slice(h * R_HD, (h + 1) * R_HD)
                    last = nc.tensor.matmul(banks[:, VALUES, cols], masked[:, par, h, :], kv[:, par, 1, cols], start=False,
                                            stop=(h == R_HEADS - 1), skip_group_check=True)
                last.then_inc(y_ready, 1)

            chunks(pe, front, back)
            pe.wait_ge(stat_done, START + 9)
            for c in range(CHUNKS):
                for n in range(4):
                    last = nc.tensor.transpose(banks[:, 5 + c % 2, n * P:(n + 1) * P], work[:, 4 * c + n, :], ident[:])
                last.then_inc(turned, 1)
                pe.wait_ge(turn_kept, START + c + 1)
                if c >= 1:
                    pe.wait_ge(added, START + c)
                nc.tensor.matmul(banks[:, 7, :], w_o[:], z_t[:, c * CHUNK:(c + 1) * CHUNK], start=True, stop=True).then_inc(out_ready, 1)

        @block.scalar
        def _(act):
            def front(i, par):
                act.wait_ge(rows_ready, START + i + 1)
                nc.scalar.activation(kv[:, par].rearrange("p m n -> p (m n)"), banks[:, par, 0:2 * P], ACT.Copy).then_inc(kv_kept, 1)

            chunks(act, front, lambda i, par, b: None)
            act.wait_ge(stat_done, START + 3)
            nc.scalar.activation(work[:], y_all[:], ACT.Square).then_inc(act_done, 1)
            act.wait_ge(stat_done, START + 5)
            nc.scalar.activation(stat[:, 1, :], stat[:, 1, :], ACT.Sqrt).then_inc(act_done, 1)
            nc.scalar.activation(g_all[:], g_all[:], ACT.Silu).then_inc(act_done, 1)
            for c in range(CHUNKS):
                act.wait_ge(turned, START + c + 1)
                nc.scalar.activation(z_t[:, c * CHUNK:(c + 1) * CHUNK], banks[:, 5 + c % 2, :], ACT.Copy).then_inc(turn_kept, 1)

        @block.gpsimd
        def _(pool):
            pool.wait_ge(loaded, START + LOADS)

            def front(i, par):
                pool.wait_ge(q_ready, START + i + 1)
                nc.gpsimd.tensor_tensor(q_heads[:, par], q_c[:, par, :].unsqueeze(1).broadcast_to([P, R_HEADS, P]),
                                        mask[:, 0:R_HEADS].unsqueeze(2).broadcast_to([P, R_HEADS, P]), ALU.mult).then_inc(heads_ready, 1)

            chunks(pool, front, lambda i, par, b: None)

        @block.vector
        def _(dve):
            dve.wait_ge(loaded, START + LOADS)
            nc.vector.tensor_tensor(w_bd[:, 0:3, :].rearrange("p m (h e) -> p m h e", h=R_HEADS),
                                    w_heads[:].unsqueeze(2).broadcast_to([P, 3, R_HEADS, R_HD]),
                                    mask[:, R_HEADS:R_HEADS + D].rearrange("p (h e) -> p h e", h=R_HEADS).unsqueeze(1)
                                    .broadcast_to([P, 3, R_HEADS, R_HD]), ALU.mult).then_inc(placed, 1)
            dve.wait_ge(placed, START + 1)
            for m in range(2):
                src = w_bd[:, m, :].rearrange("p (n two) -> p n two", two=2)
                dst = w_bd[:, 3 + m, :].rearrange("p (n two) -> p n two", two=2)
                nc.vector.tensor_copy(dst[:, :, 0:1], src[:, :, 1:2]).then_inc(swapped, 1)
                nc.vector.tensor_copy(dst[:, :, 1:2], src[:, :, 0:1]).then_inc(swapped, 1)
            for n in range(2 * CHUNKS):
                c, m = n // 2, n % 2
                cols = slice(c * CHUNK, (c + 1) * CHUNK)
                pos = slice(c * CHUNK % S, c * CHUNK % S + CHUNK)
                w = n % 2
                dve.wait_ge(proj_ready, START + n + 1)
                if n >= 2:
                    dve.wait_ge(qk_all, START + n - 1)
                nc.vector.tensor_tensor(plain[:, w, :], banks[:, 2 * w, :], tab[:, m, pos], ALU.mult).then_inc(plain_ready, 1)
                nc.vector.tensor_tensor(crossed[:, w, :], banks[:, 2 * w + 1, :], tab[:, 2 + m, pos], ALU.mult).then_inc(crossed_ready, 1)
                dve.wait_ge(plain_ready, START + n + 1)
                dve.wait_ge(crossed_ready, START + n + 1)
                nc.vector.tensor_tensor((q_all if m == 0 else k_all)[:, cols], plain[:, w, :], crossed[:, w, :], ALU.add).then_inc(qk_all, 1)
            dve.wait_ge(qk_all, START + 2 * CHUNKS)

            def start(b):
                dve.wait_ge(y_ready, START + b * R_CHUNKS)
                dve.wait_ge(summed_ready, START + b * (R_CHUNKS + 1))
                nc.vector.memset(summed[:], 0.0).then_inc(summed_ready, 1)

            def front(i, par):
                nc.vector.tensor_scalar(q_c[:, par, :], q_all[:, bass.ds(i * P, P)], 1.0, None, ALU.mult).then_inc(q_ready, 1)
                nc.vector.tensor_scalar(x_c[:, par, :], resid[:, bass.ds(i * P, P)], 1.0, None, ALU.mult).then_inc(x_ready, 1)
                nc.vector.tensor_scalar(k_c[:, par, :], k_all[:, bass.ds(i * P, P)], 1.0, None, ALU.mult).then_inc(k_ready, 1)

            def back(i, par, b):
                dve.wait_ge(summed_ready, START + i + b + 1)
                dve.wait_ge(y_ready, START + i)
                nc.vector.tensor_scalar(state[:], summed[:], mask[:, R_HEADS + D:R_HEADS + D + 1], None, ALU.mult).then_inc(state_ready, 1)
                dve.wait_ge(kv_kept, START + i + 1)
                nc.vector.tensor_scalar(g_all[:, bass.ds(i, 1), :].rearrange("p a n -> p (a n)"), banks[:, par, 2 * P:3 * P], 1.0, None,
                                        ALU.mult).then_inc(g_kept, 1)
                dve.wait_ge(raw_ready, START + i + 1)
                nc.vector.tensor_tensor(masked[:, par], banks[:, 2 + 2 * par:4 + 2 * par, :].rearrange("p a (h s) -> p (a h) s", h=4),
                                        causal[:].unsqueeze(1).broadcast_to([P, R_HEADS, P]), ALU.mult).then_inc(masked_ready, 1)
                dve.wait_ge(delta_ready, START + i + 1)
                nc.vector.tensor_tensor(update[:], banks[:, UPDATE, 0:D], mask[:, R_HEADS:R_HEADS + D], ALU.mult).then_inc(updated, 1)
                dve.wait_ge(updated, START + i + 1)
                dve.wait_ge(state_ready, START + i + 1)
                nc.vector.tensor_tensor(summed[:], state[:], update[:], ALU.add).then_inc(summed_ready, 1)
                dve.wait_ge(y_ready, START + i + 1)
                nc.vector.tensor_scalar(y_all[:, bass.ds(i, 1), :].rearrange("p a n -> p (a n)"), banks[:, VALUES, 0:D], 1.0, None,
                                        ALU.mult).then_inc(y_kept, 1)

            chunks(dve, front, back, start)
            heads = "p n (h d) -> p (n h) d"
            y_h = y_all[:].rearrange(heads, d=R_HD)
            w_h = work[:].rearrange(heads, d=R_HD)
            chain = [0]

            def done(ins):
                chain[0] += 1
                ins.then_inc(stat_done, 1)
                dve.wait_ge(stat_done, START + chain[0])

            def spread(col):
                return stat[:, col, :].unsqueeze(2).broadcast_to([P, N * R_HEADS, R_HD])

            dve.wait_ge(y_kept, START + N)
            done(nc.vector.tensor_reduce(stat[:, 0, :], y_h, AX.X, ALU.add))
            done(nc.vector.tensor_scalar(stat[:, 0, :], stat[:, 0, :], 1.0 / R_HD, None, ALU.mult))
            done(nc.vector.tensor_tensor(y_h, y_h, spread(0), ALU.subtract))
            dve.wait_ge(act_done, START + 1)
            done(nc.vector.tensor_reduce(stat[:, 1, :], w_h, AX.X, ALU.add))
            done(nc.vector.tensor_scalar(stat[:, 1, :], stat[:, 1, :], 1.0 / R_HD, EPS, ALU.mult, ALU.add))
            dve.wait_ge(act_done, START + 2)
            done(nc.vector.reciprocal(stat[:, 0, :], stat[:, 1, :]))
            done(nc.vector.tensor_tensor(w_h, y_h, spread(0), ALU.mult))
            nc.vector.tensor_tensor(work[:], work[:], gn[:, 0, :].unsqueeze(1).broadcast_to([P, N, D]), ALU.mult).then_inc(updated, 1)
            dve.wait_ge(updated, START + N + 1)
            done(nc.vector.tensor_tensor(work[:], work[:], gn[:, 1, :].unsqueeze(1).broadcast_to([P, N, D]), ALU.add))
            dve.wait_ge(act_done, START + 3)
            done(nc.vector.tensor_tensor(work[:], work[:], g_all[:], ALU.mult))
            for c in range(CHUNKS):
                cols = slice(c * CHUNK, (c + 1) * CHUNK)
                dve.wait_ge(out_ready, START + c + 1)
                nc.vector.tensor_tensor(resid[:, cols], resid[:, cols], banks[:, 7, :], ALU.add).then_inc(added, 1)
            dve.wait_ge(added, START + CHUNKS)


def expert_stage(nc, keep, xn, router_t, w12_t, w3_t, out, consts):
    resid, ident = keep["resid"], keep["ident"]
    E, N = EXPERTS, E_TILES
    with ExitStack() as stack:
        core = Core(nc, stack)
        sb, sem = core.sb, core.sem
        rw = sb("e_rw", [P, E])
        cst = sb("e_cst", [P, P + E])
        ones = sb("e_ones", [P, P])
        logit = sb("e_logit", [P, N, E])
        second = sb("e_second", [P, N, E])
        best = sb("e_best", [P, 4, N])
        hit = sb("e_hit", [P, 2, N, E])
        chosen = sb("e_chosen", [P, N, E])
        before = sb("e_before", [P, N, E])
        place = sb("e_place", [P, N, E])
        prob = sb("e_prob", [P, 4, N])
        weight = sb("e_weight", [P, E, N])
        w12 = sb("e_w12", [P, 2, 2 * D_FF])
        w3 = sb("e_w3", [P, 2, F_PARTS, D])
        silu = sb("e_silu", [P, 2, CHUNK])
        hidden = sb("e_hidden", [P, 2, F_PARTS, CHUNK])
        scaled = sb("e_scaled", [P, 2, CHUNK])
        total = sb("e_total", [P, N, D])
        pre = sb("e_pre", [P, N, D])
        stat = sb("e_stat", [P, 2, N])
        banks = core.psum("e_banks", [P, 8, CHUNK])
        names = """loaded zeroed logit_ready step prefix_ready exp_done gate_ready silu_done hid_ready y_ready scaled_ready
            total_ready x_ready act_done stored weight_ready"""
        (loaded, zeroed, logit_ready, step, prefix_ready, exp_done, gate_ready, silu_done, hid_ready, y_ready, scaled_ready,
         total_ready, x_ready, act_done, stored, weight_ready) = (sem("e_" + n) for n in names.split())
        w_in = [sem("e_w_even_in"), sem("e_w_odd_in")]
        PER = CHUNKS * F_PARTS
        start_counts(nc, core)
        block = stack.enter_context(nc.Block())

        def combine(pe, i, m):
            par = m // CHUNKS
            pe.wait_ge(hid_ready, START + i * (2 * PER) + (m + 1) * F_PARTS)
            if m >= 2:
                pe.wait_ge(scaled_ready, START + i * (2 * CHUNKS) + m - 1)
            elif m == 0:
                pe.wait_ge(scaled_ready, START + i * (2 * CHUNKS))
            for t in range(4):
                for f in range(F_PARTS):
                    last = nc.tensor.matmul(banks[:, 4 + m % 2, t * P:(t + 1) * P], hidden[:, m % 2, f, t * P:(t + 1) * P],
                                            w3[:, par, f, :], start=(f == 0), stop=(f == F_PARTS - 1))
            last.then_inc(y_ready, 1)

        def weigh(dve, i, m):
            par, c = m // CHUNKS, m % CHUNKS
            dve.wait_ge(y_ready, START + i * (2 * CHUNKS) + m + 1)
            if m >= 2:
                dve.wait_ge(total_ready, START + i * (2 * CHUNKS) + m - 1)
            else:
                dve.wait_ge(total_ready, START + i * (2 * CHUNKS))
            wcol = weight[:, bass.ds(i * 2 + par, 1), 4 * c:4 * c + 4].rearrange("p a n -> p (a n)")
            nc.vector.tensor_tensor(scaled[:, m % 2, :].rearrange("p (n d) -> p n d", d=D),
                                    banks[:, 4 + m % 2, :].rearrange("p (n d) -> p n d", d=D),
                                    wcol.unsqueeze(2).broadcast_to([P, 4, D]), ALU.mult).then_inc(scaled_ready, 1)

        @block.sync
        def _(sp):
            sp.dma_start(rw[:], router_t).then_inc(loaded, 16)
            sp.dma_start(cst[:], consts).then_inc(loaded, 16)

            def load_expert(e, par):
                sp.dma_start(w12[:, par, :], w12_t[bass.ds(e, 1), :, :].rearrange("a p n -> p (a n)")).then_inc(w_in[par], 16)
                sp.dma_start(w3[:, par], w3_t[bass.ds(e, 1), :, :, :].rearrange("a p f n -> p (a f) n")).then_inc(w_in[par], 16)

            load_expert(0, 0)
            with sp.Fori(0, E // 2 - 1) as i:
                sp.wait_ge(y_ready, START + i * (2 * CHUNKS))
                sp.sem_inc(stored, 1)
                load_expert(i * 2 + 1, 1)
                sp.wait_ge(y_ready, START + i * (2 * CHUNKS) + CHUNKS)
                sp.sem_inc(stored, 1)
                load_expert(i * 2 + 2, 0)
            sp.wait_ge(y_ready, START + (E - 2) * CHUNKS)
            load_expert(E - 1, 1)
            sp.wait_ge(step, START + FINAL)
            sp.dma_start(out.rearrange("(n p) d -> p n d", p=P), pre[:]).then_inc(loaded, 16)
            sp.wait_ge(loaded, START + 48)

        @block.tensor
        def _(pe):
            pe.wait_ge(loaded, START + 32)
            for n in range(N):
                last = nc.tensor.matmul(banks[:, 6, n * E:(n + 1) * E], xn[:, n * P:(n + 1) * P], rw[:], start=True, stop=True)
            last.then_inc(logit_ready, 1)
            pe.wait_ge(zeroed, START + 2)
            pe.wait_ge(step, START + CHOSEN)
            flat = chosen[:].rearrange("p n e -> p (n e)")
            nc.tensor.matmul(banks[:, 6, P:2 * P], cst[:, 0:P], flat, start=True, stop=True)
            nc.tensor.matmul(banks[:, 6, 2 * P:3 * P], ones[:], flat, start=True, stop=True).then_inc(prefix_ready, 1)
            with pe.Fori(0, E // 2) as i:
                for par in range(2):
                    for c in range(CHUNKS):
                        for f in range(F_PARTS):
                            k = par * PER + c * F_PARTS + f
                            if par == 0 and c == 0 and f == 0:
                                pe.wait_ge(w_in[0], START + i * 32 + 32)
                                pe.wait_ge(hid_ready, START + i * (2 * PER))
                            elif c == 0 and f == 0:
                                pe.wait_ge(w_in[1], START + i * 32 + 32)
                            if k >= 2:
                                pe.wait_ge(hid_ready, START + i * (2 * PER) + k - 1)
                            b0 = 2 * (k % 2)
                            for side in range(2):
                                last = nc.tensor.matmul(banks[:, b0 + side, :], w12[:, par, side * D_FF + f * P:side * D_FF + (f + 1) * P],
                                                        xn[:, c * CHUNK:(c + 1) * CHUNK], start=True, stop=True)
                            last.then_inc(gate_ready, 1)
                        m = par * CHUNKS + c
                        if m >= 1:
                            combine(pe, i, m - 1)
                combine(pe, i, 2 * CHUNKS - 1)
            for n in range(N):
                if n % 4 == 0:
                    pe.wait_ge(scaled_ready, START + E * CHUNKS)
                last = nc.tensor.transpose(banks[:, n // 4, (n % 4) * P:(n % 4 + 1) * P], resid[:, n * P:(n + 1) * P], ident[:])
            last.then_inc(x_ready, 1)

        @block.scalar
        def _(act):
            act.wait_ge(step, START + TOPS)
            nc.scalar.activation(prob[:, 1, :], prob[:, 0, :], ACT.Exp).then_inc(exp_done, 1)
            with act.Fori(0, E // 2) as i:
                for k in range(2 * PER):
                    act.wait_ge(gate_ready, START + i * (2 * PER) + k + 1)
                    if k >= 2:
                        act.wait_ge(hid_ready, START + i * (2 * PER) + k - 1)
                    nc.scalar.activation(silu[:, k % 2, :], banks[:, 2 * (k % 2), :], ACT.Silu).then_inc(silu_done, 1)
            act.wait_ge(step, START + SQUARE)
            nc.scalar.activation(total[:], pre[:], ACT.Square).then_inc(act_done, 1)
            act.wait_ge(step, START + ROOT)
            nc.scalar.activation(stat[:, 1, :], stat[:, 1, :], ACT.Sqrt).then_inc(act_done, 1)

        @block.gpsimd
        def _(pool):
            nc.gpsimd.memset(ones[:], 1.0).then_inc(zeroed, 1)
            nc.gpsimd.memset(total[:], 0.0).then_inc(zeroed, 1)
            pool.wait_ge(zeroed, START + 2)
            with pool.Fori(0, E // 2) as i:
                for m in range(2 * CHUNKS):
                    c = m % CHUNKS
                    pool.wait_ge(scaled_ready, START + i * (2 * CHUNKS) + m + 1)
                    pool.wait_ge(total_ready, START + i * (2 * CHUNKS) + m)
                    acc = total[:, 4 * c:4 * c + 4, :].rearrange("p n d -> p (n d)")
                    nc.gpsimd.tensor_tensor(acc, acc, scaled[:, m % 2, :], ALU.add).then_inc(total_ready, 1)

        @block.vector
        def _(dve):
            count = [0]

            def done(ins):
                count[0] += 1
                ins.then_inc(step, 1)
                dve.wait_ge(step, START + count[0])

            def over_e(a):
                return a.unsqueeze(2).broadcast_to([P, N, E])

            rev = cst[:, P:P + E].unsqueeze(1).broadcast_to([P, N, E])
            dve.wait_ge(loaded, START + 32)
            dve.wait_ge(logit_ready, START + 1)
            done(nc.vector.tensor_scalar(logit[:].rearrange("p n e -> p (n e)"), banks[:, 6, 0:N * E], CLAMP, -CLAMP, ALU.min, ALU.max))
            for k, values in enumerate((logit, second)):
                done(nc.vector.tensor_reduce(best[:, k, :], values[:], AX.X, ALU.max))
                done(nc.vector.tensor_tensor(hit[:, k], values[:], over_e(best[:, k, :]), ALU.is_equal))
                done(nc.vector.tensor_tensor(hit[:, k], hit[:, k], rev, ALU.mult))
                done(nc.vector.tensor_reduce(best[:, 2 + k, :], hit[:, k], AX.X, ALU.max))
                done(nc.vector.tensor_tensor(hit[:, k], rev, over_e(best[:, 2 + k, :]), ALU.is_equal))
                if k == 0:
                    done(nc.vector.scalar_tensor_tensor(out=second[:], in0=hit[:, 0], scalar=-1e9, in1=logit[:], op0=ALU.mult, op1=ALU.add))
            done(nc.vector.tensor_tensor(chosen[:], hit[:, 0], hit[:, 1], ALU.add))
            assert count[0] == CHOSEN
            done(nc.vector.tensor_tensor(prob[:, 0, :], best[:, 1, :], best[:, 0, :], ALU.subtract))
            assert count[0] == TOPS
            dve.wait_ge(exp_done, START + 1)
            done(nc.vector.tensor_scalar(prob[:, 2, :], prob[:, 1, :], 1.0, 1e-12, ALU.add, ALU.add))
            done(nc.vector.reciprocal(prob[:, 0, :], prob[:, 2, :]))
            done(nc.vector.tensor_tensor(prob[:, 3, :], prob[:, 1, :], prob[:, 0, :], ALU.mult))
            done(nc.vector.tensor_tensor(hit[:, 0], hit[:, 0], over_e(prob[:, 0, :]), ALU.mult))
            done(nc.vector.tensor_tensor(hit[:, 1], hit[:, 1], over_e(prob[:, 3, :]), ALU.mult))
            done(nc.vector.tensor_tensor(hit[:, 0], hit[:, 0], hit[:, 1], ALU.add))
            dve.wait_ge(prefix_ready, START + 1)
            tile_total = banks[:, 6, 2 * P:3 * P].rearrange("p (n e) -> p n e", e=E)
            done(nc.vector.memset(before[:], 0.0))
            for n in range(1, N):
                done(nc.vector.tensor_tensor(before[:, n, :], tile_total[:, n - 1, :], before[:, n - 1, :], ALU.add))
            done(nc.vector.tensor_tensor(place[:], banks[:, 6, P:2 * P].rearrange("p (n e) -> p n e", e=E), before[:], ALU.add))
            done(nc.vector.tensor_scalar(place[:], place[:], float(CAP), None, ALU.is_lt))
            nc.vector.tensor_tensor(weight[:].rearrange("p e n -> p n e"), hit[:, 0], place[:], ALU.mult).then_inc(weight_ready, 1)
            dve.wait_ge(weight_ready, START + 1)
            with dve.Fori(0, E // 2) as i:
                for m in range(2 * CHUNKS):
                    par, c = m // CHUNKS, m % CHUNKS
                    for f in range(F_PARTS):
                        k = m * F_PARTS + f
                        dve.wait_ge(silu_done, START + i * (2 * PER) + k + 1)
                        if f == 0 and m >= 2:
                            dve.wait_ge(y_ready, START + i * (2 * CHUNKS) + m - 1)
                        if f == 0 and m == 0:
                            dve.wait_ge(y_ready, START + i * (2 * CHUNKS))
                        nc.vector.tensor_tensor(hidden[:, m % 2, f, :], banks[:, 2 * (k % 2) + 1, :], silu[:, k % 2, :], ALU.mult)\
                            .then_inc(hid_ready, 1)
                    if m >= 1:
                        weigh(dve, i, m - 1)
                weigh(dve, i, 2 * CHUNKS - 1)
            dve.wait_ge(x_ready, START + 1)
            dve.wait_ge(total_ready, START + E * CHUNKS)
            fl = "p n d -> p (n d)"
            done(nc.vector.tensor_tensor(pre[:].rearrange(fl), banks[:, 0:4, :].rearrange("p a n -> p (a n)"), total[:].rearrange(fl), ALU.add))
            over_d = lambda a: a.unsqueeze(2).broadcast_to([P, N, D])
            done(nc.vector.tensor_reduce(stat[:, 0, :], pre[:], AX.X, ALU.add))
            done(nc.vector.tensor_scalar(stat[:, 0, :], stat[:, 0, :], 1.0 / D, None, ALU.mult))
            done(nc.vector.tensor_tensor(pre[:], pre[:], over_d(stat[:, 0, :]), ALU.subtract))
            assert count[0] == SQUARE
            dve.wait_ge(act_done, START + 1)
            done(nc.vector.tensor_reduce(stat[:, 1, :], total[:], AX.X, ALU.add))
            done(nc.vector.tensor_scalar(stat[:, 1, :], stat[:, 1, :], 1.0 / D, EPS, ALU.mult, ALU.add))
            assert count[0] == ROOT
            dve.wait_ge(act_done, START + 2)
            done(nc.vector.reciprocal(stat[:, 0, :], stat[:, 1, :]))
            done(nc.vector.tensor_tensor(pre[:], pre[:], over_d(stat[:, 0, :]), ALU.mult))
            assert count[0] == FINAL



def program(nc, t, c, out):
    with ExitStack() as stack:
        core = Core(nc, stack)
        keep = {"resid": core.sb("resid", [P, T]), "ident": core.sb("ident", [P, P]), "identb": core.sb("identb", [P, P], BF16),
                "mean_w": core.sb("mean_w", [P, P]), "eps": core.sb("eps", [P, 1]), "norm_sems": norm_semaphores(core)}
        load_constants(nc, keep, c)
        attention_stage(nc, keep, t["L0_attn_x"], t["L0_attn_Wqkv"], t["L0_attn_bqkv"], t["L0_attn_Wo"], t["L0_attn_bo"], c["c_sel"])
        norm_stage(nc, keep, 0)
        f = lambda n: t["L0_ffn_" + n]
        local_stage(nc, keep, f("Wqkv"), f("q_scale"), f("k_scale"), f("Wo"), f("ln_g"), f("ln_b"), f("W1"), f("b1"), f("W2"), f("b2"),
                    c["c_rotary"], c["c_band"])
        norm_stage(nc, keep, 1)
        r = lambda n: t["L1_attn_" + n]
        retention_stage(nc, keep, (r("W_Q"), r("W_K"), r("W_V")), r("W_G"), r("W_O"), r("gn_weight"), r("gn_bias"),
                        c["c_decay"], c["c_masks"], c["c_causal"])
        norm_stage(nc, keep, 2)
        with ExitStack() as last:
            xn = Core(nc, last).sb("xn", [P, T])
            norm_stage(nc, keep, 3, out=xn, affine=(t["L1_ffn_ln_gamma"], t["L1_ffn_ln_beta"]))
            expert_stage(nc, keep, xn, t["L1_ffn_router_w"], t["L1_ffn_w12"], t["L1_ffn_w3"], out, c["c_expert"])


def _shape_constants():
    import numpy as np
    c = {"c_ident": np.eye(P)}
    sel = np.zeros((P, 18))
    for q in range(4):
        for h in range(2):
            for e in range(9):
                sel[32 * q + 16 * h + e, 9 * h + e] = 1
    c["c_sel"] = sel
    half = np.arange(0, HD, 2)
    pos = np.arange(S)
    freqs = np.concatenate([pos[:, None] * (1.0 / 10000.0 ** (half / HD))[None, :]] * 2, -1)
    scale = ((half + 0.4 * HD) / (1.4 * HD))[None, :] ** ((pos - S // 2) / (WIN // 2))[:, None]
    scale = np.concatenate([scale, scale], -1)
    sign = np.where(np.arange(HD) < HD // 2, -1.0, 1.0)
    rotary = np.stack([np.cos(freqs) * scale, np.cos(freqs) / scale, np.sin(freqs) * scale * sign, np.sin(freqs) / scale * sign])
    c["c_rotary"] = rotary.reshape(4, TTILES, P, HD).transpose(2, 0, 1, 3)
    i, j = np.arange(QTILE)[:, None], np.arange(P)[None]
    c["c_band"] = np.where((i <= j) & (j <= i + WIN), 0, -1e30)
    gamma = 1.0 - np.exp(np.linspace(np.log(1.0 / 32.0), np.log(1.0 / 512.0), R_HEADS))
    gamma = np.repeat(gamma, R_HD)[:, None]
    d = R_HD
    sc = np.repeat((np.arange(0, d, 2) + 0.4 * d) / (1.4 * d), 2)[:, None] ** (pos / 512.0)[None, :]
    ang = np.repeat(1.0 / 10000.0 ** (np.arange(d // 2) / (d // 2)), 2)[:, None] * pos[None, :]
    sc, ang = np.tile(sc, (R_HEADS, 1)), np.tile(ang, (R_HEADS, 1))
    dec = gamma ** (pos % P)[None, :]
    sg = np.where(np.arange(P) % 2 == 0, -1.0, 1.0)[:, None]
    c["c_decay"] = np.stack([np.cos(ang) * sc * dec, np.cos(ang) / sc / dec, np.sin(ang) * sc * dec * sg, np.sin(ang) / sc / dec * sg], 1)
    head = np.arange(P) // R_HD
    c["c_masks"] = np.concatenate([head[:, None] == np.arange(R_HEADS)[None], head[:, None] == head[None], gamma ** P], 1)
    c["c_causal"] = np.arange(P)[:, None] <= np.arange(P)[None]
    c["c_expert"] = np.concatenate([np.arange(P)[:, None] < np.arange(P)[None], np.tile(EXPERTS - np.arange(EXPERTS), (P, 1))], 1)
    return {k: np.ascontiguousarray(v, dtype=np.float32) for k, v in c.items()}


def _laid_out(inputs):
    import numpy as np
    a = {k: np.asarray(v) for k, v in inputs.items()}
    a["L0_attn_x"] = a["L0_attn_x"].reshape(T, D)
    a["L0_attn_Wqkv"] = a["L0_attn_Wqkv"].T
    a["L0_attn_Wo"] = a["L0_attn_Wo"].T.reshape(8, 2, A_HD, D).transpose(0, 2, 1, 3).reshape(64, 2, D)
    a["L0_ffn_Wo"] = a["L0_ffn_Wo"].reshape(DEPTH, HEADS // 2, P, D).transpose(0, 2, 1, 3)
    a["L1_ffn_router_w"] = a["L1_ffn_router_w"].T
    a["L1_ffn_w12"] = a["L1_ffn_w12"].transpose(0, 2, 1)
    a["L1_ffn_w3"] = a["L1_ffn_w3"].transpose(0, 2, 1).reshape(EXPERTS, F_PARTS, P, D).transpose(0, 2, 1, 3)
    return {k: np.ascontiguousarray(v) for k, v in a.items()}


def kernel(**inputs):
    import concourse.bacc as bacc
    from concourse.bass_utils import run_bass_kernel_spmd

    nc = bacc.Bacc("TRN2", target_bir_lowering=False, num_devices=1)
    arrays, handles = {}, {}
    for name, a in {**_laid_out(inputs), **_shape_constants()}.items():
        arrays["in_" + name] = a
        handles[name] = nc.dram_tensor("in_" + name, a.shape, mybir.dt.from_np(a.dtype), kind="ExternalInput").ap()
    out = nc.dram_tensor("out_x", (T, D), F32, kind="ExternalOutput").ap()
    program(nc, handles, handles, out)
    result = run_bass_kernel_spmd(nc, [arrays], core_ids=[0])
    return result.results[0]["out_x"].reshape(B, S, D)
```
